# Optimizing a Trainium2 kernel written in Bass

```python
import numpy as np
import jax
import jax.numpy as jnp

def _softmax(x, axis=-1):
    return jax.nn.softmax(x, axis=axis)

def _gelu(x):
    return jax.nn.gelu(x, approximate=True)

def _silu(x):
    return jax.nn.silu(x)

def _sigmoid(x):
    return jax.nn.sigmoid(x)

def _layernorm(x, axis=-1, eps=1e-05):
    m = jnp.mean(x, axis=axis, keepdims=True)
    v = jnp.var(x, axis=axis, keepdims=True)
    return (x - m) / jnp.sqrt(v + eps)

def _scatter_add(tgt, idx, src, axis=0):
    return tgt.at[idx].add(src)

def _segment_sum(src, seg, n):
    return jax.ops.segment_sum(src, seg, n)
kernel_name = 'mk_flamingo_gated_d2_seqx_r8_f4dd32'

def setup_inputs(seed: int=0):
    np.random.seed(seed)
    _w = jnp.asarray

    def _rec_inputs():
        import jax
        import jax.numpy as jnp
        _rk = jax.random.key(seed)
        x = -0.0002928 + 1 * jax.random.normal(jax.random.fold_in(_rk, 1), (4, 512, 128), jnp.float32)
        _lenS = 512 - jax.random.randint(jax.random.fold_in(_rk, 7), (4,), 0, max(1, 512 // 4) + 1, jnp.int32)
        _lenS2 = 154 - jax.random.randint(jax.random.fold_in(_rk, 8), (4,), 0, max(1, 154 // 4) + 1, jnp.int32)
        _ctx_1024P = jax.random.normal(jax.random.fold_in(_rk, 11), (4, 16, 128), jnp.float32)
        _ctx_1024c = jax.random.dirichlet(jax.random.fold_in(_rk, 511), 0.3 * jnp.ones((16,), jnp.float32), (4, 154))
        _ctx_1024t = jnp.einsum('bsk,bkd->bsd', _ctx_1024c, _ctx_1024P)
        _ctx_1024t = _ctx_1024t * jax.lax.rsqrt(jnp.mean(jnp.square(_ctx_1024t)) + 1e-12) * 0.953939
        ctx_1024 = -1.39393e-06 + 0.999914 * (_ctx_1024t + 0.3 * jax.random.normal(jax.random.fold_in(_rk, 611), (4, 154, 128), jnp.float32))
        _validS = jnp.arange(512)[None, :] < _lenS[:, None]
        _validS2 = jnp.arange(154)[None, :] < _lenS2[:, None]
        _causal = jnp.tril(jnp.ones((512, 512), dtype=bool))
        mask_BxSxS2_ik1 = jnp.where(jnp.broadcast_to(_validS2[:, None, :], (4, 512, 154)), 1, 0).astype(jnp.int32)
        _g = jax.random.normal(jax.random.fold_in(_rk, 9001), (2, 2), jnp.float32)
        _g = jnp.sign(_g) * jnp.maximum(jnp.abs(_g), 1.0) + (_g == 0) * 1.0
        g_xattn = _g[0]
        g_ffn = _g[1]
        return (x, ctx_1024, mask_BxSxS2_ik1, g_xattn, g_ffn)
    x, ctx_1024, mask_BxSxS2_ik1, g_xattn, g_ffn = _rec_inputs()

    def _L0_xattn_setup():
        import jax, jax.numpy as jnp
        import numpy as np
        B, S, D, H = (2, 256, 128, 16)
        DK = D // H
        key = jax.random.key(seed)
        ks = jax.random.split(key, 9)
        query = jax.random.normal(ks[0], (B, S, D), dtype=jnp.float32)
        k_in = jax.random.normal(ks[1], (B, S, D), dtype=jnp.float32)
        v_in = jax.random.normal(ks[2], (B, S, D), dtype=jnp.float32)
        mask = jax.random.randint(ks[3], (B, S, S), 0, 2, dtype=jnp.int32)
        sc = 1.0 / np.sqrt(D)
        Wq = jax.random.normal(ks[4], (H, D, DK), dtype=jnp.float32) * sc
        Wk = jax.random.normal(ks[5], (H, D, DK), dtype=jnp.float32) * sc
        Wv = jax.random.normal(ks[6], (H, D, DK), dtype=jnp.float32) * sc
        Wu = jax.random.normal(ks[7], (D, D), dtype=jnp.float32) * sc
        bu = jax.random.normal(ks[8], (D,), dtype=jnp.float32) * 0.01
        return {'query': query, 'key': k_in, 'value': v_in, 'mask': mask, 'Wq': Wq, 'Wk': Wk, 'Wv': Wv, 'Wu': Wu, 'bu': bu}
    _L0_xattn_all = _L0_xattn_setup()
    _L0_xattn_in = {k: v for k, v in _L0_xattn_all.items() if k in ('Wq', 'Wk', 'Wv', 'Wu', 'bu')}
    del _L0_xattn_all

    def _L0_ffn_setup():
        import jax, jax.numpy as jnp
        import numpy as np
        TOP_K = 2
        key = jax.random.key(seed)
        k1, k2, k3, k4 = jax.random.split(key, 4)
        B, T, D, H, E = (4, 256, 128, 256, 8)
        scale = 0.02
        x = jax.random.normal(k1, (B, T, D), dtype=jnp.float32)
        Wg = jax.random.normal(k2, (D, E), dtype=jnp.float32) * scale
        W1 = jax.random.normal(k3, (E, D, H), dtype=jnp.float32) * scale
        W2 = jax.random.normal(k4, (E, H, D), dtype=jnp.float32) * scale
        return {'x': x, 'Wg': Wg, 'W1': W1, 'W2': W2}
    _L0_ffn_all = _L0_ffn_setup()
    _L0_ffn_in = {k: v for k, v in _L0_ffn_all.items() if k in ('Wg', 'W1', 'W2')}
    del _L0_ffn_all

    def _L1_xattn_setup():
        import jax, jax.numpy as jnp
        import numpy as np
        B, S, D = (4, 256, 128)
        key = jax.random.key(seed)
        ks = jax.random.split(key, 10)
        sc = 1.0 / np.sqrt(D)
        return {'x': jax.random.normal(ks[0], (B, S, D), dtype=jnp.float32), 'y': jax.random.normal(ks[1], (B, S, D), dtype=jnp.float32), 'Wq': jax.random.normal(ks[2], (D, D), dtype=jnp.float32) * sc, 'bq': jnp.zeros((D,), dtype=jnp.float32), 'Wk': jax.random.normal(ks[3], (D, D), dtype=jnp.float32) * sc, 'bk': jnp.zeros((D,), dtype=jnp.float32), 'Wv': jax.random.normal(ks[4], (D, D), dtype=jnp.float32) * sc, 'bv': jnp.zeros((D,), dtype=jnp.float32), 'Wr': jax.random.normal(ks[5], (D, D), dtype=jnp.float32) * sc, 'br': jnp.zeros((D,), dtype=jnp.float32)}
    _L1_xattn_all = _L1_xattn_setup()
    _L1_xattn_in = {k: v for k, v in _L1_xattn_all.items() if k in ('Wq', 'bq', 'Wk', 'bk', 'Wv', 'bv', 'Wr', 'br')}
    del _L1_xattn_all

    def _L1_ffn_setup():
        import jax, jax.numpy as jnp
        import numpy as np
        FEATURES = 128
        D_IN = 128

        def fp8_gemm_optimized(x, input_scale, kernel, kernel_scale):
            s_in = input_scale[0]
            s_k = kernel_scale[0]
            x_q = (x.astype(jnp.float32) / s_in).astype(jnp.float8_e4m3fn)
            k_q = (kernel.astype(jnp.float32) / s_k).astype(jnp.float8_e4m3fn)
            y = jnp.dot(x_q.astype(jnp.float32), k_q.astype(jnp.float32), preferred_element_type=jnp.float32)
            return y * (s_in * s_k)
        key = jax.random.key(seed)
        kx, kk, kb = jax.random.split(key, 3)
        x = jax.random.normal(kx, (4, 1024, D_IN), dtype=jnp.float32)
        limit = np.sqrt(6.0 / (D_IN + FEATURES)).astype(np.float32)
        kernel = jax.random.uniform(kk, (D_IN, FEATURES), dtype=jnp.float32, minval=-limit, maxval=limit).astype(jnp.bfloat16)
        input_scale = jnp.ones((1,), dtype=jnp.float32)
        kernel_scale = jnp.ones((1,), dtype=jnp.float32)
        bias = jnp.zeros((FEATURES,), dtype=jnp.bfloat16)
        return {'x': x, 'kernel': kernel, 'input_scale': input_scale, 'kernel_scale': kernel_scale, 'bias': bias}
    _L1_ffn_all = _L1_ffn_setup()
    _L1_ffn_in = {k: v for k, v in _L1_ffn_all.items() if k in ('kernel', 'input_scale', 'kernel_scale', 'bias')}
    del _L1_ffn_all
    return {'x': x, 'ctx_1024': ctx_1024, 'mask_BxSxS2_ik1': mask_BxSxS2_ik1, 'g_xattn': g_xattn, 'g_ffn': g_ffn, 'L0_xattn_Wq': _L0_xattn_in['Wq'], 'L0_xattn_Wk': _L0_xattn_in['Wk'], 'L0_xattn_Wv': _L0_xattn_in['Wv'], 'L0_xattn_Wu': _L0_xattn_in['Wu'], 'L0_xattn_bu': _L0_xattn_in['bu'], 'L0_ffn_Wg': _L0_ffn_in['Wg'], 'L0_ffn_W1': _L0_ffn_in['W1'], 'L0_ffn_W2': _L0_ffn_in['W2'], 'L1_xattn_Wq': _L1_xattn_in['Wq'], 'L1_xattn_bq': _L1_xattn_in['bq'], 'L1_xattn_Wk': _L1_xattn_in['Wk'], 'L1_xattn_bk': _L1_xattn_in['bk'], 'L1_xattn_Wv': _L1_xattn_in['Wv'], 'L1_xattn_bv': _L1_xattn_in['bv'], 'L1_xattn_Wr': _L1_xattn_in['Wr'], 'L1_xattn_br': _L1_xattn_in['br'], 'L1_ffn_kernel': _L1_ffn_in['kernel'], 'L1_ffn_input_scale': _L1_ffn_in['input_scale'], 'L1_ffn_kernel_scale': _L1_ffn_in['kernel_scale'], 'L1_ffn_bias': _L1_ffn_in['bias']}

def reference(x, ctx_1024, mask_BxSxS2_ik1, g_xattn, g_ffn, L0_xattn_Wq, L0_xattn_Wk, L0_xattn_Wv, L0_xattn_Wu, L0_xattn_bu, L0_ffn_Wg, L0_ffn_W1, L0_ffn_W2, L1_xattn_Wq, L1_xattn_bq, L1_xattn_Wk, L1_xattn_bk, L1_xattn_Wv, L1_xattn_bv, L1_xattn_Wr, L1_xattn_br, L1_ffn_kernel, L1_ffn_input_scale, L1_ffn_kernel_scale, L1_ffn_bias):
    import jax
    import jax.numpy as jnp

    def _L0_xattn_ref(query, key, value, mask, Wq, Wk, Wv, Wu, bu):
        import jax, jax.numpy as jnp
        import numpy as np
        B, S, D, H = (2, 256, 128, 16)
        DK = D // H
        scale = DK ** 0.25
        q = jnp.einsum('bsd,hdk->bhsk', query, Wq) / scale
        k = jnp.einsum('bsd,hdk->bhsk', key, Wk) / scale
        v = jnp.einsum('bsd,hdk->bhsk', value, Wv)
        scores = jnp.einsum('bhsk,bhtk->bhst', q, k)
        scores = jnp.where(mask[:, None, :, :] == 0, jnp.float32(-1000000000.0), scores)
        attn = jax.nn.softmax(scores, axis=-1)
        out = jnp.einsum('bhst,bhtk->bhsk', attn, v)
        out = jnp.transpose(out, (0, 2, 1, 3)).reshape(query.shape[0], query.shape[1], D)
        return out @ Wu + bu

    def _L0_ffn_ref(x, Wg, W1, W2):
        import jax, jax.numpy as jnp
        import numpy as np
        TOP_K = 2
        B, T, D = x.shape
        E = Wg.shape[1]
        x_flat = x.reshape(-1, D)
        gate_logits = x_flat @ Wg
        weights = jax.nn.softmax(gate_logits, axis=-1)
        topk_w, topk_idx = jax.lax.top_k(weights, TOP_K)
        topk_w = topk_w / jnp.sum(topk_w, axis=-1, keepdims=True)
        combine = jnp.sum(topk_w[..., None] * jax.nn.one_hot(topk_idx, E, dtype=x.dtype), axis=1)
        h = jax.nn.silu(jnp.einsum('nd,edh->enh', x_flat, W1))
        y = jnp.einsum('enh,ehd->end', h, W2)
        out = jnp.einsum('end,ne->nd', y, combine)
        return out.reshape(B, T, D)

    def _L1_xattn_ref(x, y, Wq, bq, Wk, bk, Wv, bv, Wr, br):
        import jax, jax.numpy as jnp
        import numpy as np
        B, S, D = (4, 256, 128)
        Q = jnp.einsum('bsd,de->bse', x, Wq) + bq
        K = jnp.einsum('bsd,de->bse', y, Wk) + bk
        V = jnp.einsum('bsd,de->bse', y, Wv) + bv
        K_hat = jnp.cos(jnp.einsum('bsd,dr->bsr', K, Wr) + br)
        scores = jnp.einsum('bqr,bkr->bqk', Q, K_hat)
        probs = jax.nn.softmax(scores, axis=-1)
        return jnp.einsum('bqk,bkd->bqd', probs, V)

    def _L1_ffn_ref(x, kernel, input_scale, kernel_scale, bias):
        import jax, jax.numpy as jnp
        import numpy as np
        FEATURES = 128
        D_IN = 128

        def fp8_gemm_optimized(x, input_scale, kernel, kernel_scale):
            s_in = input_scale[0]
            s_k = kernel_scale[0]
            x_q = (x.astype(jnp.float32) / s_in).astype(jnp.float8_e4m3fn)
            k_q = (kernel.astype(jnp.float32) / s_k).astype(jnp.float8_e4m3fn)
            y = jnp.dot(x_q.astype(jnp.float32), k_q.astype(jnp.float32), preferred_element_type=jnp.float32)
            return y * (s_in * s_k)
        dtype = jnp.bfloat16
        x = x.astype(dtype)
        orig_shape = x.shape
        x2 = x.reshape(-1, x.shape[-1])
        y = fp8_gemm_optimized(x2, input_scale, kernel, kernel_scale)
        y = y.astype(dtype) + bias
        return y.reshape(orig_shape[:-1] + (FEATURES,))
    x = x + jnp.tanh(g_xattn[0]) * _L0_xattn_ref(_layernorm(x, axis=-1), ctx_1024, ctx_1024, mask_BxSxS2_ik1, L0_xattn_Wq, L0_xattn_Wk, L0_xattn_Wv, L0_xattn_Wu, L0_xattn_bu)
    x = x + jnp.tanh(g_ffn[0]) * _L0_ffn_ref(_layernorm(x, axis=-1), L0_ffn_Wg, L0_ffn_W1, L0_ffn_W2)
    x = x + jnp.tanh(g_xattn[1]) * _L1_xattn_ref(_layernorm(x, axis=-1), ctx_1024, L1_xattn_Wq, L1_xattn_bq, L1_xattn_Wk, L1_xattn_bk, L1_xattn_Wv, L1_xattn_bv, L1_xattn_Wr, L1_xattn_br)
    x = x + jnp.tanh(g_ffn[1]) * _L1_ffn_ref(_layernorm(x, axis=-1), L1_ffn_kernel, L1_ffn_input_scale, L1_ffn_kernel_scale, L1_ffn_bias)
    return x

_drawn_inputs = setup_inputs


def setup_inputs(seed=0):
    import zlib

    import numpy as np

    out = dict(_drawn_inputs(seed))
    spreads = {'g_ffn': (-1.0, 0.2),
     'L1_xattn_bq': (0.0, 0.1),
     'L1_xattn_bk': (0.0, 0.1),
     'L1_xattn_bv': (0.0, 0.1),
     'L1_xattn_br': (0.0, 0.1),
     'L1_ffn_bias': (0.0, 0.1)}
    factors = {'L0_xattn_bu': 4.284}
    for name, (base, spread) in spreads.items():
        noise = np.random.default_rng([zlib.crc32(name.encode()), seed]).standard_normal(out[name].shape)
        drawn = base * np.exp(spread * noise) if base else spread * noise
        out[name] = jnp.asarray(drawn.astype(out[name].dtype))
    for name, factor in factors.items():
        out[name] = (out[name] * factor).astype(out[name].dtype)
    return out
```

```python
from contextlib import ExitStack

import concourse.bass as bass
from concourse import mybir

P = 128
ALU = mybir.AluOpType
ACT = mybir.ActivationFunctionType
X = mybir.AxisListType.X
F32 = mybir.dt.float32
BF16 = mybir.dt.bfloat16
F16 = mybir.dt.float16
I32 = mybir.dt.int32
U32 = mybir.dt.uint32

H, DK = 16, 8
HG = 4
NG = H // HG
ROWS = P // HG
MROW = 3 * DK
E_N, F_N = 8, 256
FC = E_N * F_N // P
WS = 64.0
MASKED = -1.0e30
EPS = 1e-5
TWO_PI = 6.283185307179586
TWO_PI_HI = 6.28125
TWO_PI_LO = TWO_PI - TWO_PI_HI
PI = 3.1415925
ROUND = 12582912.0

W_COLS = {}
_at = 0
for _name, _n in [("wq0", 128), ("wk0", 128), ("wv0", 128), ("wu0", 128), ("bu0", 128), ("g", 4), ("s", 2),
                  ("wg", 8), ("wq1", 128), ("wk1", 128), ("wv1", 128), ("wr1", 128), ("bq1", 1), ("bk1", 1),
                  ("br1", 1), ("bv1", 128)]:
    W_COLS[_name] = (_at, _at + _n)
    _at += _n
W_TOTAL = _at
W_EARLY = W_COLS["wg"][0]
C_COLS = {"ident": (0, 128), "lo_q": (128, 129), "lo_k": (129, 130), "one": (130, 131), "iota": (131, 139)}
C_TOTAL = 139


def flamingo_gated(nc, x, ctx_t, mask, wts, w1, w2, kern, kbias, consts, out):
    B, S, D = x.shape
    T = ctx_t.shape[2]
    ST = S // P
    T0 = P
    TR = T - T0
    TH = T // 2
    assert D == P and TR <= ROWS and T % 2 == 0

    x_v = x.rearrange("b (s p) d -> b p s d", p=P)
    out_v = out.rearrange("b (s p) d -> b p s d", p=P)
    mask_v = mask.rearrange("b (s p) t -> b p s t", p=P)

    with ExitStack() as stack:
        def sb(name, shape, dt):
            return stack.enter_context(nc.sbuf_tensor(name, shape, dt))

        def sem(name):
            return stack.enter_context(nc.semaphore(name))

        w_sb = sb("w_sb", [P, W_TOTAL], F32)
        c_sb = sb("c_sb", [P, C_TOTAL], F32)
        w1_sb = sb("w1_sb", [P, FC * P], F32)
        w1_hi = sb("w1_hi", [P, FC, P], F16)
        w1_lo = sb("w1_lo", [P, FC, P], F16)
        w1_s = sb("w1_s", [P, FC * P], F32)
        w2_sb = sb("w2_sb", [P, FC, P], F32)
        wg_s = sb("wg_s", [P, E_N], F32)
        wg_hi = sb("wg_hi", [P, E_N], F16)
        wg_lo = sb("wg_lo", [P, E_N], F16)
        wq_rep = sb("wq_rep", [P, H, ROWS], F32)
        wk_rep = sb("wk_rep", [P, H, ROWS], F32)
        kern_sb = sb("kern_sb", [P, P], BF16)
        kbias_sb = sb("kbias_sb", [P, P], BF16)
        kern_q = sb("kern_q", [P, P], BF16)
        gates = sb("gates", [P, 4], F32)
        s_inv = sb("s_inv", [P, 2], F32)
        s_prod = sb("s_prod", [P, 1], F32)
        ident16 = sb("ident16", [P, P], F16)
        identb = sb("identb", [P, P], BF16)
        sel = sb("sel", [P, E_N, P], F16)
        half_neg = sb("half_neg", [P, ST], F32)
        eps = sb("eps", [P, ST], F32)
        carrier = sb("carrier", [P, 1], F32)
        khat = sb("khat", [P, B, T], F32)
        ctx_all = sb("ctx_all", [P, B, T], F32)
        kz = sb("kz", [P, B, T], F32)
        kz_n = sb("kz_n", [P, B, T], F32)
        kz_k = sb("kz_k", [P, B, T], F32)

        ident = c_sb[:, 0:P]

        def w(name):
            a, b = W_COLS[name]
            return w_sb[:, a:b]

        def cst(name):
            a, b = C_COLS[name]
            return c_sb[:, a:b]

        x_in = sb("x_in", [P, ST, D], F32)
        ctx_sb = sb("ctx_sb", [P, T], F32)
        mask_sb = sb("mask_sb", [P, ST, T], I32)
        ctx_rem = sb("ctx_rem", [P, HG, ROWS], F32)
        is_zero = sb("is_zero", [P, ST, T], F32)
        all_zero = sb("all_zero", [P, ST], F32)
        keep = sb("keep", [P, ST], F32)
        fill = sb("fill", [P, ST], F32)
        bias_st = sb("bias_st", [P, ST, T], BF16)
        bias_rem = sb("bias_rem", [P, ST, HG, ROWS], BF16)
        bias_t = sb("bias_t", [P, 2, S], BF16)
        k_hi = sb("k_hi", [P, NG, T], F16)
        kdiag = sb("kdiag", [P, NG, HG, T], F16)
        krem = sb("krem", [P, NG, HG, ROWS], F16)
        vaug = sb("vaug", [P, H, ROWS], F32)
        vrem = sb("vrem", [P, NG, HG, ROWS], F32)
        v1 = sb("v1", [P, 2, D], F32)
        stats = sb("stats", [P, ST, 6], F32)
        mv = sb("mv", [P, ST, 2], F32)
        var_e = sb("var_e", [P, ST], F32)
        rstd = sb("rstd", [P, ST], F32)
        rstd_q = sb("rstd_q", [P, ST], F32)
        xn = sb("xn", [P, ST, D], F32)
        xn_t = sb("xn_t", [P, S], F32)
        q_hi = sb("q_hi", [P, 2, S], F16)
        qst = sb("qst", [P, NG, S], F16)
        neg_max = sb("neg_max", [P, 2, ST, P], F16)
        probs_t = sb("probs_t", [P, 2, HG + 1, S], F32)
        av_t = sb("av_t", [P, 2, S], F32)
        inv_sum = sb("inv_sum", [P, ST, HG], F32)
        att = sb("att", [P, ST, D], F32)
        att_t = sb("att_t", [P, S], F32)
        y_b = sb("y_b", [P, ST, D], F32)
        x1 = sb("x1", [P, ST, D], F32)
        xn_hi = sb("xn_hi", [P, S], F16)
        xn_lo = sb("xn_lo", [P, S], F16)
        logits = sb("logits", [P, ST, E_N], F32)
        top8 = sb("top8", [P, ST, 8], F32)
        top_i = sb("top_i", [P, ST, 8], U32)
        top_f = sb("top_f", [P, ST, 2], F32)
        gap = sb("gap", [P, ST], F32)
        e_gap = sb("e_gap", [P, ST], F32)
        gw = sb("gw", [P, 3, ST], F32)
        pick = sb("pick", [P, 3, ST, E_N], F32)
        comb = sb("comb", [P, ST, P], F16)
        comb_t = sb("comb_t", [P, S], F16)
        h_sb = sb("h_sb", [P, 3, S], F32)
        hc_sb = sb("hc_sb", [P, 3, S], F32)
        ffn_t = sb("ffn_t", [P, S], F32)
        x2 = sb("x2", [P, ST, D], F32)
        q1_t = sb("q1_t", [P, S], F32)
        nmax1 = sb("nmax1", [P, ST], F32)
        sum1 = sb("sum1", [P, ST], F32)
        r1 = sb("r1", [P, ST], F32)
        r1g = sb("r1g", [P, ST], F32)
        p1 = sb("p1", [P, ST, T], F32)
        p1_t = sb("p1_t", [P, 2, S], F32)
        x3 = sb("x3", [P, ST, D], F32)
        xb = sb("xb", [P, ST, D], BF16)
        fv = sb("fv", [P, ST * D], F32)
        fe = sb("fe", [P, ST * D], I32)
        fc = sb("fc", [P, ST * D], F32)
        fw = sb("fw", [P, ST * D], F32)
        fq = sb("fq", [P, ST * D], F32)
        fo = sb("fo", [P, ST * D], F32)
        fn = sb("fn", [P, ST * D], F32)
        xq = sb("xq", [P, ST, D], BF16)
        xq_t = sb("xq_t", [P, S], BF16)
        y_s = sb("y_s", [P, ST, D], BF16)
        y_sb = sb("y_sb", [P, ST, D], BF16)
        x4 = sb("x4", [P, ST, D], F32)

        ps = stack.enter_context(nc.psum_tensor("ps", [P, 8, 512], F32))

        def bank(n):
            return ps[:, n, :]

        def bank16(n, dt):
            return ps[:, n, :].bitcast(dt)

        k_ps = ps[:, 0:2, :].rearrange("p a (b t) -> p (a b) t", b=2)[:, :, 0:T]
        s1_ps = k_ps

        consts_in, early_in, late_in, ctx_all_in, w1_in, w2_in, kern_in = map(
            sem, ["consts_in", "early_in", "late_in", "ctx_all_in", "w1_in", "w2_in", "kern_in"])
        zeros_set, ones_set, gates_set, kc_mm, kc_ready, z_mm, z_reduced, khat_ready = map(
            sem, ["zeros_set", "ones_set", "gates_set", "kc_mm", "kc_ready", "z_mm", "z_reduced", "khat_ready"])
        attn_w_set, ffn_w_set, dve_setup = map(sem, ["attn_w_set", "ffn_w_set", "dve_setup"])
        x_loaded, ctx_loaded, mask_loaded, stored = map(sem, ["x_loaded", "ctx_loaded", "mask_loaded", "stored"])
        dve_step, pool_step = sem("dve_step"), sem("pool_step")
        DVE_STEPS, POOL_STEPS = 34, 4

        PER = {
            "ctx_rem_ready": 1, "mask_zero": 1, "bias_ready": 1, "bias_tr": 1, "bias_t_ready": 1,
            "k_mm": 1, "k_hi_ready": 1, "k_ready": 1, "v_mm": 1, "v_ready": 1,
            "var_ready": 4, "rstd_ready": 4, "xn_ready": 4, "xn_tr": 3, "xn_t_ready": 2,
            "q_mm": NG, "q_hi_ready": NG, "q_ready": NG,
            "max_mm": NG * ST, "max_done": NG * ST, "max_tr": NG, "q_shifted": NG,
            "score_mm": NG * (HG + 1), "probs_ready": NG * (HG + 1), "av_mm": NG, "av_ready": NG,
            "av_tr": NG, "att_ready": NG, "att_tr": 1, "att_t_ready": 1, "y0_mm": 1,
            "y0_read": 1, "x1_ready": 1, "xhi_ready": 1, "xlo_ready": 1, "gate_mm": 1,
            "gate_read": 1, "gap_ready": 1, "e_gap_ready": 1, "comb_ready": 1, "comb_tr": 1,
            "comb_t_ready": 1, "cbc_mm": E_N, "up_mm": FC, "h_ready": FC, "hc_ready": FC,
            "down_mm": FC, "ffn_t_ready": 1, "ffn_tr": 1, "x2_ready": 1, "q1_mm": 1,
            "q1_ready": 1, "s1_mm": 1, "nmax1_ready": 1, "p1_ready": ST, "p1_tr": 1,
            "p1a_ready": 1, "p1b_ready": 1, "o1_mm": 1, "x3_ready": 1, "xq_ready": 1,
            "xq_tr": 1, "xq_t_ready": 1, "y1_mm": 1, "y1_ready": 1, "x4_ready": 1,
        }
        SEM = {name: sem(name) for name in PER}
        def at(name, i, k=None):
            return i * PER[name] + (PER[name] if k is None else k)

        def alone(eng):
            eng.wait_ge(consts_in, 16)

        block = stack.enter_context(nc.Block())

        @block.sync
        def _(sp):
            sp.dma_start(x_in[:, :, :], x_v[0, :, :, :]).then_inc(x_loaded, 16)
            sp.dma_start(c_sb[:, :], consts[:, :]).then_inc(consts_in, 16)
            sp.dma_start(w_sb[:, 0:W_EARLY], wts[:, 0:W_EARLY]).then_inc(early_in, 16)
            sp.dma_start(ctx_sb[:, :], ctx_t[0, :, :]).then_inc(ctx_loaded, 16)
            sp.dma_start(mask_sb[:, :, :], mask_v[0, :, :, :]).then_inc(mask_loaded, 16)
            sp.dma_start(w_sb[:, W_EARLY:W_TOTAL], wts[:, W_EARLY:W_TOTAL]).then_inc(late_in, 16)
            sp.dma_start(ctx_all[:, :, :], ctx_t.rearrange("b d t -> d b t")).then_inc(ctx_all_in, 16)
            sp.dma_start(kern_sb[:, :], kern[:, :]).then_inc(kern_in, 16)
            sp.dma_start(kbias_sb[:, :], kbias[:, :]).then_inc(kern_in, 16)
            sp.dma_start(w1_sb[:, :], w1[:, :]).then_inc(w1_in, 16)
            sp.dma_start(w2_sb[:, :, :], w2.rearrange("p (c d) -> p c d", d=D)).then_inc(w2_in, 16)
            sp.sem_inc(stored, 1)

            with sp.Fori(0, B - 1) as i:
                sp.wait_ge(SEM["v_mm"], at("v_mm", i))
                sp.wait_ge(SEM["ctx_rem_ready"], at("ctx_rem_ready", i))
                sp.dma_start(ctx_sb[:, :], ctx_t[bass.ds(i + 1, 1), :, :].rearrange("a d t -> (a d) t")
                             ).then_inc(ctx_loaded, 16)
                sp.wait_ge(SEM["mask_zero"], at("mask_zero", i))
                sp.dma_start(mask_sb[:, :, :],
                             mask_v[bass.ds(i + 1, 1), :, :, :].rearrange("a p s t -> (a p) s t")
                             ).then_inc(mask_loaded, 16)
                sp.wait_ge(SEM["x1_ready"], at("x1_ready", i))
                sp.dma_start(x_in[:, :, :],
                             x_v[bass.ds(i + 1, 1), :, :, :].rearrange("a p s d -> (a p) s d")
                             ).then_inc(x_loaded, 16)
                sp.wait_ge(SEM["x4_ready"], at("x4_ready", i))
                sp.dma_start(out_v[bass.ds(i, 1), :, :, :].rearrange("a p s d -> (a p) s d"), x4[:, :, :]
                             ).then_inc(stored, 16)
            sp.wait_ge(SEM["x4_ready"], at("x4_ready", B - 1))
            sp.dma_start(out_v[B - 1, :, :, :], x4[:, :, :]).then_inc(stored, 16)
            sp.wait_ge(stored, 16 * B + 1)

        @block.gpsimd
        def _(pool):
            for t in (kdiag, krem, vaug, vrem, neg_max, comb, ctx_rem, wq_rep, wk_rep):
                nc.gpsimd.memset(t[:], 0.0).then_inc(zeros_set, 1)
            nc.gpsimd.memset(bias_rem[:], MASKED).then_inc(zeros_set, 1)
            nc.gpsimd.memset(half_neg[:], -0.5).then_inc(zeros_set, 1)
            nc.gpsimd.memset(eps[:], EPS).then_inc(zeros_set, 1)
            pool.wait_ge(zeros_set, 12)
            nc.gpsimd.memset(vaug[:, :, DK:DK + 1], 1.0).then_inc(ones_set, 1)
            for j in range(HG):
                pool.wait_ge(ones_set, j + 1)
                nc.gpsimd.memset(vrem[ROWS * j:ROWS * j + ROWS, :, j, DK:DK + 1], 1.0).then_inc(ones_set, 1)

            with pool.Fori(0, B) as i:
                steps = [0]

                def settled(ins):
                    steps[0] += 1
                    ins.then_inc(pool_step, 1)
                    pool.wait_ge(pool_step, i * POOL_STEPS + steps[0])

                for n in range(4):
                    pool.wait_ge(SEM["var_ready"], at("var_ready", i, n + 1))
                    settled(nc.gpsimd.tensor_tensor(var_e[:, :], mv[:, :, 1], eps[:, :], ALU.add))
                    nc.gpsimd.tensor_tensor(rstd[:, :], var_e[:, :], half_neg[:, :], ALU.pow
                                            ).then_inc(SEM["rstd_ready"], 1)
                assert steps[0] == POOL_STEPS

        @block.scalar
        def _(act):
            act.wait_ge(early_in, 16)
            nc.scalar.activation(gates[:, :], w("g"), ACT.Tanh).then_inc(gates_set, 1)
            act.wait_ge(late_in, 16)
            act.wait_ge(kc_mm, 1)
            nc.scalar.activation(kz[:, :, :].rearrange("p (h b) t -> p h (b t)", h=2), ps[:, 0:2, 0:2 * T],
                                 ACT.Identity, bias=w("bk1")).then_inc(kc_ready, 1)
            act.wait_ge(z_reduced, 1)
            nc.scalar.activation(khat[:, :, :], kz_n[:, :, :], ACT.Sin).then_inc(khat_ready, 1)
            act.wait_ge(consts_in, 16)

            with act.Fori(0, B) as i:
                act.wait_ge(SEM["k_mm"], at("k_mm", i))
                nc.scalar.activation(k_hi[:, :, :], k_ps, ACT.Identity, bias=cst("one")
                                     ).then_inc(SEM["k_hi_ready"], 1)
                act.wait_ge(SEM["bias_tr"], at("bias_tr", i))
                nc.scalar.activation(bias_t[:, :, :].rearrange("p a s -> p (a s)"), bank16(7, BF16), ACT.Copy
                                     ).then_inc(SEM["bias_t_ready"], 1)
                act.wait_ge(SEM["xn_tr"], at("xn_tr", i, 1))
                nc.scalar.activation(xn_t[:, :], bank(6), ACT.Copy).then_inc(SEM["xn_t_ready"], 1)
                for g in range(NG):
                    act.wait_ge(SEM["q_mm"], at("q_mm", i, g + 1))
                    if g >= 2:
                        act.wait_ge(SEM["q_ready"], at("q_ready", i, g - 1))
                    nc.scalar.activation(q_hi[:, g % 2, :], bank(4 + g % 2), ACT.Copy
                                         ).then_inc(SEM["q_hi_ready"], 1)

                def av_copy(g):
                    act.wait_ge(SEM["av_mm"], at("av_mm", i, g + 1))
                    if g >= 2:
                        act.wait_ge(SEM["av_tr"], at("av_tr", i, g - 1))
                    nc.scalar.activation(av_t[:, g % 2, :], bank(6), ACT.Copy).then_inc(SEM["av_ready"], 1)

                for g in range(NG):
                    for j in range(HG + 1):
                        n = (HG + 1) * g + j
                        act.wait_ge(SEM["score_mm"], at("score_mm", i, n + 1))
                        if g >= 2 and j == 0:
                            act.wait_ge(SEM["av_mm"], at("av_mm", i, g - 1))
                        nc.scalar.activation(probs_t[:, g % 2, j, :], bank(4 + n % 2), ACT.Exp
                                             ).then_inc(SEM["probs_ready"], 1)
                    if g >= 1:
                        av_copy(g - 1)
                av_copy(NG - 1)
                act.wait_ge(SEM["att_tr"], at("att_tr", i))
                nc.scalar.activation(att_t[:, :], bank(7), ACT.Copy).then_inc(SEM["att_t_ready"], 1)

                act.wait_ge(SEM["xn_tr"], at("xn_tr", i, 2))
                nc.scalar.activation(xn_hi[:, :], bank(7), ACT.Copy).then_inc(SEM["xhi_ready"], 1)
                act.wait_ge(SEM["gap_ready"], at("gap_ready", i))
                nc.scalar.activation(e_gap[:, :], gap[:, :], ACT.Exp, scale=1.0 / WS
                                     ).then_inc(SEM["e_gap_ready"], 1)
                act.wait_ge(SEM["comb_tr"], at("comb_tr", i))
                nc.scalar.activation(comb_t[:, :], bank16(7, F16)[:, 0:S], ACT.Copy
                                     ).then_inc(SEM["comb_t_ready"], 1)
                for f in range(FC):
                    act.wait_ge(SEM["up_mm"], at("up_mm", i, f + 1))
                    if f >= 3:
                        act.wait_ge(SEM["hc_ready"], at("hc_ready", i, f - 2))
                    nc.scalar.activation(h_sb[:, f % 3, :], bank(f % 4), ACT.Silu, scale=1.0 / WS
                                         ).then_inc(SEM["h_ready"], 1)
                act.wait_ge(SEM["down_mm"], at("down_mm", i))
                nc.scalar.activation(ffn_t[:, :], bank(6), ACT.Copy).then_inc(SEM["ffn_t_ready"], 1)

                act.wait_ge(SEM["xn_tr"], at("xn_tr", i, 3))
                nc.scalar.activation(xn_t[:, :], bank(6), ACT.Copy).then_inc(SEM["xn_t_ready"], 1)
                act.wait_ge(SEM["q1_mm"], at("q1_mm", i))
                nc.scalar.activation(q1_t[:, :], bank(7), ACT.Identity, bias=w("bq1")
                                     ).then_inc(SEM["q1_ready"], 1)
                act.wait_ge(SEM["nmax1_ready"], at("nmax1_ready", i))
                for s in range(ST):
                    nc.scalar.activation(p1[:, s, :], s1_ps[:, s, :], ACT.Exp, bias=nmax1[:, s:s + 1],
                                         accum_out=sum1[:, s:s + 1]).then_inc(SEM["p1_ready"], 1)
                act.wait_ge(SEM["p1_tr"], at("p1_tr", i))
                nc.scalar.activation(p1_t[0:TH, 0, :], ps[0:TH, 4, :], ACT.Copy).then_inc(SEM["p1a_ready"], 1)

                act.wait_ge(SEM["xq_tr"], at("xq_tr", i))
                nc.scalar.activation(xq_t[:, :], bank16(7, BF16)[:, 0:S], ACT.Copy
                                     ).then_inc(SEM["xq_t_ready"], 1)
                act.wait_ge(SEM["y1_mm"], at("y1_mm", i))
                nc.scalar.activation(y_s[:, :, :].rearrange("p s d -> p (s d)"), bank(6), ACT.Copy,
                                     scale=s_prod[:, 0:1]).then_inc(SEM["y1_ready"], 1)

        @block.vector
        def _(dve):
            setup = [0]

            def set_up(ins):
                setup[0] += 1
                ins.then_inc(dve_setup, 1)
                dve.wait_ge(dve_setup, setup[0])

            def round_e4m3(step, v, n, dst):
                step(nc.vector.tensor_scalar(fe[:, 0:n], v.bitcast(I32), 0x7F800000, None, ALU.bitwise_and))
                step(nc.vector.tensor_scalar(fc[:, 0:n], fe[:, 0:n].bitcast(F32), 2.0 ** -6, 1.5 * 2.0 ** 20,
                                             ALU.max, ALU.mult))
                step(nc.vector.tensor_tensor(fw[:, 0:n], v, fc[:, 0:n], ALU.add))
                step(nc.vector.tensor_tensor(fq[:, 0:n], fw[:, 0:n], fc[:, 0:n], ALU.subtract))
                step(nc.vector.tensor_tensor(fo[:, 0:n], fq[:, 0:n], fq[:, 0:n], ALU.mult))
                step(nc.vector.tensor_scalar(fn[:, 0:n], fo[:, 0:n], 448.0 ** 2, 3.0e38, ALU.is_gt, ALU.mult))
                step(nc.vector.tensor_scalar(fo[:, 0:n], fn[:, 0:n], 3.0e38, 0.0, ALU.mult, ALU.mult))
                return nc.vector.tensor_tensor(dst, fo[:, 0:n], fq[:, 0:n], ALU.add)

            scale = float(DK) ** -0.25
            dve.wait_ge(early_in, 16)
            dve.wait_ge(consts_in, 16)
            dve.wait_ge(zeros_set, 12)
            for r in range(3):
                for dst, src in ((wq_rep, "wq0"), (wk_rep, "wk0")):
                    nc.vector.tensor_scalar(dst[:, :, DK * r:DK * r + DK],
                                            w(src).rearrange("p (h k) -> p h k", k=DK), scale, None, ALU.mult)
            nc.vector.tensor_copy(ident16[:, :], ident)
            nc.vector.tensor_copy(identb[:, :], ident).then_inc(attn_w_set, 1)
            nc.vector.tensor_tensor(sel[:, :, :],
                                    ident[:, 0:E_N].unsqueeze(2).broadcast_to([P, E_N, P]),
                                    ident[:, E_N:2 * E_N].unsqueeze(2).broadcast_to([P, E_N, P]), ALU.add)
            set_up(nc.vector.reciprocal(s_inv[:, :], w("s")))
            nc.vector.tensor_tensor(s_prod[:, :], w("s")[:, 0:1], w("s")[:, 1:2], ALU.mult)
            dve.wait_ge(kern_in, 32)
            set_up(nc.vector.tensor_scalar(fv[:, 0:P], kern_sb[:, :], s_inv[:, 1:2], None, ALU.mult))
            set_up(round_e4m3(set_up, fv[:, 0:P], P, kern_q[:, :]))
            dve.wait_ge(late_in, 16)
            set_up(nc.vector.tensor_scalar(wg_s[:, :], w("wg"), WS, None, ALU.mult))
            set_up(nc.vector.tensor_copy(wg_hi[:, :], wg_s[:, :]))
            nc.vector.tensor_tensor(wg_lo[:, :], wg_s[:, :], wg_hi[:, :], ALU.subtract)
            dve.wait_ge(z_mm, 1)
            zf = kz[:, :, :].rearrange("p b t -> p (b t)")
            rf = kz_n[:, :, :].rearrange("p b t -> p (b t)")
            nf = kz_k[:, :, :].rearrange("p b t -> p (b t)")
            set_up(nc.vector.tensor_scalar(kz[:, :, :].rearrange("p (h b) t -> p h (b t)", h=2),
                                           ps[:, 2:4, 0:2 * T], w("br1"), None, ALU.add))
            set_up(nc.vector.tensor_scalar(zf, zf, TWO_PI / 4, None, ALU.add))
            set_up(nc.vector.tensor_scalar(nf, zf, 1.0 / TWO_PI, ROUND, ALU.mult, ALU.add))
            set_up(nc.vector.tensor_scalar(nf, nf, ROUND, None, ALU.subtract))
            set_up(nc.vector.scalar_tensor_tensor(out=rf, in0=nf, scalar=-TWO_PI_HI, in1=zf,
                                                  op0=ALU.mult, op1=ALU.add))
            set_up(nc.vector.scalar_tensor_tensor(out=zf, in0=nf, scalar=-TWO_PI_LO, in1=rf,
                                                  op0=ALU.mult, op1=ALU.add))
            nc.vector.tensor_scalar(rf, zf, PI, -PI, ALU.min, ALU.max).then_inc(z_reduced, 1)
            dve.wait_ge(w1_in, 16)
            w1_hf = w1_hi[:, :, :].rearrange("p c f -> p (c f)")
            w1_lf = w1_lo[:, :, :].rearrange("p c f -> p (c f)")
            set_up(nc.vector.tensor_scalar(w1_s[:, :], w1_sb[:, :], WS, None, ALU.mult))
            set_up(nc.vector.tensor_copy(w1_hf, w1_s[:, :]))
            nc.vector.tensor_tensor(w1_lf, w1_s[:, :], w1_hf, ALU.subtract).then_inc(ffn_w_set, 1)
            dve.wait_ge(gates_set, 1)
            dve.wait_ge(ones_set, HG + 1)

            with dve.Fori(0, B) as i:
                steps = [0]

                def settled(ins):
                    steps[0] += 1
                    ins.then_inc(dve_step, 1)
                    dve.wait_ge(dve_step, i * DVE_STEPS + steps[0])

                def layer_norm(n, src, dst):
                    for s in range(ST):
                        last = nc.vector.bn_stats(stats[:, s, :], src[:, s, :])
                    settled(last)
                    nc.vector.memset(carrier[:, :], 0.0)
                    for s in range(ST):
                        last = nc.vector.bn_aggr(mv[:, s, :], stats[:, s, :])
                    last.then_inc(SEM["var_ready"], 1)
                    dve.wait_ge(SEM["rstd_ready"], at("rstd_ready", i, n + 1))
                    by = rstd
                    if n == 0:
                        settled(nc.vector.tensor_tensor(rstd_q[:, :], rstd[:, :], keep[:, :], ALU.mult))
                        by = rstd_q
                    for s in range(ST):
                        last = nc.vector.tensor_scalar(dst[:, s, :], src[:, s, :], mv[:, s, 0:1],
                                                       by[:, s:s + 1], ALU.subtract, ALU.mult)
                    last.then_inc(SEM["xn_ready"], 1)

                dve.wait_ge(ctx_loaded, i * 16 + 16)
                nc.vector.tensor_copy(ctx_rem[:, :, 0:TR],
                                      ctx_sb[:, T0:T].unsqueeze(1).broadcast_to([P, HG, TR])
                                      ).then_inc(SEM["ctx_rem_ready"], 1)
                dve.wait_ge(mask_loaded, i * 16 + 16)
                nc.vector.tensor_scalar(is_zero[:, :, :], mask_sb[:, :, :], 0.0, None, ALU.is_equal
                                        ).then_inc(SEM["mask_zero"], 1)
                dve.wait_ge(SEM["mask_zero"], at("mask_zero", i))
                settled(nc.vector.tensor_reduce(all_zero[:, :], is_zero[:, :, :], X, ALU.min))
                settled(nc.vector.tensor_scalar(keep[:, :], all_zero[:, :], -1.0, 1.0, ALU.mult, ALU.add))
                settled(nc.vector.tensor_scalar(fill[:, :], keep[:, :], MASKED, None, ALU.mult))
                nc.vector.tensor_tensor(bias_st[:, :, :], is_zero[:, :, :],
                                        fill[:, :].unsqueeze(2).broadcast_to([P, ST, T]), ALU.mult)
                for j in range(HG):
                    last = nc.vector.tensor_tensor(bias_rem[:, :, j, 0:TR], is_zero[:, :, T0:T],
                                                   fill[:, :].unsqueeze(2).broadcast_to([P, ST, TR]), ALU.mult)
                last.then_inc(SEM["bias_ready"], 1)

                dve.wait_ge(SEM["k_hi_ready"], at("k_hi_ready", i))
                for j in range(HG):
                    r = slice(ROWS * j, ROWS * j + ROWS)
                    last = nc.vector.scalar_tensor_tensor(out=kdiag[r, :, j, :], in0=k_hi[r, :, :],
                                                          scalar=cst("lo_k")[r, :], in1=k_ps[r, :, :],
                                                          op0=ALU.mult, op1=ALU.add)
                settled(last)
                for j in range(HG):
                    r = slice(ROWS * j, ROWS * j + ROWS)
                    last = nc.vector.tensor_copy(krem[r, :, j, 0:TR], kdiag[r, :, j, T0:T])
                last.then_inc(SEM["k_ready"], 1)
                dve.wait_ge(SEM["v_mm"], at("v_mm", i))
                nc.vector.tensor_copy(vaug[:, :, 0:DK], ps[:, 4, 0:P].rearrange("p (h k) -> p h k", k=DK))
                for j in range(HG):
                    r = slice(ROWS * j, ROWS * j + ROWS)
                    nc.vector.tensor_copy(vrem[r, :, j, 0:DK],
                                          ps[r, 4, P:2 * P].rearrange("p (g j k) -> p g j k", j=HG, k=DK)[:, :, j, :])
                nc.vector.tensor_tensor(v1[0:TH, :, :], ps[0:TH, 4, 2 * P:4 * P].rearrange("p (c d) -> p c d", c=2),
                                        w("bv1")[0:TH, :].unsqueeze(1).broadcast_to([TH, 2, D]), ALU.add
                                        ).then_inc(SEM["v_ready"], 1)

                dve.wait_ge(x_loaded, i * 16 + 16)
                layer_norm(0, x_in, xn)
                for g in range(NG):
                    dve.wait_ge(SEM["q_hi_ready"], at("q_hi_ready", i, g + 1))
                    nc.vector.scalar_tensor_tensor(out=qst[:, g, :], in0=q_hi[:, g % 2, :], scalar=cst("lo_q"),
                                                   in1=bank(4 + g % 2), op0=ALU.mult, op1=ALU.add
                                                   ).then_inc(SEM["q_ready"], 1)

                def row_max(g):
                    for s in range(ST):
                        n = ST * g + s
                        u = n % 2
                        dve.wait_ge(SEM["max_mm"], at("max_mm", i, n + 1))
                        nc.vector.tensor_reduce(
                            neg_max[:, g % 2, s, :].rearrange("p (j r) -> p j r", r=ROWS)[:, :, MROW],
                            ps[:, 2 * u:2 * u + 2, 0:2 * T].rearrange("p a (h t) -> p a h t", t=T),
                            X, ALU.max, negate=True).then_inc(SEM["max_done"], 1)

                def shift(g):
                    dve.wait_ge(SEM["max_tr"], at("max_tr", i, g + 1))
                    nc.vector.tensor_tensor(qst[:, g, :], qst[:, g, :], bank16(7, F16)[:, 0:S], ALU.add
                                            ).then_inc(SEM["q_shifted"], 1)

                def normalize(g):
                    dve.wait_ge(SEM["av_tr"], at("av_tr", i, g + 1))
                    o = bank(7).rearrange("p (s j r) -> p s j r", s=ST, r=ROWS)
                    settled(nc.vector.reciprocal(inv_sum[:, :, :], o[:, :, :, DK]))
                    nc.vector.tensor_tensor(
                        att[:, :, ROWS * g:ROWS * g + ROWS].rearrange("p s (j k) -> p s j k", k=DK),
                        o[:, :, :, 0:DK], inv_sum[:, :, :].unsqueeze(3).broadcast_to([P, ST, HG, DK]), ALU.mult
                    ).then_inc(SEM["att_ready"], 1)

                row_max(0)
                row_max(1)
                shift(0)
                for g in range(NG):
                    if g + 2 < NG:
                        row_max(g + 2)
                    if g + 1 < NG:
                        shift(g + 1)
                    if g >= 1:
                        normalize(g - 1)
                normalize(NG - 1)

                dve.wait_ge(SEM["y0_mm"], at("y0_mm", i))
                nc.vector.tensor_tensor(y_b[:, :, :], bank(6).rearrange("p (s d) -> p s d", d=D),
                                        w("bu0").unsqueeze(1).broadcast_to([P, ST, D]), ALU.add
                                        ).then_inc(SEM["y0_read"], 1)
                dve.wait_ge(SEM["y0_read"], at("y0_read", i))
                nc.vector.scalar_tensor_tensor(out=x1[:, :, :], in0=y_b[:, :, :], scalar=gates[:, 0:1],
                                               in1=x_in[:, :, :], op0=ALU.mult, op1=ALU.add
                                               ).then_inc(SEM["x1_ready"], 1)
                dve.wait_ge(SEM["x1_ready"], at("x1_ready", i))

                layer_norm(1, x1, xn)
                dve.wait_ge(SEM["xhi_ready"], at("xhi_ready", i))
                nc.vector.tensor_tensor(xn_lo[:, :], bank(7), xn_hi[:, :], ALU.subtract
                                        ).then_inc(SEM["xlo_ready"], 1)
                dve.wait_ge(SEM["gate_mm"], at("gate_mm", i))
                nc.vector.tensor_copy(logits[:, :, :], bank(6)[:, 0:ST * E_N].rearrange("p (s e) -> p s e", e=E_N)
                                      ).then_inc(SEM["gate_read"], 1)
                alone(dve)
                dve.wait_ge(SEM["gate_read"], at("gate_read", i))
                for s in range(ST):
                    last = nc.vector.max(top8[:, s, :], logits[:, s, :])
                settled(last)
                nc.vector.tensor_tensor(gap[:, :], top8[:, :, 1], top8[:, :, 0], ALU.subtract
                                        ).then_inc(SEM["gap_ready"], 1)
                for s in range(ST):
                    last = nc.vector.max_index(top_i[:, s, :], top8[:, s, :], logits[:, s, :])
                settled(last)
                settled(nc.vector.tensor_copy(top_f[:, :, :], top_i[:, :, 0:2]))
                dve.wait_ge(SEM["e_gap_ready"], at("e_gap_ready", i))
                settled(nc.vector.tensor_scalar(gw[:, 0, :], e_gap[:, :], 1.0, None, ALU.add))
                settled(nc.vector.reciprocal(gw[:, 1, :], gw[:, 0, :]))
                nc.vector.tensor_tensor(gw[:, 2, :], e_gap[:, :], gw[:, 1, :], ALU.mult)
                for k in range(2):
                    settled(nc.vector.tensor_tensor(pick[:, k, :, :],
                                                    cst("iota").unsqueeze(1).broadcast_to([P, ST, E_N]),
                                                    top_f[:, :, k].unsqueeze(2).broadcast_to([P, ST, E_N]),
                                                    ALU.is_equal))
                    settled(nc.vector.tensor_tensor(pick[:, k, :, :], pick[:, k, :, :],
                                                    gw[:, k + 1, :].unsqueeze(2).broadcast_to([P, ST, E_N]),
                                                    ALU.mult))
                settled(nc.vector.tensor_tensor(pick[:, 2, :, :], pick[:, 0, :, :], pick[:, 1, :, :], ALU.add))
                settled(nc.vector.tensor_copy(comb[:, :, 0:E_N], pick[:, 2, :, :]))
                nc.vector.tensor_tensor(comb[:, :, E_N:2 * E_N], pick[:, 2, :, :], comb[:, :, 0:E_N],
                                        ALU.subtract).then_inc(SEM["comb_ready"], 1)
                for f in range(FC):
                    e = f * P // F_N
                    dve.wait_ge(SEM["h_ready"], at("h_ready", i, f + 1))
                    dve.wait_ge(SEM["cbc_mm"], at("cbc_mm", i, e + 1))
                    if f >= 3:
                        dve.wait_ge(SEM["down_mm"], at("down_mm", i, f - 2))
                    nc.vector.tensor_tensor(hc_sb[:, f % 3, :], h_sb[:, f % 3, :], bank(4 + e % 2), ALU.mult
                                            ).then_inc(SEM["hc_ready"], 1)
                dve.wait_ge(SEM["ffn_tr"], at("ffn_tr", i))
                nc.vector.scalar_tensor_tensor(out=x2[:, :, :].rearrange("p s d -> p (s d)"), in0=bank(7),
                                               scalar=gates[:, 1:2],
                                               in1=x1[:, :, :].rearrange("p s d -> p (s d)"),
                                               op0=ALU.mult, op1=ALU.add).then_inc(SEM["x2_ready"], 1)
                dve.wait_ge(SEM["x2_ready"], at("x2_ready", i))

                layer_norm(2, x2, xn)
                dve.wait_ge(SEM["s1_mm"], at("s1_mm", i))
                nc.vector.tensor_reduce(nmax1[:, :], s1_ps, X, ALU.max, negate=True
                                        ).then_inc(SEM["nmax1_ready"], 1)
                dve.wait_ge(SEM["p1_ready"], at("p1_ready", i))
                settled(nc.vector.reciprocal(r1[:, :], sum1[:, :]))
                nc.vector.tensor_scalar(r1g[:, :], r1[:, :], gates[:, 2:3], None, ALU.mult)
                dve.wait_ge(SEM["p1_tr"], at("p1_tr", i))
                nc.vector.tensor_copy(p1_t[0:TH, 1, :], ps[0:TH, 5, :]).then_inc(SEM["p1b_ready"], 1)
                dve.wait_ge(SEM["p1b_ready"], at("p1b_ready", i))
                dve.wait_ge(SEM["o1_mm"], at("o1_mm", i))
                for s in range(ST):
                    last = nc.vector.scalar_tensor_tensor(out=x3[:, s, :], in0=bank(6)[:, D * s:D * s + D],
                                                          scalar=r1g[:, s:s + 1], in1=x2[:, s, :],
                                                          op0=ALU.mult, op1=ALU.add)
                last.then_inc(SEM["x3_ready"], 1)
                dve.wait_ge(SEM["x3_ready"], at("x3_ready", i))

                layer_norm(3, x3, xb)
                dve.wait_ge(SEM["xn_ready"], at("xn_ready", i))
                settled(nc.vector.tensor_scalar(fv[:, :], xb[:, :, :].rearrange("p s d -> p (s d)"),
                                                s_inv[:, 0:1], None, ALU.mult))
                round_e4m3(settled, fv[:, :], ST * D, xq[:, :, :].rearrange("p s d -> p (s d)")
                           ).then_inc(SEM["xq_ready"], 1)
                dve.wait_ge(SEM["y1_ready"], at("y1_ready", i))
                settled(nc.vector.tensor_tensor(y_sb[:, :, :], y_s[:, :, :],
                                                kbias_sb[:, :].unsqueeze(1).broadcast_to([P, ST, D]), ALU.add))
                dve.wait_ge(stored, i * 16 + 1)
                nc.vector.scalar_tensor_tensor(out=x4[:, :, :], in0=y_sb[:, :, :], scalar=gates[:, 3:4],
                                               in1=x3[:, :, :], op0=ALU.mult, op1=ALU.add
                                               ).then_inc(SEM["x4_ready"], 1)
                assert steps[0] == DVE_STEPS, steps[0]

        @block.tensor
        def _(pe):
            pe.wait_ge(late_in, 16)
            pe.wait_ge(ctx_all_in, 16)
            for h in range(2):
                last = nc.tensor.matmul(ps[:, h, 0:2 * T], w("wk1"),
                                        ctx_all[:, 2 * h:2 * h + 2, :].rearrange("p b t -> p (b t)"),
                                        start=True, stop=True)
            last.then_inc(kc_mm, 1)
            pe.wait_ge(kc_ready, 1)
            for h in range(2):
                last = nc.tensor.matmul(ps[:, 2 + h, 0:2 * T], w("wr1"),
                                        kz[:, 2 * h:2 * h + 2, :].rearrange("p b t -> p (b t)"),
                                        start=True, stop=True)
            last.then_inc(z_mm, 1)
            pe.wait_ge(attn_w_set, 1)

            def transposes(dst, src, idn):
                for s in range(ST):
                    last = nc.tensor.transpose(dst[:, P * s:P * s + P], src[:, s, :], idn)
                return last

            with pe.Fori(0, B) as i:
                pe.wait_ge(ctx_loaded, i * 16 + 16)
                pe.wait_ge(z_reduced, 1)
                for g in range(NG):
                    last = nc.tensor.matmul(k_ps[:, g, :], wk_rep[:, HG * g:HG * g + HG, :].rearrange(
                        "p h r -> p (h r)"), ctx_sb[:, :], start=True, stop=True)
                last.then_inc(SEM["k_mm"], 1)
                pe.wait_ge(SEM["ctx_rem_ready"], at("ctx_rem_ready", i))
                nc.tensor.matmul(ps[:, 4, 0:P], ctx_sb[:, 0:T0], w("wv0"), start=True, stop=True)
                nc.tensor.matmul(ps[:, 4, P:2 * P], ctx_rem[:, :, :].rearrange("p j r -> p (j r)"), w("wv0"),
                                 start=True, stop=True)
                for c in range(2):
                    last = nc.tensor.matmul(ps[0:TH, 4, (2 + c) * P:(3 + c) * P], ctx_sb[:, TH * c:TH * c + TH],
                                            w("wv1"), start=True, stop=True)
                last.then_inc(SEM["v_mm"], 1)
                pe.wait_ge(SEM["bias_ready"], at("bias_ready", i))
                b7 = bank16(7, BF16)
                transposes(b7[:, 0:S], bias_st[:, :, 0:T0], identb[:, :])
                transposes(b7[:, S:2 * S], bias_rem[:, :, :, :].rearrange("p s j r -> p s (j r)"), identb[:, :]
                           ).then_inc(SEM["bias_tr"], 1)
                pe.wait_ge(SEM["xn_ready"], at("xn_ready", i, 1))
                transposes(bank(6), xn, ident).then_inc(SEM["xn_tr"], 1)
                pe.wait_ge(SEM["xn_t_ready"], at("xn_t_ready", i, 1))
                for g in range(NG):
                    if g == 0:
                        pe.wait_ge(SEM["v_ready"], at("v_ready", i))
                    elif g >= 2:
                        pe.wait_ge(SEM["q_ready"], at("q_ready", i, g - 1))
                    nc.tensor.matmul(bank(4 + g % 2), wq_rep[:, HG * g:HG * g + HG, :].rearrange(
                        "p h r -> p (h r)"), xn_t[:, :], start=True, stop=True).then_inc(SEM["q_mm"], 1)

                def row_scores(g):
                    pe.wait_ge(SEM["q_ready"], at("q_ready", i, g + 1))
                    if g == 0:
                        pe.wait_ge(SEM["k_ready"], at("k_ready", i))
                    for s in range(ST):
                        n = ST * g + s
                        if n >= 2:
                            pe.wait_ge(SEM["max_done"], at("max_done", i, n - 1))
                        for h in range(2):
                            b = ps[:, 2 * (n % 2) + h, 0:2 * T]
                            nc.tensor.matmul(b, qst[:, g, P * s:P * s + P],
                                             kdiag[:, g, 2 * h:2 * h + 2, :].rearrange("p h t -> p (h t)"),
                                             start=True, stop=False)
                            last = nc.tensor.matmul(b.rearrange("p (h t) -> p h t", h=2), identb[:, :],
                                                    bias_st[:, s, :].unsqueeze(1).broadcast_to([P, 2, T]),
                                                    start=False, stop=True)
                        last.then_inc(SEM["max_mm"], 1)

                def max_rows(g):
                    pe.wait_ge(SEM["max_done"], at("max_done", i, ST * (g + 1)))
                    if g == 0:
                        pe.wait_ge(SEM["bias_t_ready"], at("bias_t_ready", i))
                    if g >= 3:
                        pe.wait_ge(SEM["att_ready"], at("att_ready", i, g - 2))
                    transposes(bank16(7, F16)[:, 0:S], neg_max[:, g % 2, :, :], ident16[:, :]
                               ).then_inc(SEM["max_tr"], 1)

                def scores(g):
                    pe.wait_ge(SEM["q_shifted"], at("q_shifted", i, g + 1))
                    for j in range(HG + 1):
                        n = (HG + 1) * g + j
                        if n >= 2:
                            pe.wait_ge(SEM["probs_ready"], at("probs_ready", i, n - 1))
                        keys = (kdiag[:, g, j, 0:T0] if j < HG else
                                krem[:, g, :, :].rearrange("p j r -> p (j r)"))
                        nc.tensor.matmul(bank(4 + n % 2), keys, qst[:, g, :], start=True, stop=False)
                        nc.tensor.matmul(bank(4 + n % 2), identb[:, :], bias_t[:, j // HG, :],
                                         start=False, stop=True).then_inc(SEM["score_mm"], 1)

                def weighted_v(g):
                    if g == 0:
                        pe.wait_ge(SEM["xn_t_ready"], at("xn_t_ready", i, 1))
                    else:
                        pe.wait_ge(SEM["av_ready"], at("av_ready", i, g))
                    for j in range(HG):
                        pe.wait_ge(SEM["probs_ready"], at("probs_ready", i, (HG + 1) * g + j + 1))
                        nc.tensor.matmul(ps[ROWS * j:ROWS * j + ROWS, 6, :], vaug[:, HG * g + j, :],
                                         probs_t[:, g % 2, j, :], start=True, stop=False, skip_group_check=True)
                    pe.wait_ge(SEM["probs_ready"], at("probs_ready", i, (HG + 1) * (g + 1)))
                    nc.tensor.matmul(bank(6), vrem[:, g, :, :].rearrange("p j r -> p (j r)"),
                                     probs_t[:, g % 2, HG, :], start=False, stop=True, skip_group_check=True
                                     ).then_inc(SEM["av_mm"], 1)

                def values_back(g):
                    pe.wait_ge(SEM["av_ready"], at("av_ready", i, g + 1))
                    pe.wait_ge(SEM["q_shifted"], at("q_shifted", i, min(g + 3, NG)))
                    if g >= 1:
                        pe.wait_ge(SEM["att_ready"], at("att_ready", i, g))
                    transposes(bank(7), av_t[:, g % 2, :].rearrange("p (s q) -> p s q", q=P), ident
                               ).then_inc(SEM["av_tr"], 1)

                row_scores(0)
                row_scores(1)
                max_rows(0)
                for g in range(NG):
                    scores(g)
                    if g + 2 < NG:
                        row_scores(g + 2)
                    if g + 1 < NG:
                        if g + 1 == 1:
                            pe.wait_ge(SEM["q_shifted"], at("q_shifted", i, 1))
                        max_rows(g + 1)
                    weighted_v(g)
                    if g >= 1:
                        values_back(g - 1)
                values_back(NG - 1)

                pe.wait_ge(SEM["att_ready"], at("att_ready", i))
                transposes(bank(7), att, ident).then_inc(SEM["att_tr"], 1)
                pe.wait_ge(SEM["att_t_ready"], at("att_t_ready", i))
                for s in range(ST):
                    last = nc.tensor.matmul(bank(6)[:, D * s:D * s + D], att_t[:, P * s:P * s + P], w("wu0"),
                                            start=True, stop=True)
                last.then_inc(SEM["y0_mm"], 1)

                pe.wait_ge(SEM["xn_ready"], at("xn_ready", i, 2))
                transposes(bank(7), xn, ident).then_inc(SEM["xn_tr"], 1)
                pe.wait_ge(ffn_w_set, 1)
                pe.wait_ge(SEM["xlo_ready"], at("xlo_ready", i))
                pe.wait_ge(SEM["y0_read"], at("y0_read", i))
                for s in range(ST):
                    o = bank(6)[:, E_N * s:E_N * s + E_N]
                    hi, lo = xn_hi[:, P * s:P * s + P], xn_lo[:, P * s:P * s + P]
                    nc.tensor.matmul(o, hi, wg_hi[:, :], start=True, stop=False)
                    nc.tensor.matmul(o, hi, wg_lo[:, :], start=False, stop=False)
                    last = nc.tensor.matmul(o, lo, wg_hi[:, :], start=False, stop=True)
                last.then_inc(SEM["gate_mm"], 1)

                def up(f):
                    if f >= 4:
                        pe.wait_ge(SEM["h_ready"], at("h_ready", i, f - 3))
                    nc.tensor.matmul(bank(f % 4), w1_hi[:, f, :], xn_hi[:, :], start=True, stop=False)
                    nc.tensor.matmul(bank(f % 4), w1_hi[:, f, :], xn_lo[:, :], start=False, stop=False)
                    nc.tensor.matmul(bank(f % 4), w1_lo[:, f, :], xn_hi[:, :], start=False, stop=True
                                     ).then_inc(SEM["up_mm"], 1)

                def spread(e):
                    if e >= 2:
                        pe.wait_ge(SEM["hc_ready"], at("hc_ready", i, 2 * (e - 1)))
                    nc.tensor.matmul(bank(4 + e % 2), sel[:, e, :], comb_t[:, :], start=True, stop=True
                                     ).then_inc(SEM["cbc_mm"], 1)

                def down(f):
                    pe.wait_ge(SEM["hc_ready"], at("hc_ready", i, f + 1))
                    nc.tensor.matmul(bank(6), w2_sb[:, f, :], hc_sb[:, f % 3, :], start=(f == 0),
                                     stop=(f == FC - 1)).then_inc(SEM["down_mm"], 1)

                for f in range(3):
                    up(f)
                pe.wait_ge(SEM["comb_ready"], at("comb_ready", i))
                transposes(bank16(7, F16)[:, 0:S], comb, ident16[:, :]).then_inc(SEM["comb_tr"], 1)
                pe.wait_ge(SEM["comb_t_ready"], at("comb_t_ready", i))
                pe.wait_ge(w2_in, 16)
                spread(0)
                for f in range(FC):
                    if f % 2 == 0 and f // 2 + 1 < E_N:
                        spread(f // 2 + 1)
                    if f + 3 < FC:
                        up(f + 3)
                    down(f)
                pe.wait_ge(SEM["ffn_t_ready"], at("ffn_t_ready", i))
                transposes(bank(7), ffn_t[:, :].rearrange("p (s q) -> p s q", q=P), ident
                           ).then_inc(SEM["ffn_tr"], 1)

                pe.wait_ge(SEM["xn_ready"], at("xn_ready", i, 3))
                transposes(bank(6), xn, ident).then_inc(SEM["xn_tr"], 1)
                pe.wait_ge(SEM["xn_t_ready"], at("xn_t_ready", i, 2))
                pe.wait_ge(SEM["x2_ready"], at("x2_ready", i))
                nc.tensor.matmul(bank(7), w("wq1"), xn_t[:, :], start=True, stop=True
                                 ).then_inc(SEM["q1_mm"], 1)
                pe.wait_ge(SEM["q1_ready"], at("q1_ready", i))
                pe.wait_ge(khat_ready, 1)
                for s in range(ST):
                    last = nc.tensor.matmul(s1_ps[:, s, :], q1_t[:, P * s:P * s + P],
                                            khat[:, bass.ds(i, 1), :].rearrange("p b t -> p (b t)"),
                                            start=True, stop=True)
                last.then_inc(SEM["s1_mm"], 1)
                for s in range(ST):
                    pe.wait_ge(SEM["p1_ready"], at("p1_ready", i, s + 1))
                    for c in range(2):
                        last = nc.tensor.transpose(ps[0:TH, 4 + c, P * s:P * s + P],
                                                   p1[:, s, TH * c:TH * c + TH], ident)
                last.then_inc(SEM["p1_tr"], 1)
                pe.wait_ge(SEM["p1a_ready"], at("p1a_ready", i))
                pe.wait_ge(SEM["p1b_ready"], at("p1b_ready", i))
                for s in range(ST):
                    for c in range(2):
                        last = nc.tensor.matmul(bank(6)[:, D * s:D * s + D], p1_t[0:TH, c, P * s:P * s + P],
                                                v1[0:TH, c, :], start=(c == 0), stop=(c == 1))
                last.then_inc(SEM["o1_mm"], 1)

                pe.wait_ge(SEM["xq_ready"], at("xq_ready", i))
                transposes(bank16(7, BF16)[:, 0:S], xq, identb[:, :]).then_inc(SEM["xq_tr"], 1)
                pe.wait_ge(SEM["xq_t_ready"], at("xq_t_ready", i))
                pe.wait_ge(SEM["x3_ready"], at("x3_ready", i))
                for s in range(ST):
                    last = nc.tensor.matmul(bank(6)[:, D * s:D * s + D], xq_t[:, P * s:P * s + P], kern_q[:, :],
                                            start=True, stop=True)
                last.then_inc(SEM["y1_mm"], 1)


def kernel(**inputs):
    import numpy as _np
    import concourse.bacc as _bacc
    from concourse import mybir as _mybir
    from concourse.bass_utils import run_bass_kernel_spmd as _run

    a = {n: _np.asarray(v) for n, v in inputs.items()}

    def rows(v):
        return _np.broadcast_to(v.reshape(1, -1), (P, v.size))

    def heads(v):
        return v.transpose(1, 0, 2).reshape(P, P)

    parts = {
        "wq0": heads(a["L0_xattn_Wq"]), "wk0": heads(a["L0_xattn_Wk"]), "wv0": heads(a["L0_xattn_Wv"]),
        "wu0": a["L0_xattn_Wu"], "bu0": rows(a["L0_xattn_bu"]),
        "g": rows(_np.stack([a["g_xattn"], a["g_ffn"]], 1)),
        "s": rows(_np.concatenate([a["L1_ffn_input_scale"], a["L1_ffn_kernel_scale"]])),
        "wg": a["L0_ffn_Wg"], "wq1": a["L1_xattn_Wq"], "wk1": a["L1_xattn_Wk"], "wv1": a["L1_xattn_Wv"],
        "wr1": a["L1_xattn_Wr"], "bq1": a["L1_xattn_bq"].reshape(P, 1), "bk1": a["L1_xattn_bk"].reshape(P, 1),
        "br1": a["L1_xattn_br"].reshape(P, 1), "bv1": rows(a["L1_xattn_bv"]),
    }
    wts = _np.concatenate([parts[n] for n in W_COLS], 1)
    row = _np.arange(P) % ROWS
    part = row // DK
    consts = _np.zeros((P, C_TOTAL), _np.float32)
    consts[:, 0:P] = _np.eye(P)
    consts[:, C_COLS["lo_q"][0]] = -(part == 1).astype(_np.float32)
    consts[:, C_COLS["lo_k"][0]] = (row == MROW).astype(_np.float32) - (part == 2)
    consts[:, C_COLS["one"][0]] = row == MROW
    consts[:, slice(*C_COLS["iota"])] = _np.arange(E_N)
    arrays = {
        "x": a["x"],
        "ctx_t": a["ctx_1024"].transpose(0, 2, 1),
        "mask": a["mask_BxSxS2_ik1"],
        "wts": wts,
        "w1": a["L0_ffn_W1"].transpose(1, 0, 2).reshape(P, -1),
        "w2": a["L0_ffn_W2"].reshape(FC, P, P).transpose(1, 0, 2).reshape(P, -1),
        "kern": a["L1_ffn_kernel"],
        "kbias": rows(a["L1_ffn_bias"]),
        "consts": consts,
    }
    arrays = {n: _np.ascontiguousarray(v) for n, v in arrays.items()}
    nc = _bacc.Bacc("TRN2", target_bir_lowering=False, num_devices=1)
    args = [nc.dram_tensor(n, v.shape, _mybir.dt.from_np(v.dtype), kind="ExternalInput").ap()
            for n, v in arrays.items()]
    out = nc.dram_tensor("out", a["x"].shape, F32, kind="ExternalOutput").ap()
    flamingo_gated(nc, *args, out)
    return _run(nc, [arrays], core_ids=[0]).results[0]["out"]
```

```python
from contextlib import ExitStack

import concourse.bass as bass
from concourse import mybir

P = 128
ALU = mybir.AluOpType
ACT = mybir.ActivationFunctionType
X = mybir.AxisListType.X
F32 = mybir.dt.float32
BF16 = mybir.dt.bfloat16
F16 = mybir.dt.float16
I32 = mybir.dt.int32
U32 = mybir.dt.uint32

H, DK = 16, 8
HG = 4
NG = H // HG
ROWS = P // HG
MROW = 3 * DK
E_N, F_N = 8, 256
FC = E_N * F_N // P
WS = 64.0
MASKED = -1.0e30
EPS = 1e-5
TWO_PI = 6.283185307179586
TWO_PI_HI = 6.28125
TWO_PI_LO = TWO_PI - TWO_PI_HI
PI = 3.1415925
ROUND = 12582912.0

W_COLS = {}
_at = 0
for _name, _n in [("wq0", 128), ("wk0", 128), ("wv0", 128), ("wu0", 128), ("bu0", 128), ("g", 4), ("s", 2),
                  ("wg", 8), ("wq1", 128), ("wk1", 128), ("wv1", 128), ("wr1", 128), ("bq1", 1), ("bk1", 1),
                  ("br1", 1), ("bv1", 128)]:
    W_COLS[_name] = (_at, _at + _n)
    _at += _n
W_TOTAL = _at
W_EARLY = W_COLS["wg"][0]
C_COLS = {"ident": (0, 128), "lo_q": (128, 129), "lo_k": (129, 130), "one": (130, 131), "iota": (131, 139)}
C_TOTAL = 139


def flamingo_gated(nc, x, ctx_t, mask, wts, w1, w2, kern, kbias, consts, out):
    B, S, D = x.shape
    T = ctx_t.shape[2]
    ST = S // P
    T0 = P
    TR = T - T0
    TH = T // 2
    assert D == P and TR <= ROWS and T % 2 == 0

    x_v = x.rearrange("b (s p) d -> b p s d", p=P)
    out_v = out.rearrange("b (s p) d -> b p s d", p=P)
    mask_v = mask.rearrange("b (s p) t -> b p s t", p=P)

    with ExitStack() as stack:
        def sb(name, shape, dt):
            return stack.enter_context(nc.sbuf_tensor(name, shape, dt))

        def sem(name):
            return stack.enter_context(nc.semaphore(name))

        w_sb = sb("w_sb", [P, W_TOTAL], F32)
        c_sb = sb("c_sb", [P, C_TOTAL], F32)
        w1_sb = sb("w1_sb", [P, FC * P], F32)
        w1_hi = sb("w1_hi", [P, FC, P], F16)
        w1_lo = sb("w1_lo", [P, FC, P], F16)
        w1_s = sb("w1_s", [P, FC * P], F32)
        w2_sb = sb("w2_sb", [P, FC, P], F32)
        wg_s = sb("wg_s", [P, E_N], F32)
        wg_hi = sb("wg_hi", [P, E_N], F16)
        wg_lo = sb("wg_lo", [P, E_N], F16)
        wq_rep = sb("wq_rep", [P, H, ROWS], F32)
        wk_rep = sb("wk_rep", [P, H, ROWS], F32)
        kern_sb = sb("kern_sb", [P, P], BF16)
        kbias_sb = sb("kbias_sb", [P, P], BF16)
        kern_q = sb("kern_q", [P, P], BF16)
        gates = sb("gates", [P, 4], F32)
        s_inv = sb("s_inv", [P, 2], F32)
        s_prod = sb("s_prod", [P, 1], F32)
        ident16 = sb("ident16", [P, P], F16)
        identb = sb("identb", [P, P], BF16)
        sel = sb("sel", [P, E_N, P], F16)
        half_neg = sb("half_neg", [P, ST], F32)
        eps = sb("eps", [P, ST], F32)
        carrier = sb("carrier", [P, 1], F32)
        khat = sb("khat", [P, B, T], F32)
        ctx_all = sb("ctx_all", [P, B, T], F32)
        v1 = sb("v1", [P, B, 2, D], F32)
        kz = sb("kz", [P, B, T], F32)
        kz_n = sb("kz_n", [P, B, T], F32)
        kz_k = sb("kz_k", [P, B, T], F32)

        ident = c_sb[:, 0:P]

        def w(name):
            a, b = W_COLS[name]
            return w_sb[:, a:b]

        def cst(name):
            a, b = C_COLS[name]
            return c_sb[:, a:b]

        x_in = sb("x_in", [P, ST, D], F32)
        x_res = sb("x_res", [P, ST, D], F32)
        ctx_sb = sb("ctx_sb", [P, T], F32)
        mask_sb = sb("mask_sb", [P, ST, T], I32)
        ctx_rem = sb("ctx_rem", [P, HG, ROWS], F32)
        is_zero = sb("is_zero", [P, ST, T], F32)
        all_zero = sb("all_zero", [P, ST], F32)
        keep = sb("keep", [P, ST], F32)
        fill = sb("fill", [P, ST], F32)
        bias_st = sb("bias_st", [P, ST, T], BF16)
        bias_rem = sb("bias_rem", [P, ST, HG, ROWS], BF16)
        bias_t = sb("bias_t", [P, 2, S], BF16)
        k_hi = sb("k_hi", [P, NG, T], F16)
        kdiag = sb("kdiag", [P, NG, HG, T], F16)
        krem = sb("krem", [P, NG, HG, ROWS], F16)
        vaug = sb("vaug", [P, H, ROWS], F32)
        vrem = sb("vrem", [P, NG, HG, ROWS], F32)
        stats = sb("stats", [P, 4, ST, 6], F32)
        mv = sb("mv", [P, 4, ST, 2], F32)
        var_e = sb("var_e", [P, 4, ST], F32)
        rstd = sb("rstd", [P, 4, ST], F32)
        rstd_q = sb("rstd_q", [P, ST], F32)
        xn0 = sb("xn0", [P, ST, D], F32)
        xn0_t = sb("xn0_t", [P, S], F32)
        xn = sb("xn", [P, ST, D], F32)
        xn_t = sb("xn_t", [P, S], F32)
        q_hi = sb("q_hi", [P, 2, S], F16)
        qst = sb("qst", [P, NG, S], F16)
        neg_max = sb("neg_max", [P, NG, ST, P], F16)
        probs_t = sb("probs_t", [P, 2, HG + 1, S], F32)
        av_t = sb("av_t", [P, 2, S], F32)
        inv_sum = sb("inv_sum", [P, ST, HG], F32)
        att = sb("att", [P, ST, D], F32)
        att_t = sb("att_t", [P, S], F32)
        y_b = sb("y_b", [P, ST, D], F32)
        x1 = sb("x1", [P, ST, D], F32)
        xn_hi = sb("xn_hi", [P, S], F16)
        xn_lo = sb("xn_lo", [P, S], F16)
        logits = sb("logits", [P, ST, E_N], F32)
        top8 = sb("top8", [P, ST, 8], F32)
        top_i = sb("top_i", [P, ST, 8], U32)
        top_f = sb("top_f", [P, ST, 2], F32)
        gap = sb("gap", [P, ST], F32)
        e_gap = sb("e_gap", [P, ST], F32)
        gw = sb("gw", [P, 3, ST], F32)
        pick = sb("pick", [P, 3, ST, E_N], F32)
        comb = sb("comb", [P, ST, P], F16)
        comb_t = sb("comb_t", [P, S], F16)
        cbc = sb("cbc", [P, E_N, S], F32)
        h_sb = sb("h_sb", [P, 3, S], F32)
        hc_sb = sb("hc_sb", [P, 3, S], F32)
        ffn_t = sb("ffn_t", [P, S], F32)
        x2 = sb("x2", [P, ST, D], F32)
        q1_t = sb("q1_t", [P, S], F32)
        nmax1 = sb("nmax1", [P, ST], F32)
        sum1 = sb("sum1", [P, ST], F32)
        r1 = sb("r1", [P, ST], F32)
        r1g = sb("r1g", [P, ST], F32)
        p1 = sb("p1", [P, ST, T], F32)
        p1_t = sb("p1_t", [P, 2, S], F32)
        x3 = sb("x3", [P, ST, D], F32)
        xb = sb("xb", [P, ST, D], BF16)
        fv = sb("fv", [P, ST * D], F32)
        fe = sb("fe", [P, ST * D], I32)
        fc = sb("fc", [P, ST * D], F32)
        fw = sb("fw", [P, ST * D], F32)
        fq = sb("fq", [P, ST * D], F32)
        fo = sb("fo", [P, ST * D], F32)
        fn = sb("fn", [P, ST * D], F32)
        xq = sb("xq", [P, ST, D], BF16)
        xq_t = sb("xq_t", [P, S], BF16)
        y_s = sb("y_s", [P, ST, D], BF16)
        y_sb = sb("y_sb", [P, ST, D], BF16)
        x4 = sb("x4", [P, ST, D], F32)

        ps = stack.enter_context(nc.psum_tensor("ps", [P, 8, 512], F32))

        def bank(n):
            return ps[:, n, :]

        def bank16(n, dt):
            return ps[:, n, :].bitcast(dt)

        ROWB, SCB, AVB, TRB, BA, BB = (0, 1), (2, 3), 4, 5, 6, 7

        def halves(b):
            return ps[:, b:b + 2, :].rearrange("p a (b t) -> p (a b) t", b=2)[:, :, 0:T]

        k_ps, s1_ps = halves(ROWB[0]), halves(BA)

        consts_in, early_in, late_in, ctx_all_in, w1_in, w2_in, kern_in = map(
            sem, ["consts_in", "early_in", "late_in", "ctx_all_in", "w1_in", "w2_in", "kern_in"])
        zeros_set, ones_set, gates_set, kc_mm, kc_ready, z_mm, z_reduced, khat_ready = map(
            sem, ["zeros_set", "ones_set", "gates_set", "kc_mm", "kc_ready", "z_mm", "z_reduced", "khat_ready"])
        attn_w_set, ffn_w_set, dve_setup, v1_mm, v1_ready = map(
            sem, ["attn_w_set", "ffn_w_set", "dve_setup", "v1_mm", "v1_ready"])
        x_loaded, x_res_loaded, ctx_loaded, mask_loaded, stored = map(
            sem, ["x_loaded", "x_res_loaded", "ctx_loaded", "mask_loaded", "stored"])
        dve_step, pool_step = sem("dve_step"), sem("pool_step")
        DVE_FRONT, DVE_BACK = 10, 22
        POOL_FRONT, POOL_BACK = 1, 3

        PER = {
            "ctx_rem_ready": 1, "mask_zero": 1, "bias_ready": 1, "bias_tr": 1, "bias_t_ready": 1,
            "k_mm": 1, "k_hi_ready": 1, "k_ready": 1, "v_mm": 1, "v_ready": 1,
            "var0_ready": 1, "rstd0_ready": 1, "xn0_ready": 1, "xn0_tr": 1, "xn0_t_ready": 1,
            "q_mm": NG, "q_hi_ready": NG, "q_ready": NG,
            "max_mm": 2 * NG * ST, "max_done": 2 * NG * ST, "max_tr": NG, "q_shifted": NG,
            "score_mm": NG * (HG + 1), "probs_ready": NG * (HG + 1), "av_mm": NG, "av_ready": NG,
            "av_tr": NG, "att_ready": NG, "att_tr": 1, "att_t_ready": 1, "y0_mm": 1,
            "y0_read": 1, "x1_ready": 1,
            "var1_ready": 1, "rstd1_ready": 1, "xn1_ready": 1, "xn1_tr": 1, "xhi_ready": 1, "xlo_ready": 1,
            "gate_mm": 1, "gate_read": 1, "gap_ready": 1, "e_gap_ready": 1, "comb_ready": 1, "comb_tr": 1,
            "comb_t_ready": 1, "cbc_mm": E_N, "cbc_ready": E_N, "up_mm": FC, "h_ready": FC, "hc_ready": FC,
            "down_mm": FC, "ffn_t_ready": 1, "ffn_tr": 1, "x2_ready": 1,
            "var2_ready": 1, "rstd2_ready": 1, "xn2_ready": 1, "xn2_tr": 1, "xn2_t_ready": 1, "q1_mm": 1,
            "q1_ready": 1, "s1_mm": 1, "nmax1_ready": 1, "p1_ready": ST, "p1_tr": 1,
            "p1a_ready": 1, "p1b_ready": 1, "o1_mm": 1, "x3_ready": 1,
            "var3_ready": 1, "rstd3_ready": 1, "xn3_ready": 1, "xq_ready": 1,
            "xq_tr": 1, "xq_t_ready": 1, "y1_mm": 1, "y1_ready": 1, "x4_ready": 1,
        }
        SEM = {name: sem(name) for name in PER}

        def at(name, b, k=None):
            return b * PER[name] + (PER[name] if k is None else k)

        rows = [("row_scores", ST * g + s) for g in range(NG) for s in range(ST)]
        for g in reversed(range(NG)):
            rows.insert(ST * g + ST + (1 if g < NG - 1 else 0), ("max_rows", g))
        prep = [("context", 0), ("bias", 0), ("norm_a", 0), ("k_blocks", 0), ("norm_b", 0), ("v_blocks", 0),
                ("bias_t", 0), ("xn0_t", 0), ("queries", 0), ("queries", 1), ("queries", 2), ("queries", 3)]

        def score_steps(g):
            return [("scores", (HG + 1) * g + j) for j in range(HG + 1)]

        attn = (score_steps(0) + score_steps(1) + [("weighted_v", 0), ("av_copy", 0)]
                + score_steps(2) + [("values_back", 0), ("weighted_v", 1), ("av_copy", 1)]
                + score_steps(3) + [("values_back", 1), ("weighted_v", 2), ("av_copy", 2), ("values_back", 2),
                                    ("weighted_v", 3), ("av_copy", 3), ("values_back", 3), ("project", 0)])
        gate = [("norm_a", 1), ("norm_b", 1), ("xn1_t", 0), ("gate", 0), ("top2", 0), ("combine", 0),
                ("comb_t", 0)] + [("spread", e) for e in range(E_N)]
        ffn = [("up", 0)] + [("ffn", f) for f in range(FC)]
        tail = [("ffn_out", 0), ("norm_a", 2), ("norm_b", 2), ("xn2_t", 0), ("q1", 0), ("s1", 0), ("p1_t", 0),
                ("o1", 0), ("norm_a", 3), ("norm_b", 3), ("quantize", 0), ("xq_t", 0), ("y1", 0)]
        FRONT = prep + rows + attn
        BACK = gate + ffn + tail

        def merged(a, b):
            out, n = [], 0
            for k, step in enumerate(a):
                out.append(step)
                while n < len(b) and (n + 1) * len(a) <= (k + 1) * len(b):
                    out.append(b[n])
                    n += 1
            return out + b[n:]

        BOTH = merged(gate, prep) + merged(ffn, rows) + merged(attn, tail)
        front_names = {name for name, _ in FRONT if name not in ("norm_a", "norm_b")}

        def in_front(name, k):
            return name in front_names or (name in ("norm_a", "norm_b") and k == 0)

        def run(steps, order, front, back):
            for name, k in order:
                if name in steps:
                    steps[name](front if in_front(name, k) else back, k)

        def alone(eng):
            eng.wait_ge(consts_in, 16)

        block = stack.enter_context(nc.Block())

        @block.sync
        def _(sp):
            sp.dma_start(x_in[:, :, :], x_v[0, :, :, :]).then_inc(x_loaded, 16)
            sp.dma_start(w_sb[:, 0:W_EARLY], wts[:, 0:W_EARLY]).then_inc(early_in, 16)
            sp.dma_start(ctx_sb[:, :], ctx_t[0, :, :]).then_inc(ctx_loaded, 16)
            sp.dma_start(c_sb[:, :], consts[:, :]).then_inc(consts_in, 16)
            sp.dma_start(mask_sb[:, :, :], mask_v[0, :, :, :]).then_inc(mask_loaded, 16)
            sp.dma_start(w_sb[:, W_EARLY:W_TOTAL], wts[:, W_EARLY:W_TOTAL]).then_inc(late_in, 16)
            sp.dma_start(ctx_all[:, :, :], ctx_t.rearrange("b d t -> d b t")).then_inc(ctx_all_in, 16)
            sp.dma_start(w1_sb[:, :], w1[:, :]).then_inc(w1_in, 16)
            sp.dma_start(kern_sb[:, :], kern[:, :]).then_inc(kern_in, 16)
            sp.dma_start(kbias_sb[:, :], kbias[:, :]).then_inc(kern_in, 16)
            sp.dma_start(x_res[:, :, :], x_v[0, :, :, :]).then_inc(x_res_loaded, 16)
            sp.dma_start(w2_sb[:, :, :], w2.rearrange("p (c d) -> p c d", d=D)).then_inc(w2_in, 16)
            sp.sem_inc(stored, 1)

            def one(b):
                return b if isinstance(b, int) else bass.ds(b, 1)

            def tokens(v, b):
                return v[b, :, :, :] if isinstance(b, int) else v[bass.ds(b, 1), :, :, :].rearrange(
                    "a p s d -> (a p) s d")

            def load_next(b):
                sp.wait_ge(SEM["v_mm"], at("v_mm", b - 1))
                sp.dma_start(ctx_sb[:, :], ctx_t[b, :, :] if isinstance(b, int) else
                             ctx_t[bass.ds(b, 1), :, :].rearrange("a d t -> (a d) t")).then_inc(ctx_loaded, 16)
                sp.wait_ge(SEM["mask_zero"], at("mask_zero", b - 1))
                sp.dma_start(mask_sb[:, :, :], tokens(mask_v, b)).then_inc(mask_loaded, 16)
                sp.wait_ge(SEM["xn0_ready"], at("xn0_ready", b - 1))
                sp.dma_start(x_in[:, :, :], tokens(x_v, b)).then_inc(x_loaded, 16)

            def load_residual(b):
                sp.wait_ge(SEM["x1_ready"], at("x1_ready", b - 1))
                sp.dma_start(x_res[:, :, :], tokens(x_v, b)).then_inc(x_res_loaded, 16)

            def store(b):
                sp.wait_ge(SEM["x4_ready"], at("x4_ready", b))
                sp.dma_start(tokens(out_v, b), x4[:, :, :]).then_inc(stored, 16)

            load_next(1)
            load_residual(1)
            with sp.Fori(0, B - 2) as i:
                load_next(i + 2)
                store(i)
                load_residual(i + 2)
            store(B - 2)
            store(B - 1)
            sp.wait_ge(stored, 16 * B + 1)

        @block.gpsimd
        def _(pool):
            for t in (wq_rep, wk_rep, ctx_rem, kdiag, krem, neg_max, vaug, vrem, comb):
                nc.gpsimd.memset(t[:], 0.0).then_inc(zeros_set, 1)
            nc.gpsimd.memset(bias_rem[:], MASKED).then_inc(zeros_set, 1)
            nc.gpsimd.memset(half_neg[:], -0.5).then_inc(zeros_set, 1)
            nc.gpsimd.memset(eps[:], EPS).then_inc(zeros_set, 1)
            pool.wait_ge(zeros_set, 12)
            nc.gpsimd.memset(vaug[:, :, DK:DK + 1], 1.0).then_inc(ones_set, 1)
            for j in range(HG):
                pool.wait_ge(ones_set, j + 1)
                nc.gpsimd.memset(vrem[ROWS * j:ROWS * j + ROWS, :, j, DK:DK + 1], 1.0).then_inc(ones_set, 1)

            chain = [0, 0]

            def norm_a(b, n):
                pool.wait_ge(SEM[f"var{n}_ready"], at(f"var{n}_ready", b))
                chain[1] += 1
                nc.gpsimd.tensor_tensor(var_e[:, n, :], mv[:, n, :, 1], eps[:, :], ALU.add).then_inc(pool_step, 1)
                pool.wait_ge(pool_step, chain[0] + chain[1])
                nc.gpsimd.tensor_tensor(rstd[:, n, :], var_e[:, n, :], half_neg[:, :], ALU.pow
                                        ).then_inc(SEM[f"rstd{n}_ready"], 1)

            steps = {"norm_a": norm_a}
            run(steps, FRONT, 0, None)
            assert chain[1] == POOL_FRONT
            with pool.Fori(0, B - 1) as i:
                chain[:] = [POOL_FRONT + i * (POOL_FRONT + POOL_BACK), 0]
                run(steps, BOTH, i + 1, i)
            chain[:] = [POOL_FRONT + (B - 1) * (POOL_FRONT + POOL_BACK), 0]
            run(steps, BACK, None, B - 1)
            assert chain[1] == POOL_BACK

        @block.scalar
        def _(act):
            def context_features():
                act.wait_ge(late_in, 16)
                act.wait_ge(kc_mm, 1)
                nc.scalar.activation(kz[:, :, :].rearrange("p (h b) t -> p h (b t)", h=2),
                                     ps[:, BA:BB + 1, 0:2 * T], ACT.Identity, bias=w("bk1")).then_inc(kc_ready, 1)

            def cosines():
                act.wait_ge(z_reduced, 1)
                nc.scalar.activation(khat[:, :, :], kz_n[:, :, :], ACT.Sin).then_inc(khat_ready, 1)

            def context(b, _):
                act.wait_ge(SEM["k_mm"], at("k_mm", b))
                nc.scalar.activation(k_hi[:, :, :], k_ps, ACT.Identity, bias=cst("one")
                                     ).then_inc(SEM["k_hi_ready"], 1)

            def copy_bias(b, _):
                act.wait_ge(SEM["bias_tr"], at("bias_tr", b))
                nc.scalar.activation(bias_t[:, :, :].rearrange("p a s -> p (a s)"), bank16(TRB, BF16), ACT.Copy
                                     ).then_inc(SEM["bias_t_ready"], 1)

            def copy_xn0(b, _):
                act.wait_ge(SEM["xn0_tr"], at("xn0_tr", b))
                nc.scalar.activation(xn0_t[:, :], bank(TRB), ACT.Copy).then_inc(SEM["xn0_t_ready"], 1)

            def queries(b, g):
                act.wait_ge(SEM["q_mm"], at("q_mm", b, g + 1))
                if g >= 2:
                    act.wait_ge(SEM["q_ready"], at("q_ready", b, g - 1))
                nc.scalar.activation(q_hi[:, g % 2, :], bank(SCB[g % 2]), ACT.Copy
                                     ).then_inc(SEM["q_hi_ready"], 1)

            def scores(b, n):
                g, j = divmod(n, HG + 1)
                act.wait_ge(SEM["score_mm"], at("score_mm", b, n + 1))
                if g >= 2 and j == 0:
                    act.wait_ge(SEM["av_mm"], at("av_mm", b, g - 1))
                nc.scalar.activation(probs_t[:, g % 2, j, :], bank(SCB[n % 2]), ACT.Exp
                                     ).then_inc(SEM["probs_ready"], 1)

            def av_copy(b, g):
                act.wait_ge(SEM["av_mm"], at("av_mm", b, g + 1))
                if g >= 2:
                    act.wait_ge(SEM["av_tr"], at("av_tr", b, g - 1))
                nc.scalar.activation(av_t[:, g % 2, :], bank(AVB), ACT.Copy).then_inc(SEM["av_ready"], 1)

            def project(b, _):
                act.wait_ge(SEM["att_tr"], at("att_tr", b))
                nc.scalar.activation(att_t[:, :], bank(TRB), ACT.Copy).then_inc(SEM["att_t_ready"], 1)

            def copy_xn1(b, _):
                act.wait_ge(SEM["xn1_tr"], at("xn1_tr", b))
                nc.scalar.activation(xn_hi[:, :], bank(BA), ACT.Copy).then_inc(SEM["xhi_ready"], 1)

            def top2(b, _):
                act.wait_ge(SEM["gap_ready"], at("gap_ready", b))
                nc.scalar.activation(e_gap[:, :], gap[:, :], ACT.Exp, scale=1.0 / WS
                                     ).then_inc(SEM["e_gap_ready"], 1)

            def comb_turn(b, _):
                act.wait_ge(SEM["comb_tr"], at("comb_tr", b))
                nc.scalar.activation(comb_t[:, :], bank16(BA, F16)[:, 0:S], ACT.Copy
                                     ).then_inc(SEM["comb_t_ready"], 1)

            def spread(b, e):
                act.wait_ge(SEM["cbc_mm"], at("cbc_mm", b, e + 1))
                nc.scalar.activation(cbc[:, e, :], bank((BB, BA)[e % 2]), ACT.Copy).then_inc(SEM["cbc_ready"], 1)

            def silu(b, f):
                act.wait_ge(SEM["up_mm"], at("up_mm", b, f + 1))
                if f >= 3:
                    act.wait_ge(SEM["hc_ready"], at("hc_ready", b, f - 2))
                nc.scalar.activation(h_sb[:, f % 3, :], bank(BA), ACT.Silu, scale=1.0 / WS
                                     ).then_inc(SEM["h_ready"], 1)

            def ffn_step(b, f):
                if f + 1 < FC:
                    silu(b, f + 1)

            def ffn_out(b, _):
                act.wait_ge(SEM["down_mm"], at("down_mm", b))
                nc.scalar.activation(ffn_t[:, :], bank(BB), ACT.Copy).then_inc(SEM["ffn_t_ready"], 1)

            def copy_xn2(b, _):
                act.wait_ge(SEM["xn2_tr"], at("xn2_tr", b))
                nc.scalar.activation(xn_t[:, :], bank(BB), ACT.Copy).then_inc(SEM["xn2_t_ready"], 1)

            def q1(b, _):
                act.wait_ge(SEM["q1_mm"], at("q1_mm", b))
                nc.scalar.activation(q1_t[:, :], bank(BA), ACT.Identity, bias=w("bq1")
                                     ).then_inc(SEM["q1_ready"], 1)

            def s1(b, _):
                act.wait_ge(SEM["nmax1_ready"], at("nmax1_ready", b))
                for s in range(ST):
                    nc.scalar.activation(p1[:, s, :], s1_ps[:, s, :], ACT.Exp, bias=nmax1[:, s:s + 1],
                                         accum_out=sum1[:, s:s + 1]).then_inc(SEM["p1_ready"], 1)

            def copy_p1(b, _):
                act.wait_ge(SEM["p1_tr"], at("p1_tr", b))
                nc.scalar.activation(p1_t[0:TH, 0, :], ps[0:TH, BA, :], ACT.Copy).then_inc(SEM["p1a_ready"], 1)

            def copy_xq(b, _):
                act.wait_ge(SEM["xq_tr"], at("xq_tr", b))
                nc.scalar.activation(xq_t[:, :], bank16(BB, BF16)[:, 0:S], ACT.Copy
                                     ).then_inc(SEM["xq_t_ready"], 1)

            def y1(b, _):
                act.wait_ge(SEM["y1_mm"], at("y1_mm", b))
                nc.scalar.activation(y_s[:, :, :].rearrange("p s d -> p (s d)"), bank(BA), ACT.Copy,
                                     scale=s_prod[:, 0:1]).then_inc(SEM["y1_ready"], 1)

            steps = {
                "context": context, "bias_t": copy_bias, "xn0_t": copy_xn0, "queries": queries, "scores": scores,
                "av_copy": av_copy, "project": project, "xn1_t": copy_xn1, "top2": top2, "comb_t": comb_turn,
                "spread": spread, "up": silu, "ffn": ffn_step, "ffn_out": ffn_out, "xn2_t": copy_xn2, "q1": q1,
                "s1": s1, "p1_t": copy_p1, "xq_t": copy_xq, "y1": y1,
            }
            act.wait_ge(early_in, 16)
            nc.scalar.activation(gates[:, :], w("g"), ACT.Tanh).then_inc(gates_set, 1)
            act.wait_ge(consts_in, 16)
            run(steps, prep, 0, None)
            context_features()
            cosines()
            run(steps, rows + attn, 0, None)
            with act.Fori(0, B - 1) as i:
                run(steps, BOTH, i + 1, i)
            run(steps, BACK, None, B - 1)

        @block.vector
        def _(dve):
            setup = [0]

            def set_up(ins):
                setup[0] += 1
                ins.then_inc(dve_setup, 1)
                dve.wait_ge(dve_setup, setup[0])

            def round_e4m3(step, v, n, dst):
                step(nc.vector.tensor_scalar(fe[:, 0:n], v.bitcast(I32), 0x7F800000, None, ALU.bitwise_and))
                step(nc.vector.tensor_scalar(fc[:, 0:n], fe[:, 0:n].bitcast(F32), 2.0 ** -6, 1.5 * 2.0 ** 20,
                                             ALU.max, ALU.mult))
                step(nc.vector.tensor_tensor(fw[:, 0:n], v, fc[:, 0:n], ALU.add))
                step(nc.vector.tensor_tensor(fq[:, 0:n], fw[:, 0:n], fc[:, 0:n], ALU.subtract))
                step(nc.vector.tensor_tensor(fo[:, 0:n], fq[:, 0:n], fq[:, 0:n], ALU.mult))
                step(nc.vector.tensor_scalar(fn[:, 0:n], fo[:, 0:n], 448.0 ** 2, 3.0e38, ALU.is_gt, ALU.mult))
                step(nc.vector.tensor_scalar(fo[:, 0:n], fn[:, 0:n], 3.0e38, 0.0, ALU.mult, ALU.mult))
                return nc.vector.tensor_tensor(dst, fo[:, 0:n], fq[:, 0:n], ALU.add)

            scale = float(DK) ** -0.25
            dve.wait_ge(early_in, 16)
            dve.wait_ge(zeros_set, 12)
            for dst, src in ((wk_rep, "wk0"), (wq_rep, "wq0")):
                for r in range(3):
                    nc.vector.tensor_scalar(dst[:, :, DK * r:DK * r + DK],
                                            w(src).rearrange("p (h k) -> p h k", k=DK), scale, None, ALU.mult)
            dve.wait_ge(consts_in, 16)
            nc.vector.tensor_copy(ident16[:, :], ident)
            nc.vector.tensor_copy(identb[:, :], ident).then_inc(attn_w_set, 1)
            nc.vector.tensor_tensor(sel[:, :, :],
                                    ident[:, 0:E_N].unsqueeze(2).broadcast_to([P, E_N, P]),
                                    ident[:, E_N:2 * E_N].unsqueeze(2).broadcast_to([P, E_N, P]), ALU.add)
            dve.wait_ge(ones_set, HG + 1)

            def cosine_arguments():
                dve.wait_ge(late_in, 16)
                dve.wait_ge(z_mm, 1)
                zf = kz[:, :, :].rearrange("p b t -> p (b t)")
                rf = kz_n[:, :, :].rearrange("p b t -> p (b t)")
                nf = kz_k[:, :, :].rearrange("p b t -> p (b t)")
                set_up(nc.vector.tensor_scalar(kz[:, :, :].rearrange("p (h b) t -> p h (b t)", h=2),
                                               ps[:, BA:BB + 1, 0:2 * T], w("br1"), None, ALU.add))
                set_up(nc.vector.tensor_scalar(zf, zf, TWO_PI / 4, None, ALU.add))
                set_up(nc.vector.tensor_scalar(nf, zf, 1.0 / TWO_PI, ROUND, ALU.mult, ALU.add))
                set_up(nc.vector.tensor_scalar(nf, nf, ROUND, None, ALU.subtract))
                set_up(nc.vector.scalar_tensor_tensor(out=rf, in0=nf, scalar=-TWO_PI_HI, in1=zf,
                                                      op0=ALU.mult, op1=ALU.add))
                set_up(nc.vector.scalar_tensor_tensor(out=zf, in0=nf, scalar=-TWO_PI_LO, in1=rf,
                                                      op0=ALU.mult, op1=ALU.add))
                nc.vector.tensor_scalar(rf, zf, PI, -PI, ALU.min, ALU.max).then_inc(z_reduced, 1)

            def second_values():
                dve.wait_ge(v1_mm, 1)
                nc.vector.tensor_tensor(
                    v1[0:TH, :, :, :].rearrange("p b c d -> p (b c) d"),
                    ps[0:TH, BA:BB + 1, :].rearrange("p a (c d) -> p (a c) d", d=D),
                    w("bv1")[0:TH, :].unsqueeze(1).broadcast_to([TH, 2 * B, D]), ALU.add).then_inc(v1_ready, 1)

            def ffn_weights():
                set_up(nc.vector.tensor_scalar(wg_s[:, :], w("wg"), WS, None, ALU.mult))
                set_up(nc.vector.tensor_copy(wg_hi[:, :], wg_s[:, :]))
                nc.vector.tensor_tensor(wg_lo[:, :], wg_s[:, :], wg_hi[:, :], ALU.subtract)
                dve.wait_ge(w1_in, 16)
                w1_hf = w1_hi[:, :, :].rearrange("p c f -> p (c f)")
                w1_lf = w1_lo[:, :, :].rearrange("p c f -> p (c f)")
                set_up(nc.vector.tensor_scalar(w1_s[:, :], w1_sb[:, :], WS, None, ALU.mult))
                set_up(nc.vector.tensor_copy(w1_hf, w1_s[:, :]))
                nc.vector.tensor_tensor(w1_lf, w1_s[:, :], w1_hf, ALU.subtract).then_inc(ffn_w_set, 1)
                set_up(nc.vector.reciprocal(s_inv[:, :], w("s")))
                nc.vector.tensor_tensor(s_prod[:, :], w("s")[:, 0:1], w("s")[:, 1:2], ALU.mult)
                dve.wait_ge(kern_in, 32)
                set_up(nc.vector.tensor_scalar(fv[:, 0:P], kern_sb[:, :], s_inv[:, 1:2], None, ALU.mult))
                set_up(round_e4m3(set_up, fv[:, 0:P], P, kern_q[:, :]))
                dve.wait_ge(gates_set, 1)

            chain = [0, 0]

            def settled(ins):
                chain[1] += 1
                ins.then_inc(dve_step, 1)
                dve.wait_ge(dve_step, chain[0] + chain[1])

            def norm_source(n):
                return (x_in, x1, x2, x3)[n]

            def norm_a(b, n):
                if n == 0:
                    dve.wait_ge(x_loaded, b * 16 + 16)
                else:
                    name = f"x{n}_ready"
                    dve.wait_ge(SEM[name], at(name, b))
                for s in range(ST):
                    last = nc.vector.bn_stats(stats[:, n, s, :], norm_source(n)[:, s, :])
                settled(last)
                nc.vector.memset(carrier[:, :], 0.0)
                for s in range(ST):
                    last = nc.vector.bn_aggr(mv[:, n, s, :], stats[:, n, s, :])
                last.then_inc(SEM[f"var{n}_ready"], 1)

            def norm_b(b, n):
                dve.wait_ge(SEM[f"rstd{n}_ready"], at(f"rstd{n}_ready", b))
                by = rstd[:, n, :]
                if n == 0:
                    settled(nc.vector.tensor_tensor(rstd_q[:, :], rstd[:, 0, :], keep[:, :], ALU.mult))
                    by = rstd_q
                dst = (xn0, xn, xn, xb)[n]
                for s in range(ST):
                    last = nc.vector.tensor_scalar(dst[:, s, :], norm_source(n)[:, s, :], mv[:, n, s, 0:1],
                                                   by[:, s:s + 1], ALU.subtract, ALU.mult)
                last.then_inc(SEM[f"xn{n}_ready"], 1)

            def context(b, _):
                dve.wait_ge(ctx_loaded, b * 16 + 16)
                nc.vector.tensor_copy(ctx_rem[:, :, 0:TR],
                                      ctx_sb[:, T0:T].unsqueeze(1).broadcast_to([P, HG, TR])
                                      ).then_inc(SEM["ctx_rem_ready"], 1)

            def mask_bias(b, _):
                dve.wait_ge(mask_loaded, b * 16 + 16)
                nc.vector.tensor_scalar(is_zero[:, :, :], mask_sb[:, :, :], 0.0, None, ALU.is_equal
                                        ).then_inc(SEM["mask_zero"], 1)
                dve.wait_ge(SEM["mask_zero"], at("mask_zero", b))
                settled(nc.vector.tensor_reduce(all_zero[:, :], is_zero[:, :, :], X, ALU.min))
                settled(nc.vector.tensor_scalar(keep[:, :], all_zero[:, :], -1.0, 1.0, ALU.mult, ALU.add))
                settled(nc.vector.tensor_scalar(fill[:, :], keep[:, :], MASKED, None, ALU.mult))
                nc.vector.tensor_tensor(bias_st[:, :, :], is_zero[:, :, :],
                                        fill[:, :].unsqueeze(2).broadcast_to([P, ST, T]), ALU.mult)
                for j in range(HG):
                    last = nc.vector.tensor_tensor(bias_rem[:, :, j, 0:TR], is_zero[:, :, T0:T],
                                                   fill[:, :].unsqueeze(2).broadcast_to([P, ST, TR]), ALU.mult)
                last.then_inc(SEM["bias_ready"], 1)

            def k_blocks(b, _):
                dve.wait_ge(SEM["k_hi_ready"], at("k_hi_ready", b))
                for j in range(HG):
                    r = slice(ROWS * j, ROWS * j + ROWS)
                    last = nc.vector.scalar_tensor_tensor(out=kdiag[r, :, j, :], in0=k_hi[r, :, :],
                                                          scalar=cst("lo_k")[r, :], in1=k_ps[r, :, :],
                                                          op0=ALU.mult, op1=ALU.add)
                settled(last)
                for j in range(HG):
                    r = slice(ROWS * j, ROWS * j + ROWS)
                    last = nc.vector.tensor_copy(krem[r, :, j, 0:TR], kdiag[r, :, j, T0:T])
                last.then_inc(SEM["k_ready"], 1)

            def v_blocks(b, _):
                dve.wait_ge(SEM["v_mm"], at("v_mm", b))
                vb = bank(SCB[0])
                nc.vector.tensor_copy(vaug[:, :, 0:DK], vb[:, 0:P].rearrange("p (h k) -> p h k", k=DK))
                for j in range(HG):
                    r = slice(ROWS * j, ROWS * j + ROWS)
                    last = nc.vector.tensor_copy(
                        vrem[r, :, j, 0:DK],
                        vb[r, P:2 * P].rearrange("p (g j k) -> p g j k", j=HG, k=DK)[:, :, j, :])
                last.then_inc(SEM["v_ready"], 1)

            def queries(b, g):
                dve.wait_ge(SEM["q_hi_ready"], at("q_hi_ready", b, g + 1))
                nc.vector.scalar_tensor_tensor(out=qst[:, g, :], in0=q_hi[:, g % 2, :], scalar=cst("lo_q"),
                                               in1=bank(SCB[g % 2]), op0=ALU.mult, op1=ALU.add
                                               ).then_inc(SEM["q_ready"], 1)

            def row_max(b, n):
                g, s = divmod(n, ST)
                for h in range(2):
                    dve.wait_ge(SEM["max_mm"], at("max_mm", b, 2 * n + h + 1))
                    nc.vector.tensor_reduce(
                        neg_max[:, g, s, :].rearrange("p (j r) -> p j r", r=ROWS)[:, 2 * h:2 * h + 2, MROW],
                        bank(ROWB[h])[:, 0:2 * T].rearrange("p (h t) -> p h t", t=T),
                        X, ALU.max, negate=True).then_inc(SEM["max_done"], 1)

            def shift(b, g):
                dve.wait_ge(SEM["max_tr"], at("max_tr", b, g + 1))
                nc.vector.tensor_tensor(qst[:, g, :], qst[:, g, :], bank16(TRB, F16)[:, 0:S], ALU.add
                                        ).then_inc(SEM["q_shifted"], 1)

            def normalize(b, g):
                dve.wait_ge(SEM["av_tr"], at("av_tr", b, g + 1))
                o = bank(TRB).rearrange("p (s j r) -> p s j r", s=ST, r=ROWS)
                settled(nc.vector.reciprocal(inv_sum[:, :, :], o[:, :, :, DK]))
                nc.vector.tensor_tensor(
                    att[:, :, ROWS * g:ROWS * g + ROWS].rearrange("p s (j k) -> p s j k", k=DK),
                    o[:, :, :, 0:DK], inv_sum[:, :, :].unsqueeze(3).broadcast_to([P, ST, HG, DK]), ALU.mult
                ).then_inc(SEM["att_ready"], 1)

            def project(b, _):
                dve.wait_ge(SEM["y0_mm"], at("y0_mm", b))
                nc.vector.tensor_tensor(y_b[:, :, :], bank(AVB).rearrange("p (s d) -> p s d", d=D),
                                        w("bu0").unsqueeze(1).broadcast_to([P, ST, D]), ALU.add
                                        ).then_inc(SEM["y0_read"], 1)
                dve.wait_ge(x_res_loaded, b * 16 + 16)
                dve.wait_ge(SEM["y0_read"], at("y0_read", b))
                nc.vector.scalar_tensor_tensor(out=x1[:, :, :], in0=y_b[:, :, :], scalar=gates[:, 0:1],
                                               in1=x_res[:, :, :], op0=ALU.mult, op1=ALU.add
                                               ).then_inc(SEM["x1_ready"], 1)

            def low_part(b, _):
                dve.wait_ge(SEM["xhi_ready"], at("xhi_ready", b))
                nc.vector.tensor_tensor(xn_lo[:, :], bank(BA), xn_hi[:, :], ALU.subtract
                                        ).then_inc(SEM["xlo_ready"], 1)

            def top2(b, _):
                dve.wait_ge(SEM["gate_mm"], at("gate_mm", b))
                nc.vector.tensor_copy(logits[:, :, :], bank(BB)[:, 0:ST * E_N].rearrange("p (s e) -> p s e", e=E_N)
                                      ).then_inc(SEM["gate_read"], 1)
                alone(dve)
                dve.wait_ge(SEM["gate_read"], at("gate_read", b))
                for s in range(ST):
                    last = nc.vector.max(top8[:, s, :], logits[:, s, :])
                settled(last)
                nc.vector.tensor_tensor(gap[:, :], top8[:, :, 1], top8[:, :, 0], ALU.subtract
                                        ).then_inc(SEM["gap_ready"], 1)
                for s in range(ST):
                    last = nc.vector.max_index(top_i[:, s, :], top8[:, s, :], logits[:, s, :])
                settled(last)
                settled(nc.vector.tensor_copy(top_f[:, :, :], top_i[:, :, 0:2]))

            def combine(b, _):
                dve.wait_ge(SEM["e_gap_ready"], at("e_gap_ready", b))
                settled(nc.vector.tensor_scalar(gw[:, 0, :], e_gap[:, :], 1.0, None, ALU.add))
                settled(nc.vector.reciprocal(gw[:, 1, :], gw[:, 0, :]))
                nc.vector.tensor_tensor(gw[:, 2, :], e_gap[:, :], gw[:, 1, :], ALU.mult)
                for k in range(2):
                    last = nc.vector.tensor_tensor(pick[:, k, :, :],
                                                   cst("iota").unsqueeze(1).broadcast_to([P, ST, E_N]),
                                                   top_f[:, :, k].unsqueeze(2).broadcast_to([P, ST, E_N]),
                                                   ALU.is_equal)
                settled(last)
                for k in range(2):
                    last = nc.vector.tensor_tensor(pick[:, k, :, :], pick[:, k, :, :],
                                                   gw[:, k + 1, :].unsqueeze(2).broadcast_to([P, ST, E_N]),
                                                   ALU.mult)
                settled(last)
                settled(nc.vector.tensor_tensor(pick[:, 2, :, :], pick[:, 0, :, :], pick[:, 1, :, :], ALU.add))
                settled(nc.vector.tensor_copy(comb[:, :, 0:E_N], pick[:, 2, :, :]))
                nc.vector.tensor_tensor(comb[:, :, E_N:2 * E_N], pick[:, 2, :, :], comb[:, :, 0:E_N],
                                        ALU.subtract).then_inc(SEM["comb_ready"], 1)

            def weigh(b, f):
                e = f * P // F_N
                dve.wait_ge(SEM["h_ready"], at("h_ready", b, f + 1))
                if f == 0:
                    dve.wait_ge(SEM["cbc_ready"], at("cbc_ready", b))
                if f >= 3:
                    dve.wait_ge(SEM["down_mm"], at("down_mm", b, f - 2))
                nc.vector.tensor_tensor(hc_sb[:, f % 3, :], h_sb[:, f % 3, :], cbc[:, e, :], ALU.mult
                                        ).then_inc(SEM["hc_ready"], 1)

            def ffn_step(b, f):
                if f + 1 < FC:
                    weigh(b, f + 1)

            def ffn_out(b, _):
                dve.wait_ge(SEM["ffn_tr"], at("ffn_tr", b))
                nc.vector.scalar_tensor_tensor(out=x2[:, :, :].rearrange("p s d -> p (s d)"), in0=bank(BA),
                                               scalar=gates[:, 1:2],
                                               in1=x1[:, :, :].rearrange("p s d -> p (s d)"),
                                               op0=ALU.mult, op1=ALU.add).then_inc(SEM["x2_ready"], 1)

            def s1(b, _):
                dve.wait_ge(SEM["s1_mm"], at("s1_mm", b))
                nc.vector.tensor_reduce(nmax1[:, :], s1_ps, X, ALU.max, negate=True
                                        ).then_inc(SEM["nmax1_ready"], 1)

            def copy_p1(b, _):
                dve.wait_ge(SEM["p1_ready"], at("p1_ready", b))
                settled(nc.vector.reciprocal(r1[:, :], sum1[:, :]))
                nc.vector.tensor_scalar(r1g[:, :], r1[:, :], gates[:, 2:3], None, ALU.mult)
                dve.wait_ge(SEM["p1_tr"], at("p1_tr", b))
                nc.vector.tensor_copy(p1_t[0:TH, 1, :], ps[0:TH, BB, :]).then_inc(SEM["p1b_ready"], 1)

            def o1(b, _):
                dve.wait_ge(SEM["p1b_ready"], at("p1b_ready", b))
                dve.wait_ge(SEM["o1_mm"], at("o1_mm", b))
                for s in range(ST):
                    last = nc.vector.scalar_tensor_tensor(out=x3[:, s, :], in0=bank(BA)[:, D * s:D * s + D],
                                                          scalar=r1g[:, s:s + 1], in1=x2[:, s, :],
                                                          op0=ALU.mult, op1=ALU.add)
                last.then_inc(SEM["x3_ready"], 1)

            def quantize(b, _):
                dve.wait_ge(SEM["xn3_ready"], at("xn3_ready", b))
                settled(nc.vector.tensor_scalar(fv[:, :], xb[:, :, :].rearrange("p s d -> p (s d)"),
                                                s_inv[:, 0:1], None, ALU.mult))
                round_e4m3(settled, fv[:, :], ST * D, xq[:, :, :].rearrange("p s d -> p (s d)")
                           ).then_inc(SEM["xq_ready"], 1)

            def y1(b, _):
                dve.wait_ge(SEM["y1_ready"], at("y1_ready", b))
                settled(nc.vector.tensor_tensor(y_sb[:, :, :], y_s[:, :, :],
                                                kbias_sb[:, :].unsqueeze(1).broadcast_to([P, ST, D]), ALU.add))
                dve.wait_ge(stored, b * 16 + 1)
                nc.vector.scalar_tensor_tensor(out=x4[:, :, :], in0=y_sb[:, :, :], scalar=gates[:, 3:4],
                                               in1=x3[:, :, :], op0=ALU.mult, op1=ALU.add
                                               ).then_inc(SEM["x4_ready"], 1)

            steps = {
                "context": context, "bias": mask_bias, "norm_a": norm_a, "norm_b": norm_b, "k_blocks": k_blocks,
                "v_blocks": v_blocks, "queries": queries, "row_scores": row_max, "max_rows": shift,
                "values_back": normalize, "project": project, "xn1_t": low_part, "top2": top2,
                "combine": combine, "up": weigh, "ffn": ffn_step, "ffn_out": ffn_out, "s1": s1, "p1_t": copy_p1,
                "o1": o1, "quantize": quantize, "y1": y1,
            }
            run(steps, prep, 0, None)
            cosine_arguments()
            run(steps, rows, 0, None)
            second_values()
            ffn_weights()
            run(steps, attn, 0, None)
            assert chain[1] == DVE_FRONT, chain[1]
            with dve.Fori(0, B - 1) as i:
                chain[:] = [DVE_FRONT + i * (DVE_FRONT + DVE_BACK), 0]
                run(steps, BOTH, i + 1, i)
            chain[:] = [DVE_FRONT + (B - 1) * (DVE_FRONT + DVE_BACK), 0]
            run(steps, BACK, None, B - 1)
            assert chain[1] == DVE_BACK, chain[1]

        @block.tensor
        def _(pe):
            def transposes(dst, src, idn):
                for s in range(ST):
                    last = nc.tensor.transpose(dst[:, P * s:P * s + P], src[:, s, :], idn)
                return last

            def context_features():
                pe.wait_ge(late_in, 16)
                pe.wait_ge(ctx_all_in, 16)
                for h in range(2):
                    last = nc.tensor.matmul(ps[:, BA + h, 0:2 * T], w("wk1"),
                                            ctx_all[:, 2 * h:2 * h + 2, :].rearrange("p b t -> p (b t)"),
                                            start=True, stop=True)
                last.then_inc(kc_mm, 1)

            def context_projections():
                pe.wait_ge(kc_ready, 1)
                for h in range(2):
                    last = nc.tensor.matmul(ps[:, BA + h, 0:2 * T], w("wr1"),
                                            kz[:, 2 * h:2 * h + 2, :].rearrange("p b t -> p (b t)"),
                                            start=True, stop=True)
                last.then_inc(z_mm, 1)

            def second_values():
                pe.wait_ge(z_reduced, 1)
                for b in range(B):
                    for c in range(2):
                        o = ps[0:TH, BA + b // 2, D * (2 * (b % 2) + c):D * (2 * (b % 2) + c + 1)]
                        last = nc.tensor.matmul(o, ctx_all[:, b, TH * c:TH * c + TH], w("wv1"),
                                                start=True, stop=True)
                last.then_inc(v1_mm, 1)

            def context(b, _):
                pe.wait_ge(ctx_loaded, b * 16 + 16)
                for g in range(NG):
                    last = nc.tensor.matmul(k_ps[:, g, :], wk_rep[:, HG * g:HG * g + HG, :].rearrange(
                        "p h r -> p (h r)"), ctx_sb[:, :], start=True, stop=True)
                last.then_inc(SEM["k_mm"], 1)
                pe.wait_ge(SEM["ctx_rem_ready"], at("ctx_rem_ready", b))
                vb = bank(SCB[0])
                nc.tensor.matmul(vb[:, 0:P], ctx_sb[:, 0:T0], w("wv0"), start=True, stop=True)
                nc.tensor.matmul(vb[:, P:2 * P], ctx_rem[:, :, :].rearrange("p j r -> p (j r)"), w("wv0"),
                                 start=True, stop=True).then_inc(SEM["v_mm"], 1)

            def turn_bias(b, _):
                pe.wait_ge(SEM["bias_ready"], at("bias_ready", b))
                t = bank16(TRB, BF16)
                transposes(t[:, 0:S], bias_st[:, :, 0:T0], identb[:, :])
                transposes(t[:, S:2 * S], bias_rem[:, :, :, :].rearrange("p s j r -> p s (j r)"), identb[:, :]
                           ).then_inc(SEM["bias_tr"], 1)

            def turn_xn0(b, _):
                pe.wait_ge(SEM["xn0_ready"], at("xn0_ready", b))
                pe.wait_ge(SEM["bias_t_ready"], at("bias_t_ready", b))
                transposes(bank(TRB), xn0, ident).then_inc(SEM["xn0_tr"], 1)

            def queries(b, g):
                if g == 0:
                    pe.wait_ge(SEM["xn0_t_ready"], at("xn0_t_ready", b))
                    pe.wait_ge(SEM["v_ready"], at("v_ready", b))
                elif g >= 2:
                    pe.wait_ge(SEM["q_ready"], at("q_ready", b, g - 1))
                nc.tensor.matmul(bank(SCB[g % 2]), wq_rep[:, HG * g:HG * g + HG, :].rearrange("p h r -> p (h r)"),
                                 xn0_t[:, :], start=True, stop=True).then_inc(SEM["q_mm"], 1)

            def row_scores(b, n):
                g, s = divmod(n, ST)
                if s == 0:
                    pe.wait_ge(SEM["q_ready"], at("q_ready", b, g + 1))
                if n == 0:
                    pe.wait_ge(SEM["k_ready"], at("k_ready", b))
                for h in range(2):
                    if n >= 1:
                        pe.wait_ge(SEM["max_done"], at("max_done", b, 2 * n + h - 1))
                    o = bank(ROWB[h])[:, 0:2 * T]
                    nc.tensor.matmul(o, qst[:, g, P * s:P * s + P],
                                     kdiag[:, g, 2 * h:2 * h + 2, :].rearrange("p h t -> p (h t)"),
                                     start=True, stop=False)
                    nc.tensor.matmul(o.rearrange("p (h t) -> p h t", h=2), identb[:, :],
                                     bias_st[:, s, :].unsqueeze(1).broadcast_to([P, 2, T]),
                                     start=False, stop=True).then_inc(SEM["max_mm"], 1)

            def max_rows(b, g):
                pe.wait_ge(SEM["max_done"], at("max_done", b, 2 * ST * (g + 1)))
                if g >= 1:
                    pe.wait_ge(SEM["q_shifted"], at("q_shifted", b, g))
                transposes(bank16(TRB, F16)[:, 0:S], neg_max[:, g, :, :], ident16[:, :]
                           ).then_inc(SEM["max_tr"], 1)

            def scores(b, n):
                g, j = divmod(n, HG + 1)
                pe.wait_ge(SEM["q_shifted"], at("q_shifted", b, g + 1))
                if n == 0:
                    pe.wait_ge(SEM["q_ready"], at("q_ready", b))
                if n >= 2:
                    pe.wait_ge(SEM["probs_ready"], at("probs_ready", b, n - 1))
                keys = kdiag[:, g, j, 0:T0] if j < HG else krem[:, g, :, :].rearrange("p j r -> p (j r)")
                nc.tensor.matmul(bank(SCB[n % 2]), keys, qst[:, g, :], start=True, stop=False)
                nc.tensor.matmul(bank(SCB[n % 2]), identb[:, :], bias_t[:, j // HG, :],
                                 start=False, stop=True).then_inc(SEM["score_mm"], 1)

            def weighted_v(b, g):
                if g >= 1:
                    pe.wait_ge(SEM["av_ready"], at("av_ready", b, g))
                for j in range(HG):
                    pe.wait_ge(SEM["probs_ready"], at("probs_ready", b, (HG + 1) * g + j + 1))
                    nc.tensor.matmul(ps[ROWS * j:ROWS * j + ROWS, AVB, :], vaug[:, HG * g + j, :],
                                     probs_t[:, g % 2, j, :], start=True, stop=False, skip_group_check=True)
                pe.wait_ge(SEM["probs_ready"], at("probs_ready", b, (HG + 1) * (g + 1)))
                nc.tensor.matmul(bank(AVB), vrem[:, g, :, :].rearrange("p j r -> p (j r)"),
                                 probs_t[:, g % 2, HG, :], start=False, stop=True, skip_group_check=True
                                 ).then_inc(SEM["av_mm"], 1)

            def values_back(b, g):
                pe.wait_ge(SEM["av_ready"], at("av_ready", b, g + 1))
                if g == 0:
                    pe.wait_ge(SEM["q_shifted"], at("q_shifted", b))
                else:
                    pe.wait_ge(SEM["att_ready"], at("att_ready", b, g))
                transposes(bank(TRB), av_t[:, g % 2, :].rearrange("p (s q) -> p s q", q=P), ident
                           ).then_inc(SEM["av_tr"], 1)

            def project(b, _):
                pe.wait_ge(SEM["att_ready"], at("att_ready", b))
                transposes(bank(TRB), att, ident).then_inc(SEM["att_tr"], 1)
                pe.wait_ge(SEM["att_t_ready"], at("att_t_ready", b))
                for s in range(ST):
                    last = nc.tensor.matmul(bank(AVB)[:, D * s:D * s + D], att_t[:, P * s:P * s + P], w("wu0"),
                                            start=True, stop=True)
                last.then_inc(SEM["y0_mm"], 1)

            def turn_xn1(b, _):
                pe.wait_ge(SEM["xn1_ready"], at("xn1_ready", b))
                transposes(bank(BA), xn, ident).then_inc(SEM["xn1_tr"], 1)

            def gate_logits(b, _):
                pe.wait_ge(SEM["xlo_ready"], at("xlo_ready", b))
                for s in range(ST):
                    o = bank(BB)[:, E_N * s:E_N * s + E_N]
                    hi, lo = xn_hi[:, P * s:P * s + P], xn_lo[:, P * s:P * s + P]
                    nc.tensor.matmul(o, hi, wg_hi[:, :], start=True, stop=False)
                    nc.tensor.matmul(o, hi, wg_lo[:, :], start=False, stop=False)
                    last = nc.tensor.matmul(o, lo, wg_hi[:, :], start=False, stop=True)
                last.then_inc(SEM["gate_mm"], 1)

            def comb_turn(b, _):
                pe.wait_ge(SEM["comb_ready"], at("comb_ready", b))
                transposes(bank16(BA, F16)[:, 0:S], comb, ident16[:, :]).then_inc(SEM["comb_tr"], 1)

            def spread(b, e):
                if e == 0:
                    pe.wait_ge(SEM["comb_t_ready"], at("comb_t_ready", b))
                if e >= 2:
                    pe.wait_ge(SEM["cbc_ready"], at("cbc_ready", b, e - 1))
                nc.tensor.matmul(bank((BB, BA)[e % 2]), sel[:, e, :], comb_t[:, :], start=True, stop=True
                                 ).then_inc(SEM["cbc_mm"], 1)

            def up(b, f):
                if f == 0:
                    pe.wait_ge(SEM["cbc_ready"], at("cbc_ready", b))
                else:
                    pe.wait_ge(SEM["h_ready"], at("h_ready", b, f))
                nc.tensor.matmul(bank(BA), w1_hi[:, f, :], xn_hi[:, :], start=True, stop=False)
                nc.tensor.matmul(bank(BA), w1_hi[:, f, :], xn_lo[:, :], start=False, stop=False)
                nc.tensor.matmul(bank(BA), w1_lo[:, f, :], xn_hi[:, :], start=False, stop=True
                                 ).then_inc(SEM["up_mm"], 1)

            def ffn_step(b, f):
                if f + 1 < FC:
                    up(b, f + 1)
                pe.wait_ge(SEM["hc_ready"], at("hc_ready", b, f + 1))
                nc.tensor.matmul(bank(BB), w2_sb[:, f, :], hc_sb[:, f % 3, :], start=(f == 0),
                                 stop=(f == FC - 1)).then_inc(SEM["down_mm"], 1)

            def ffn_out(b, _):
                pe.wait_ge(SEM["ffn_t_ready"], at("ffn_t_ready", b))
                transposes(bank(BA), ffn_t[:, :].rearrange("p (s q) -> p s q", q=P), ident
                           ).then_inc(SEM["ffn_tr"], 1)

            def turn_xn2(b, _):
                pe.wait_ge(SEM["xn2_ready"], at("xn2_ready", b))
                transposes(bank(BB), xn, ident).then_inc(SEM["xn2_tr"], 1)

            def q1(b, _):
                pe.wait_ge(SEM["xn2_t_ready"], at("xn2_t_ready", b))
                nc.tensor.matmul(bank(BA), w("wq1"), xn_t[:, :], start=True, stop=True
                                 ).then_inc(SEM["q1_mm"], 1)

            def s1(b, _):
                pe.wait_ge(SEM["q1_ready"], at("q1_ready", b))
                for s in range(ST):
                    keys = khat[:, b, :] if isinstance(b, int) else khat[:, bass.ds(b, 1), :].rearrange(
                        "p b t -> p (b t)")
                    last = nc.tensor.matmul(s1_ps[:, s, :], q1_t[:, P * s:P * s + P], keys, start=True, stop=True)
                last.then_inc(SEM["s1_mm"], 1)

            def turn_p1(b, _):
                pe.wait_ge(SEM["p1_ready"], at("p1_ready", b))
                for s in range(ST):
                    for c in range(2):
                        last = nc.tensor.transpose(ps[0:TH, (BA, BB)[c], P * s:P * s + P],
                                                   p1[:, s, TH * c:TH * c + TH], ident)
                last.then_inc(SEM["p1_tr"], 1)

            def o1(b, _):
                pe.wait_ge(SEM["p1a_ready"], at("p1a_ready", b))
                pe.wait_ge(SEM["p1b_ready"], at("p1b_ready", b))
                for s in range(ST):
                    for c in range(2):
                        values = v1[0:TH, b, c, :] if isinstance(b, int) else v1[
                            0:TH, bass.ds(b, 1), c, :].rearrange("p b d -> p (b d)")
                        last = nc.tensor.matmul(bank(BA)[:, D * s:D * s + D], p1_t[0:TH, c, P * s:P * s + P],
                                                values, start=(c == 0), stop=(c == 1))
                last.then_inc(SEM["o1_mm"], 1)

            def turn_xq(b, _):
                pe.wait_ge(SEM["xq_ready"], at("xq_ready", b))
                transposes(bank16(BB, BF16)[:, 0:S], xq, identb[:, :]).then_inc(SEM["xq_tr"], 1)

            def y1(b, _):
                pe.wait_ge(SEM["xq_t_ready"], at("xq_t_ready", b))
                for s in range(ST):
                    last = nc.tensor.matmul(bank(BA)[:, D * s:D * s + D], xq_t[:, P * s:P * s + P], kern_q[:, :],
                                            start=True, stop=True)
                last.then_inc(SEM["y1_mm"], 1)

            steps = {
                "context": context, "bias_t": turn_bias, "xn0_t": turn_xn0, "queries": queries,
                "row_scores": row_scores, "max_rows": max_rows, "scores": scores, "weighted_v": weighted_v,
                "values_back": values_back, "project": project, "xn1_t": turn_xn1, "gate": gate_logits,
                "comb_t": comb_turn, "spread": spread, "up": up, "ffn": ffn_step, "ffn_out": ffn_out,
                "xn2_t": turn_xn2, "q1": q1, "s1": s1, "p1_t": turn_p1, "o1": o1, "xq_t": turn_xq, "y1": y1,
            }
            pe.wait_ge(attn_w_set, 1)
            run(steps, prep, 0, None)
            context_features()
            context_projections()
            run(steps, rows, 0, None)
            second_values()
            run(steps, attn, 0, None)
            pe.wait_ge(v1_ready, 1)
            pe.wait_ge(ffn_w_set, 1)
            pe.wait_ge(w2_in, 16)
            pe.wait_ge(khat_ready, 1)
            with pe.Fori(0, B - 1) as i:
                run(steps, BOTH, i + 1, i)
            run(steps, BACK, None, B - 1)


def kernel(**inputs):
    import numpy as _np
    import concourse.bacc as _bacc
    from concourse import mybir as _mybir
    from concourse.bass_utils import run_bass_kernel_spmd as _run

    a = {n: _np.asarray(v) for n, v in inputs.items()}

    def rows(v):
        return _np.broadcast_to(v.reshape(1, -1), (P, v.size))

    def heads(v):
        return v.transpose(1, 0, 2).reshape(P, P)

    parts = {
        "wq0": heads(a["L0_xattn_Wq"]), "wk0": heads(a["L0_xattn_Wk"]), "wv0": heads(a["L0_xattn_Wv"]),
        "wu0": a["L0_xattn_Wu"], "bu0": rows(a["L0_xattn_bu"]),
        "g": rows(_np.stack([a["g_xattn"], a["g_ffn"]], 1)),
        "s": rows(_np.concatenate([a["L1_ffn_input_scale"], a["L1_ffn_kernel_scale"]])),
        "wg": a["L0_ffn_Wg"], "wq1": a["L1_xattn_Wq"], "wk1": a["L1_xattn_Wk"], "wv1": a["L1_xattn_Wv"],
        "wr1": a["L1_xattn_Wr"], "bq1": a["L1_xattn_bq"].reshape(P, 1), "bk1": a["L1_xattn_bk"].reshape(P, 1),
        "br1": a["L1_xattn_br"].reshape(P, 1), "bv1": rows(a["L1_xattn_bv"]),
    }
    wts = _np.concatenate([parts[n] for n in W_COLS], 1)
    row = _np.arange(P) % ROWS
    part = row // DK
    consts = _np.zeros((P, C_TOTAL), _np.float32)
    consts[:, 0:P] = _np.eye(P)
    consts[:, C_COLS["lo_q"][0]] = -(part == 1).astype(_np.float32)
    consts[:, C_COLS["lo_k"][0]] = (row == MROW).astype(_np.float32) - (part == 2)
    consts[:, C_COLS["one"][0]] = row == MROW
    consts[:, slice(*C_COLS["iota"])] = _np.arange(E_N)
    arrays = {
        "x": a["x"],
        "ctx_t": a["ctx_1024"].transpose(0, 2, 1),
        "mask": a["mask_BxSxS2_ik1"],
        "wts": wts,
        "w1": a["L0_ffn_W1"].transpose(1, 0, 2).reshape(P, -1),
        "w2": a["L0_ffn_W2"].reshape(FC, P, P).transpose(1, 0, 2).reshape(P, -1),
        "kern": a["L1_ffn_kernel"],
        "kbias": rows(a["L1_ffn_bias"]),
        "consts": consts,
    }
    arrays = {n: _np.ascontiguousarray(v) for n, v in arrays.items()}
    nc = _bacc.Bacc("TRN2", target_bir_lowering=False, num_devices=1)
    args = [nc.dram_tensor(n, v.shape, _mybir.dt.from_np(v.dtype), kind="ExternalInput").ap()
            for n, v in arrays.items()]
    out = nc.dram_tensor("out", a["x"].shape, F32, kind="ExternalOutput").ap()
    flamingo_gated(nc, *args, out)
    return _run(nc, [arrays], core_ids=[0]).results[0]["out"]
```

```python
from contextlib import ExitStack

import concourse.bass as bass
from concourse import mybir

P = 128
ALU = mybir.AluOpType
ACT = mybir.ActivationFunctionType
X = mybir.AxisListType.X
F32 = mybir.dt.float32
BF16 = mybir.dt.bfloat16
F16 = mybir.dt.float16
I32 = mybir.dt.int32
U32 = mybir.dt.uint32

H, DK = 16, 8
HG = 4
NG = H // HG
ROWS = P // HG
MROW = 3 * DK
E_N, F_N = 8, 256
FC = E_N * F_N // P
NH = 6
WS = 64.0
MASKED = -1.0e30
EPS = 1e-5
TWO_PI = 6.283185307179586
TWO_PI_HI = 6.28125
TWO_PI_LO = TWO_PI - TWO_PI_HI
PI = 3.1415925
ROUND = 12582912.0

W_COLS = {}
_at = 0
for _name, _n in [("wq0", 128), ("wk0", 128), ("wv0", 128), ("wu0", 128), ("bu0", 128), ("g", 4), ("s", 2),
                  ("wg", 8), ("wq1", 128), ("wk1", 128), ("wv1", 128), ("wr1", 128), ("bq1", 1), ("bk1", 1),
                  ("br1", 1), ("bv1", 128)]:
    W_COLS[_name] = (_at, _at + _n)
    _at += _n
W_TOTAL = _at
W_EARLY = W_COLS["wg"][0]
C_COLS = {"ident": (0, 128), "one": (128, 129), "iota": (129, 137)}
C_TOTAL = 137


def flamingo_gated(nc, x, ctx_t, mask, wts, w1, w2, kern, kbias, consts, out):
    B, S, D = x.shape
    T = ctx_t.shape[2]
    ST = S // P
    T0 = P
    TR = T - T0
    SH = S // 2
    TH = T // 2
    assert D == P and TR <= ROWS and T % 2 == 0

    x_v = x.rearrange("b (s p) d -> b p s d", p=P)
    out_v = out.rearrange("b (s p) d -> b p s d", p=P)
    mask_v = mask.rearrange("b (s p) t -> b p s t", p=P)

    with ExitStack() as stack:
        def sb(name, shape, dt):
            return stack.enter_context(nc.sbuf_tensor(name, shape, dt))

        def sem(name):
            return stack.enter_context(nc.semaphore(name))

        w_sb = sb("w_sb", [P, W_TOTAL], F32)
        c_sb = sb("c_sb", [P, C_TOTAL], F32)
        w1_sb = sb("w1_sb", [P, FC * P], F32)
        w1_hi = sb("w1_hi", [P, FC, P], F16)
        w1_lo = sb("w1_lo", [P, FC, P], F16)
        w1_s = sb("w1_s", [P, FC * P], F32)
        w2_sb = sb("w2_sb", [P, FC, P], F32)
        wg_s = sb("wg_s", [P, E_N], F32)
        wg_hi = sb("wg_hi", [P, E_N], F16)
        wg_lo = sb("wg_lo", [P, E_N], F16)
        wk_s = sb("wk_s", [P, P], F32)
        wq_s = sb("wq_s", [P, P], F32)
        q_rep_hi = sb("q_rep_hi", [P, H, ROWS], F16)
        q_rep_lo = sb("q_rep_lo", [P, H, ROWS], F16)
        k_rep_hi = sb("k_rep_hi", [P, H, ROWS], F16)
        k_rep_lo = sb("k_rep_lo", [P, H, ROWS], F16)
        kern_sb = sb("kern_sb", [P, P], BF16)
        kbias_sb = sb("kbias_sb", [P, P], BF16)
        kern_q = sb("kern_q", [P, P], BF16)
        gates = sb("gates", [P, 4], F32)
        s_inv = sb("s_inv", [P, 2], F32)
        s_prod = sb("s_prod", [P, 1], F32)
        ident16 = sb("ident16", [P, P], F16)
        identb = sb("identb", [P, P], BF16)
        half_neg = sb("half_neg", [P, ST], F32)
        eps = sb("eps", [P, ST], F32)
        carrier = sb("carrier", [P, 1], F32)
        khat = sb("khat", [P, B, T], F32)
        ctx_all = sb("ctx_all", [P, B, T], F32)
        v1 = sb("v1", [P, B, 2, D], F32)
        kz = sb("kz", [P, B, T], F32)
        kz_n = sb("kz_n", [P, B, T], F32)
        kz_k = sb("kz_k", [P, B, T], F32)

        ident = c_sb[:, 0:P]

        def w(name):
            a, b = W_COLS[name]
            return w_sb[:, a:b]

        def cst(name):
            a, b = C_COLS[name]
            return c_sb[:, a:b]

        x_in = sb("x_in", [P, ST, D], F32)
        x_res = sb("x_res", [P, ST, D], F32)
        ctx_sb = sb("ctx_sb", [P, T], F32)
        mask_sb = sb("mask_sb", [P, ST, T], I32)
        ctx_rem = sb("ctx_rem", [P, HG, ROWS], F32)
        is_zero = sb("is_zero", [P, ST, T], F32)
        all_zero = sb("all_zero", [P, ST], F32)
        keep = sb("keep", [P, ST], F32)
        fill = sb("fill", [P, ST], F32)
        bias_st = sb("bias_st", [P, ST, T], BF16)
        bias_rem = sb("bias_rem", [P, ST, HG, ROWS], BF16)
        bias_t = sb("bias_t", [P, 2, S], BF16)
        k_hi = sb("k_hi", [P, T], F16)
        k_lo = sb("k_lo", [P, T], F16)
        kdiag = sb("kdiag", [P, NG, HG, T], F16)
        krem = sb("krem", [P, NG, HG, ROWS], F16)
        vaug = sb("vaug", [P, H, ROWS], F32)
        vrem = sb("vrem", [P, NG, HG, ROWS], F32)
        stats = sb("stats", [P, 4, ST, 6], F32)
        mv = sb("mv", [P, 4, ST, 2], F32)
        var_e = sb("var_e", [P, 4, ST], F32)
        rstd = sb("rstd", [P, 4, ST], F32)
        rstd_q = sb("rstd_q", [P, ST], F32)
        xn0 = sb("xn0", [P, ST, D], F32)
        xn0_t = sb("xn0_t", [P, S], F32)
        xn = sb("xn", [P, ST, D], F32)
        xn_t = sb("xn_t", [P, S], F32)
        q_hi = sb("q_hi", [P, S], F16)
        q_lo = sb("q_lo", [P, S], F16)
        qst = sb("qst", [P, NG, S], F16)
        neg_max = sb("neg_max", [P, NG, ST, P], F16)
        probs_t = sb("probs_t", [P, 2, HG + 1, S], F32)
        av_t = sb("av_t", [P, 2, S], F32)
        inv_sum = sb("inv_sum", [P, ST, HG], F32)
        att = sb("att", [P, ST, D], F32)
        att_t = sb("att_t", [P, S], F32)
        y_b = sb("y_b", [P, ST, D], F32)
        x1 = sb("x1", [P, ST, D], F32)
        xn_hi = sb("xn_hi", [P, S], F16)
        xn_lo = sb("xn_lo", [P, S], F16)
        logits = sb("logits", [P, ST, E_N], F32)
        top8 = sb("top8", [P, ST, 8], F32)
        top_i = sb("top_i", [P, ST, 8], U32)
        top_f = sb("top_f", [P, ST, 2], F32)
        gap = sb("gap", [P, ST], F32)
        e_gap = sb("e_gap", [P, ST], F32)
        gw = sb("gw", [P, 3, ST], F32)
        pick = sb("pick", [P, 3, ST, E_N], F32)
        wx = sb("wx", [P, ST, E_N], F32)
        h_sb = sb("h_sb", [P, NH, S], F32)
        acc = sb("acc", [P, 2, ST, D], F32)
        q1_t = sb("q1_t", [P, S], F32)
        nmax1 = sb("nmax1", [P, ST], F32)
        sum1 = sb("sum1", [P, ST], F32)
        r1 = sb("r1", [P, ST], F32)
        r1g = sb("r1g", [P, ST], F32)
        p1 = sb("p1", [P, ST, T], F32)
        p1_t = sb("p1_t", [P, 2, 2 * SH], F32)
        x3 = sb("x3", [P, ST, D], F32)
        xb = sb("xb", [P, ST, D], BF16)
        fv = sb("fv", [P, ST * D], F32)
        fe = sb("fe", [P, ST * D], I32)
        fc = sb("fc", [P, ST * D], F32)
        fw = sb("fw", [P, ST * D], F32)
        fq = sb("fq", [P, ST * D], F32)
        fo = sb("fo", [P, ST * D], F32)
        xq = sb("xq", [P, ST, D], BF16)
        xq_t = sb("xq_t", [P, S], BF16)
        y_s = sb("y_s", [P, ST, D], BF16)
        y_sb = sb("y_sb", [P, ST, D], BF16)
        x4 = sb("x4", [P, ST, D], F32)

        ps = stack.enter_context(nc.psum_tensor("ps", [P, 8, 512], F32))

        def bank(n):
            return ps[:, n, :]

        def bank16(n, dt):
            return ps[:, n, :].bitcast(dt)

        ROWB, SCB, AVB, TRB, BA, BB = (0, 1), (2, 3), 4, 5, 6, 7

        def halves(b):
            return ps[:, b:b + 2, :].rearrange("p a (b t) -> p (a b) t", b=2)[:, :, 0:T]

        UPB, DOWNB = (BA, AVB), (BB, SCB[1])
        k_ps = halves(ROWB[0])

        def half_bank(h):
            return ps[:, (BA, BB)[h], :].rearrange("p (s t) -> p s t", s=2)

        consts_in, early_in, late_in, ctx_all_in, w1_in, w2_in, kern_in = map(
            sem, ["consts_in", "early_in", "late_in", "ctx_all_in", "w1_in", "w2_in", "kern_in"])
        zeros_set, ones_set, gates_set, kc_mm, kc_ready, z_mm, z_reduced, khat_ready = map(
            sem, ["zeros_set", "ones_set", "gates_set", "kc_mm", "kc_ready", "z_mm", "z_reduced", "khat_ready"])
        attn_w_set, ffn_w_set, dve_setup, v1_mm, v1_ready = map(
            sem, ["attn_w_set", "ffn_w_set", "dve_setup", "v1_mm", "v1_ready"])
        w1_steps = sem("w1_steps")
        x_loaded, x_res_loaded, ctx_loaded, mask_loaded, stored = map(
            sem, ["x_loaded", "x_res_loaded", "ctx_loaded", "mask_loaded", "stored"])
        dve_step, pool_step = sem("dve_step"), sem("pool_step")
        DVE_START, DVE_LOOP = 15, 39
        POOL_START, POOL_LOOP = 3, 6

        PER = {
            "ctx_rem_ready": 1, "mask_zero": 1, "bias_ready": 1, "bias_tr": 1, "bias_t_ready": 1,
            "k_mm": 1, "k_hi_ready": 1, "k_lo_ready": 1, "k_rep_mm": 1, "k_diag_ready": 1, "k_ready": 1,
            "v_mm": 1, "v_ready": 1,
            "var0_ready": 1, "rstd0_ready": 1, "xn0_ready": 1, "xn0_tr": 1, "xn0_t_ready": 1,
            "q_mm": 1, "q_hi_ready": 1, "q_lo_ready": 1, "q_rep_mm": NG, "q_ready": NG,
            "max_mm": 2 * NG * ST, "max_done": 2 * NG * ST, "max_tr": NG, "q_shifted": NG,
            "score_mm": NG * (HG + 1), "probs_ready": NG * (HG + 1), "av_mm": NG, "av_ready": NG,
            "av_tr": NG, "att_ready": NG, "att_tr": 1, "att_t_ready": 1, "y0_mm": 1,
            "y0_read": 1, "x1_ready": 1,
            "var1_ready": 1, "rstd1_ready": 1, "xn1_ready": 1, "xn1_tr": 1, "xhi_ready": 1, "xlo_ready": 1,
            "gate_mm": 1, "gate_read": 1, "gap_ready": 1, "e_gap_ready": 1, "up_mm": FC, "h_ready": FC,
            "down_mm": E_N, "added": E_N,
            "var2_ready": 2, "rstd2_ready": 2, "xn2_ready": 2, "xn2_tr": 2, "xn2_t_ready": 2, "q1_mm": 2,
            "q1_ready": 2, "s1_mm": 2, "nmax1_ready": 2, "p1_ready": 2, "p1_tr": 2, "p1_t_ready": 2,
            "r1_ready": 2, "o1_mm": 2, "x3_ready": 2,
            "var3_ready": 2, "rstd3_ready": 2, "xn3_ready": 2, "xq_ready": 2,
            "xq_tr": 2, "xq_t_ready": 2, "y1_mm": 2, "y1_ready": 2, "x4_ready": 2,
        }
        SEM = {name: sem(name) for name in PER}

        def at(name, b, k=None):
            return b * PER[name] + (PER[name] if k is None else k)

        PREP = {"ctx_rem", "mask", "norm0_a", "norm0_b", "bias", "context", "k_blocks", "v_blocks", "bias_t",
                "xn0_t", "q_parts", "queries", "k_lo", "k_rows"}
        ONCE = {"kc", "z", "v1", "w_up", "w_gate", "w_fp8"}
        ATTENTION = {"row_scores", "max_rows", "scores", "weighted_v", "av_copy", "values_back", "project",
                     "norm1_a", "norm1_b", "xn1_t"}

        def listed(text):
            return [(step.partition(":")[0], int(step.partition(":")[2] or 0)) for step in text.split()]

        FIRST = listed("""
            norm0_a mask ctx_rem norm0_b bias warm context k_lo v_blocks xn0_t bias_t q_parts k_rows
            k_blocks queries:0 queries:1 queries:2 queries:3
            """)
        START = listed("""
            row_scores:0 row_scores:1 row_scores:2 row_scores:3 row_scores:4 row_scores:5
            row_scores:6 max_rows:0 row_scores:7 row_scores:8 row_scores:9 max_rows:1 scores:0
            scores:1 row_scores:10 scores:2 row_scores:11 scores:3 row_scores:12 scores:4 max_rows:2
            scores:5 row_scores:13 w_up:0 scores:6 row_scores:14 scores:7 scores:8 w_up:1
            row_scores:15 kc scores:9 scores:10 ctx_rem av_copy:0 norm0_a w_gate mask max_rows:3
            weighted_v:0 scores:11 scores:12 z weighted_v:1 norm0_b scores:13 scores:14
            values_back:0 scores:15 av_copy:1 scores:16 bias scores:17 values_back:1 scores:18 w_fp8
            v1 weighted_v:2 scores:19 av_copy:2 values_back:2 k_lo weighted_v:3 context k_rows
            av_copy:3 w_up:2 values_back:3 project k_blocks xn0_t norm1_a v_blocks bias_t q_parts
            queries:0 norm1_b xn1_t queries:1 queries:2 queries:3
            """)
        LOOP = listed("""
            row_scores:0 gate top2 combine row_scores:1 up:0 up:1 up:2 row_scores:2 row_scores:3
            row_scores:4 up:3 row_scores:5 up:4 row_scores:6 down:0 max_rows:0 row_scores:7 down:1
            up:5 row_scores:8 max_rows:1 up:6 row_scores:9 up:7 row_scores:10 down:2 up:8
            row_scores:11 row_scores:12 down:3 row_scores:13 up:9 max_rows:2 up:10 row_scores:14
            mask norm0_a up:11 row_scores:15 up:12 down:4 up:13 bias down:5 norm0_b up:14 max_rows:3
            up:15 down:6 down:7 scores:0 scores:1 warm_last norm2_a:0 scores:2 warm_last norm2_a:1
            scores:3 xn2_t:0 scores:4 scores:5 xn2_t:1 scores:6 q1:0 scores:7 q1:1 ctx_rem norm2_b:0
            scores:8 scores:9 norm2_b:1 s1:0 s1:1 scores:10 weighted_v:0 p1_t:0 scores:11 p1_t:1
            scores:12 o1:0 av_copy:0 scores:13 norm3_a:0 o1:1 scores:14 warm_last values_back:0
            warm_last weighted_v:1 norm3_a:1 av_copy:1 scores:15 norm3_b:0 scores:16 av_copy:2
            weighted_v:2 quantize:0 norm3_b:1 scores:17 quantize:1 values_back:1 xq_t:0 scores:18
            y1:0 scores:19 weighted_v:3 values_back:2 av_copy:3 xn0_t context k_lo xq_t:1
            values_back:3 v_blocks q_parts y1:1 warm_last project norm1_a queries:0 norm1_b k_rows
            k_blocks queries:1 queries:2 bias_t xn1_t queries:3
            """)

        for order in (FIRST, START, LOOP):
            names = [name for name, _ in order]
            for earlier, later in (("mask", "norm0_b"), ("mask", "bias"), ("top2", "combine"), ("combine", "down")):
                assert later not in names or earlier not in names or names.index(earlier) < names.index(later)

        def run(steps, order, b):
            for name, k in order:
                ahead = 2 if name in PREP else 1 if name in ATTENTION | ONCE else 0
                exists = not isinstance(b, int) or 0 <= b + ahead < B
                if name == "warm_last":
                    exists = isinstance(b, int) and b == B - 1
                if name in steps and (exists or name == "warm"):
                    steps[name](b + ahead, k)

        def tiles(half):
            return (slice(0, ST), 1) if half is None else (slice(ST // 2 * half, ST // 2 * (half + 1)), half + 1)

        def alone(eng):
            eng.wait_ge(consts_in, 16)

        block = stack.enter_context(nc.Block())

        @block.sync
        def _(sp):
            sp.dma_start(x_in[:, :, :], x_v[0, :, :, :]).then_inc(x_loaded, 16)
            sp.dma_start(w_sb[:, 0:W_EARLY], wts[:, 0:W_EARLY]).then_inc(early_in, 16)
            sp.dma_start(ctx_sb[:, :], ctx_t[0, :, :]).then_inc(ctx_loaded, 16)
            sp.dma_start(c_sb[:, :], consts[:, :]).then_inc(consts_in, 16)
            sp.dma_start(mask_sb[:, :, :], mask_v[0, :, :, :]).then_inc(mask_loaded, 16)
            sp.dma_start(w_sb[:, W_EARLY:W_TOTAL], wts[:, W_EARLY:W_TOTAL]).then_inc(late_in, 16)
            sp.dma_start(ctx_all[:, :, :], ctx_t.rearrange("b d t -> d b t")).then_inc(ctx_all_in, 16)
            sp.dma_start(w1_sb[:, :], w1[:, :]).then_inc(w1_in, 16)
            sp.dma_start(kern_sb[:, :], kern[:, :]).then_inc(kern_in, 16)
            sp.dma_start(kbias_sb[:, :], kbias[:, :]).then_inc(kern_in, 16)
            sp.dma_start(x_res[:, :, :], x_v[0, :, :, :]).then_inc(x_res_loaded, 16)
            sp.dma_start(w2_sb[:, :, :], w2.rearrange("p (c d) -> p c d", d=D)).then_inc(w2_in, 16)
            sp.sem_inc(stored, 1)

            def tokens(v, b):
                return v[b, :, :, :] if isinstance(b, int) else v[bass.ds(b, 1), :, :, :].rearrange(
                    "a p s d -> (a p) s d")

            def load_next(b):
                sp.wait_ge(SEM["v_mm"], at("v_mm", b - 1))
                sp.dma_start(ctx_sb[:, :], ctx_t[b, :, :] if isinstance(b, int) else
                             ctx_t[bass.ds(b, 1), :, :].rearrange("a d t -> (a d) t")).then_inc(ctx_loaded, 16)
                sp.wait_ge(SEM["mask_zero"], at("mask_zero", b - 1))
                sp.dma_start(mask_sb[:, :, :], tokens(mask_v, b)).then_inc(mask_loaded, 16)
                sp.wait_ge(SEM["xn0_ready"], at("xn0_ready", b - 1))
                sp.dma_start(x_in[:, :, :], tokens(x_v, b)).then_inc(x_loaded, 16)

            def load_residual(b):
                sp.wait_ge(SEM["x1_ready"], at("x1_ready", b - 1))
                sp.dma_start(x_res[:, :, :], tokens(x_v, b)).then_inc(x_res_loaded, 16)

            def store(b):
                sp.wait_ge(SEM["x4_ready"], at("x4_ready", b))
                sp.dma_start(tokens(out_v, b), x4[:, :, :]).then_inc(stored, 16)

            load_next(1)
            load_residual(1)
            with sp.Fori(0, B - 2) as i:
                load_next(i + 2)
                store(i)
                load_residual(i + 2)
            store(B - 2)
            store(B - 1)
            sp.wait_ge(stored, 16 * B + 1)

        @block.gpsimd
        def _(pool):
            for t in (q_rep_hi, q_rep_lo, k_rep_hi, k_rep_lo, ctx_rem, krem, vaug, vrem):
                nc.gpsimd.memset(t[:], 0.0).then_inc(zeros_set, 1)
            nc.gpsimd.memset(bias_rem[:], MASKED).then_inc(zeros_set, 1)
            nc.gpsimd.memset(half_neg[:], -0.5).then_inc(zeros_set, 1)
            nc.gpsimd.memset(eps[:], EPS).then_inc(zeros_set, 1)
            pool.wait_ge(zeros_set, 11)
            nc.gpsimd.memset(vaug[:, :, DK:DK + 1], 1.0).then_inc(ones_set, 1)
            for j in range(HG):
                pool.wait_ge(ones_set, j + 1)
                nc.gpsimd.memset(vrem[ROWS * j:ROWS * j + ROWS, :, j, DK:DK + 1], 1.0).then_inc(ones_set, 1)

            chain = [0, 0]

            def norm_a(b, n, half=None):
                t, k = tiles(half)
                pool.wait_ge(SEM[f"var{n}_ready"], at(f"var{n}_ready", b, k))
                chain[1] += 1
                nc.gpsimd.tensor_tensor(var_e[:, n, t], mv[:, n, t, 1], eps[:, t], ALU.add).then_inc(pool_step, 1)
                pool.wait_ge(pool_step, chain[0] + chain[1])
                nc.gpsimd.tensor_tensor(rstd[:, n, t], var_e[:, n, t], half_neg[:, t], ALU.pow
                                        ).then_inc(SEM[f"rstd{n}_ready"], 1)

            def up_weights(_, k):
                w1_hf = w1_hi[:, :, :].rearrange("p c f -> p (c f)")
                w1_lf = w1_lo[:, :, :].rearrange("p c f -> p (c f)")
                if k == 0:
                    pool.wait_ge(w1_in, 16)
                    nc.gpsimd.tensor_scalar(w1_s[:, :], w1_sb[:, :], WS, None, ALU.mult).then_inc(w1_steps, 1)
                elif k == 1:
                    pool.wait_ge(w1_steps, 1)
                    nc.gpsimd.tensor_copy(w1_hf, w1_s[:, :]).then_inc(w1_steps, 1)
                else:
                    pool.wait_ge(w1_steps, 2)
                    nc.gpsimd.tensor_tensor(w1_lf, w1_s[:, :], w1_hf, ALU.subtract).then_inc(ffn_w_set, 1)

            steps = {"norm0_a": lambda b, _: norm_a(b, 0), "norm1_a": lambda b, _: norm_a(b, 1),
                     "norm2_a": lambda b, half: norm_a(b, 2, half),
                     "norm3_a": lambda b, half: norm_a(b, 3, half), "w_up": up_weights}
            run(steps, FIRST, -2)
            run(steps, START, -1)
            assert chain[1] == POOL_START
            with pool.Fori(0, B - 2) as i:
                chain[:] = [POOL_START + i * POOL_LOOP, 0]
                run(steps, LOOP, i)
            assert chain[1] == POOL_LOOP
            chain[:] = [POOL_START + (B - 2) * POOL_LOOP, 0]
            run(steps, LOOP, B - 2)
            run(steps, LOOP, B - 1)

        @block.scalar
        def _(act):
            def context_features(*_):
                act.wait_ge(late_in, 16)
                act.wait_ge(kc_mm, 1)
                nc.scalar.activation(kz[:, :, :].rearrange("p (h b) t -> p h (b t)", h=2),
                                     ps[:, BA:BB + 1, 0:2 * T], ACT.Identity, bias=w("bk1")).then_inc(kc_ready, 1)

            def cosines(*_):
                act.wait_ge(z_reduced, 1)
                nc.scalar.activation(khat[:, :, :], kz_n[:, :, :], ACT.Sin).then_inc(khat_ready, 1)

            def context(b, _):
                act.wait_ge(SEM["k_mm"], at("k_mm", b))
                nc.scalar.activation(k_hi[:, :], bank(ROWB[1])[:, 0:T], ACT.Copy).then_inc(SEM["k_hi_ready"], 1)

            def k_blocks(b, _):
                act.wait_ge(SEM["k_rep_mm"], at("k_rep_mm", b))
                for j in range(HG):
                    r = slice(ROWS * j, ROWS * j + ROWS)
                    last = nc.scalar.activation(kdiag[r, :, j, :], k_ps[r, :, :], ACT.Identity,
                                                bias=cst("one")[r, :])
                last.then_inc(SEM["k_diag_ready"], 1)

            def copy_bias(b, _):
                act.wait_ge(SEM["bias_tr"], at("bias_tr", b))
                nc.scalar.activation(bias_t[:, :, :].rearrange("p a s -> p (a s)"), bank16(TRB, BF16), ACT.Copy
                                     ).then_inc(SEM["bias_t_ready"], 1)

            def copy_xn0(b, _):
                act.wait_ge(SEM["xn0_tr"], at("xn0_tr", b))
                nc.scalar.activation(xn0_t[:, :], bank(SCB[1]), ACT.Copy).then_inc(SEM["xn0_t_ready"], 1)

            def query_parts(b, _):
                act.wait_ge(SEM["q_mm"], at("q_mm", b))
                nc.scalar.activation(q_hi[:, :], bank(SCB[1]), ACT.Copy).then_inc(SEM["q_hi_ready"], 1)

            def queries(b, g):
                act.wait_ge(SEM["q_rep_mm"], at("q_rep_mm", b, g + 1))
                nc.scalar.activation(qst[:, g, :], bank(SCB[g % 2]), ACT.Copy
                                     ).then_inc(SEM["q_ready"], 1)

            def scores(b, n):
                g, j = divmod(n, HG + 1)
                act.wait_ge(SEM["score_mm"], at("score_mm", b, n + 1))
                if g >= 2 and j == 0:
                    act.wait_ge(SEM["av_mm"], at("av_mm", b, g - 1))
                nc.scalar.activation(probs_t[:, g % 2, j, :], bank(SCB[n % 2]), ACT.Exp
                                     ).then_inc(SEM["probs_ready"], 1)

            def av_copy(b, g):
                act.wait_ge(SEM["av_mm"], at("av_mm", b, g + 1))
                if g >= 2:
                    act.wait_ge(SEM["av_tr"], at("av_tr", b, g - 1))
                nc.scalar.activation(av_t[:, g % 2, :], bank(AVB), ACT.Copy).then_inc(SEM["av_ready"], 1)

            def project(b, _):
                act.wait_ge(SEM["att_tr"], at("att_tr", b))
                nc.scalar.activation(att_t[:, :], bank(TRB), ACT.Copy).then_inc(SEM["att_t_ready"], 1)

            def copy_xn1(b, _):
                act.wait_ge(SEM["xn1_tr"], at("xn1_tr", b))
                nc.scalar.activation(xn_hi[:, :], bank(BA), ACT.Copy).then_inc(SEM["xhi_ready"], 1)

            def top2(b, _):
                act.wait_ge(SEM["gap_ready"], at("gap_ready", b))
                nc.scalar.activation(e_gap[:, :], gap[:, :], ACT.Exp, scale=1.0 / WS
                                     ).then_inc(SEM["e_gap_ready"], 1)

            def silu(b, f):
                act.wait_ge(SEM["up_mm"], at("up_mm", b, f + 1))
                if f >= NH:
                    act.wait_ge(SEM["down_mm"], at("down_mm", b, (f - NH) // 2 + 1))
                nc.scalar.activation(h_sb[:, f % NH, :], bank(UPB[f % 2]), ACT.Silu, scale=1.0 / WS
                                     ).then_inc(SEM["h_ready"], 1)

            def copy_xn2(b, h):
                act.wait_ge(SEM["xn2_tr"], at("xn2_tr", b, h + 1))
                nc.scalar.activation(xn_t[:, SH * h:SH * h + SH], bank((BA, BB)[h])[:, 0:SH], ACT.Copy
                                     ).then_inc(SEM["xn2_t_ready"], 1)

            def q1(b, h):
                act.wait_ge(SEM["q1_mm"], at("q1_mm", b, h + 1))
                nc.scalar.activation(q1_t[:, SH * h:SH * h + SH], bank((BA, BB)[h])[:, 0:SH], ACT.Identity,
                                     bias=w("bq1")).then_inc(SEM["q1_ready"], 1)

            def s1(b, h):
                act.wait_ge(SEM["nmax1_ready"], at("nmax1_ready", b, h + 1))
                for s in range(ST // 2):
                    t = ST // 2 * h + s
                    last = nc.scalar.activation(p1[:, t, :], half_bank(h)[:, s, 0:T], ACT.Exp,
                                                bias=nmax1[:, t:t + 1], accum_out=sum1[:, t:t + 1])
                last.then_inc(SEM["p1_ready"], 1)

            def copy_p1(b, h):
                act.wait_ge(SEM["p1_tr"], at("p1_tr", b, h + 1))
                nc.scalar.activation(p1_t[0:TH, h, :], ps[0:TH, (BA, BB)[h], :], ACT.Copy
                                     ).then_inc(SEM["p1_t_ready"], 1)

            def copy_xq(b, h):
                act.wait_ge(SEM["xq_tr"], at("xq_tr", b, h + 1))
                nc.scalar.activation(xq_t[:, SH * h:SH * h + SH], bank16((BA, BB)[h], BF16)[:, 0:SH], ACT.Copy
                                     ).then_inc(SEM["xq_t_ready"], 1)

            def y1(b, h):
                act.wait_ge(SEM["y1_mm"], at("y1_mm", b, h + 1))
                nc.scalar.activation(y_s[:, tiles(h)[0], :].rearrange("p s d -> p (s d)"),
                                     bank((BA, BB)[h])[:, 0:SH], ACT.Copy,
                                     scale=s_prod[:, 0:1]).then_inc(SEM["y1_ready"], 1)

            steps = {
                "kc": context_features, "z": cosines, "context": context, "k_blocks": k_blocks, "bias_t": copy_bias,
                "xn0_t": copy_xn0, "q_parts": query_parts, "queries": queries, "scores": scores,
                "av_copy": av_copy, "project": project, "xn1_t": copy_xn1, "top2": top2,
                "up": silu, "xn2_t": copy_xn2, "q1": q1,
                "s1": s1, "p1_t": copy_p1, "xq_t": copy_xq, "y1": y1,
            }
            act.wait_ge(early_in, 16)
            nc.scalar.activation(gates[:, :], w("g"), ACT.Tanh).then_inc(gates_set, 1)
            act.wait_ge(consts_in, 16)
            run(steps, FIRST, -2)
            run(steps, START, -1)
            with act.Fori(0, B - 2) as i:
                run(steps, LOOP, i)
            run(steps, LOOP, B - 2)
            run(steps, LOOP, B - 1)

        @block.vector
        def _(dve):
            setup = [0]

            def set_up(ins):
                setup[0] += 1
                ins.then_inc(dve_setup, 1)
                dve.wait_ge(dve_setup, setup[0])

            def round_e4m3(step, v, c, dst):
                step(nc.vector.tensor_scalar(fe[:, c], v.bitcast(I32), 0x7F800000, None, ALU.bitwise_and))
                step(nc.vector.tensor_scalar(fc[:, c], fe[:, c].bitcast(F32), 2.0 ** -6, 1.5 * 2.0 ** 20,
                                             ALU.max, ALU.mult))
                step(nc.vector.tensor_tensor(fw[:, c], v, fc[:, c], ALU.add))
                step(nc.vector.tensor_tensor(fq[:, c], fw[:, c], fc[:, c], ALU.subtract))
                step(nc.vector.tensor_scalar(fo[:, c], fq[:, c], 7.2e35, 0.0, ALU.mult, ALU.mult))
                return nc.vector.tensor_tensor(dst, fo[:, c], fq[:, c], ALU.add)

            set_up(nc.vector.memset(kdiag[:], 0.0))
            set_up(nc.vector.memset(neg_max[:], 0.0))
            scale = float(DK) ** -0.25
            dve.wait_ge(early_in, 16)
            dve.wait_ge(zeros_set, 11)
            nc.vector.tensor_scalar(wk_s[:, :], w("wk0"), scale, None, ALU.mult)
            nc.vector.tensor_scalar(wq_s[:, :], w("wq0"), scale, None, ALU.mult)
            dve.wait_ge(consts_in, 16)
            nc.vector.tensor_copy(ident16[:, :], ident)
            for dst, r in ((q_rep_hi, 0), (q_rep_lo, 1), (q_rep_hi, 2), (k_rep_hi, 0), (k_rep_hi, 1), (k_rep_lo, 2)):
                nc.vector.tensor_copy(dst[:, :, DK * r:DK * r + DK], ident.rearrange("p (h k) -> p h k", k=DK))
            nc.vector.tensor_copy(identb[:, :], ident).then_inc(attn_w_set, 1)
            dve.wait_ge(ones_set, HG + 1)

            def cosine_arguments(*_):
                dve.wait_ge(late_in, 16)
                dve.wait_ge(z_mm, 1)
                zf = kz[:, :, :].rearrange("p b t -> p (b t)")
                rf = kz_n[:, :, :].rearrange("p b t -> p (b t)")
                nf = kz_k[:, :, :].rearrange("p b t -> p (b t)")
                set_up(nc.vector.tensor_scalar(kz[:, :, :].rearrange("p (h b) t -> p h (b t)", h=2),
                                               ps[:, BA:BB + 1, 0:2 * T], w("br1"), None, ALU.add))
                set_up(nc.vector.tensor_scalar(zf, zf, TWO_PI / 4, None, ALU.add))
                set_up(nc.vector.tensor_scalar(nf, zf, 1.0 / TWO_PI, ROUND, ALU.mult, ALU.add))
                set_up(nc.vector.tensor_scalar(nf, nf, ROUND, None, ALU.subtract))
                set_up(nc.vector.scalar_tensor_tensor(out=rf, in0=nf, scalar=-TWO_PI_HI, in1=zf,
                                                      op0=ALU.mult, op1=ALU.add))
                set_up(nc.vector.scalar_tensor_tensor(out=zf, in0=nf, scalar=-TWO_PI_LO, in1=rf,
                                                      op0=ALU.mult, op1=ALU.add))
                nc.vector.tensor_scalar(rf, zf, PI, -PI, ALU.min, ALU.max).then_inc(z_reduced, 1)

            def second_values(*_):
                dve.wait_ge(v1_mm, 1)
                nc.vector.tensor_tensor(
                    v1[0:TH, :, :, :].rearrange("p b c d -> p (b c) d"),
                    ps[0:TH, BA:BB + 1, :].rearrange("p a (c d) -> p (a c) d", d=D),
                    w("bv1")[0:TH, :].unsqueeze(1).broadcast_to([TH, 2 * B, D]), ALU.add).then_inc(v1_ready, 1)

            def gate_weights(*_):
                set_up(nc.vector.tensor_scalar(wg_s[:, :], w("wg"), WS, None, ALU.mult))
                set_up(nc.vector.tensor_copy(wg_hi[:, :], wg_s[:, :]))
                nc.vector.tensor_tensor(wg_lo[:, :], wg_s[:, :], wg_hi[:, :], ALU.subtract)

            def fp8_weights(*_):
                set_up(nc.vector.reciprocal(s_inv[:, :], w("s")))
                nc.vector.tensor_tensor(s_prod[:, :], w("s")[:, 0:1], w("s")[:, 1:2], ALU.mult)
                dve.wait_ge(kern_in, 32)
                set_up(nc.vector.tensor_scalar(fv[:, 0:P], kern_sb[:, :], s_inv[:, 1:2], None, ALU.mult))
                set_up(round_e4m3(set_up, fv[:, 0:P], slice(0, P), kern_q[:, :]))

            chain = [0, 0]

            def settled(ins):
                chain[1] += 1
                ins.then_inc(dve_step, 1)
                dve.wait_ge(dve_step, chain[0] + chain[1])

            def norm_source(n):
                return (x_in, x1, acc[:, 1], x3)[n]

            def norm_a(b, n, half=None):
                t, k = tiles(half)
                if n == 0:
                    dve.wait_ge(x_loaded, b * 16 + 16)
                elif n == 3:
                    dve.wait_ge(SEM["x3_ready"], at("x3_ready", b, k))
                else:
                    name = (None, "x1_ready", "added")[n]
                    dve.wait_ge(SEM[name], at(name, b))
                for s in range(t.start, t.stop):
                    last = nc.vector.bn_stats(stats[:, n, s, :], norm_source(n)[:, s, :])
                settled(last)
                nc.vector.memset(carrier[:, :], 0.0)
                for s in range(t.start, t.stop):
                    last = nc.vector.bn_aggr(mv[:, n, s, :], stats[:, n, s, :])
                last.then_inc(SEM[f"var{n}_ready"], 1)

            def norm_b(b, n, half=None):
                t, k = tiles(half)
                dve.wait_ge(SEM[f"rstd{n}_ready"], at(f"rstd{n}_ready", b, k))
                by = rstd[:, n, :]
                if n == 0:
                    settled(nc.vector.tensor_tensor(rstd_q[:, :], rstd[:, 0, :], keep[:, :], ALU.mult))
                    by = rstd_q
                dst = (xn0, xn, xn, xb)[n]
                for s in range(t.start, t.stop):
                    last = nc.vector.tensor_scalar(dst[:, s, :], norm_source(n)[:, s, :], mv[:, n, s, 0:1],
                                                   by[:, s:s + 1], ALU.subtract, ALU.mult)
                last.then_inc(SEM[f"xn{n}_ready"], 1)

            def context_rest(b, _):
                dve.wait_ge(ctx_loaded, b * 16 + 16)
                nc.vector.tensor_copy(ctx_rem[:, :, 0:TR],
                                      ctx_sb[:, T0:T].unsqueeze(1).broadcast_to([P, HG, TR])
                                      ).then_inc(SEM["ctx_rem_ready"], 1)

            def mask_rows(b, _):
                dve.wait_ge(mask_loaded, b * 16 + 16)
                nc.vector.tensor_scalar(is_zero[:, :, :], mask_sb[:, :, :], 0.0, None, ALU.is_equal
                                        ).then_inc(SEM["mask_zero"], 1)
                dve.wait_ge(SEM["mask_zero"], at("mask_zero", b))
                settled(nc.vector.tensor_reduce(all_zero[:, :], is_zero[:, :, :], X, ALU.min))
                settled(nc.vector.tensor_scalar(keep[:, :], all_zero[:, :], -1.0, 1.0, ALU.mult, ALU.add))
                settled(nc.vector.tensor_scalar(fill[:, :], keep[:, :], MASKED, None, ALU.mult))

            def mask_bias(b, _):
                nc.vector.tensor_tensor(bias_st[:, :, :], is_zero[:, :, :],
                                        fill[:, :].unsqueeze(2).broadcast_to([P, ST, T]), ALU.mult)
                for j in range(HG):
                    last = nc.vector.tensor_tensor(bias_rem[:, :, j, 0:TR], is_zero[:, :, T0:T],
                                                   fill[:, :].unsqueeze(2).broadcast_to([P, ST, TR]), ALU.mult)
                last.then_inc(SEM["bias_ready"], 1)

            def k_low(b, _):
                dve.wait_ge(SEM["k_hi_ready"], at("k_hi_ready", b))
                nc.vector.tensor_tensor(k_lo[:, :], bank(ROWB[1])[:, 0:T], k_hi[:, :], ALU.subtract
                                        ).then_inc(SEM["k_lo_ready"], 1)

            def k_blocks(b, _):
                dve.wait_ge(SEM["k_diag_ready"], at("k_diag_ready", b))
                for j in range(HG):
                    r = slice(ROWS * j, ROWS * j + ROWS)
                    last = nc.vector.tensor_copy(krem[r, :, j, 0:TR], kdiag[r, :, j, T0:T])
                last.then_inc(SEM["k_ready"], 1)

            def v_blocks(b, _):
                dve.wait_ge(SEM["v_mm"], at("v_mm", b))
                vb = bank(SCB[0])
                nc.vector.tensor_copy(vaug[:, :, 0:DK], vb[:, 0:P].rearrange("p (h k) -> p h k", k=DK))
                for j in range(HG):
                    r = slice(ROWS * j, ROWS * j + ROWS)
                    last = nc.vector.tensor_copy(
                        vrem[r, :, j, 0:DK],
                        vb[r, P:2 * P].rearrange("p (g j k) -> p g j k", j=HG, k=DK)[:, :, j, :])
                last.then_inc(SEM["v_ready"], 1)

            def query_parts(b, _):
                dve.wait_ge(SEM["q_hi_ready"], at("q_hi_ready", b))
                nc.vector.tensor_tensor(q_lo[:, :], bank(SCB[1]), q_hi[:, :], ALU.subtract
                                        ).then_inc(SEM["q_lo_ready"], 1)

            def row_max(b, n):
                g, s = divmod(n, ST)
                for h in range(2):
                    dve.wait_ge(SEM["max_mm"], at("max_mm", b, 2 * n + h + 1))
                    nc.vector.tensor_reduce(
                        neg_max[:, g, s, :].rearrange("p (j r) -> p j r", r=ROWS)[:, 2 * h:2 * h + 2, MROW],
                        bank(ROWB[h])[:, 0:2 * T].rearrange("p (h t) -> p h t", t=T),
                        X, ALU.max, negate=True).then_inc(SEM["max_done"], 1)

            def shift(b, g):
                dve.wait_ge(SEM["max_tr"], at("max_tr", b, g + 1))
                nc.vector.tensor_tensor(qst[:, g, :], qst[:, g, :], bank16(TRB, F16)[:, 0:S], ALU.add
                                        ).then_inc(SEM["q_shifted"], 1)

            def normalize(b, g):
                dve.wait_ge(SEM["av_tr"], at("av_tr", b, g + 1))
                o = bank(TRB).rearrange("p (s j r) -> p s j r", s=ST, r=ROWS)
                settled(nc.vector.reciprocal(inv_sum[:, :, :], o[:, :, :, DK]))
                nc.vector.tensor_tensor(
                    att[:, :, ROWS * g:ROWS * g + ROWS].rearrange("p s (j k) -> p s j k", k=DK),
                    o[:, :, :, 0:DK], inv_sum[:, :, :].unsqueeze(3).broadcast_to([P, ST, HG, DK]), ALU.mult
                ).then_inc(SEM["att_ready"], 1)

            def project(b, _):
                dve.wait_ge(SEM["y0_mm"], at("y0_mm", b))
                nc.vector.tensor_tensor(y_b[:, :, :], bank(AVB).rearrange("p (s d) -> p s d", d=D),
                                        w("bu0").unsqueeze(1).broadcast_to([P, ST, D]), ALU.add
                                        ).then_inc(SEM["y0_read"], 1)
                dve.wait_ge(x_res_loaded, b * 16 + 16)
                dve.wait_ge(SEM["y0_read"], at("y0_read", b))
                nc.vector.scalar_tensor_tensor(out=x1[:, :, :], in0=y_b[:, :, :], scalar=gates[:, 0:1],
                                               in1=x_res[:, :, :], op0=ALU.mult, op1=ALU.add
                                               ).then_inc(SEM["x1_ready"], 1)

            def low_part(b, _):
                dve.wait_ge(SEM["xhi_ready"], at("xhi_ready", b))
                nc.vector.tensor_tensor(xn_lo[:, :], bank(BA), xn_hi[:, :], ALU.subtract
                                        ).then_inc(SEM["xlo_ready"], 1)

            def top2(b, _):
                dve.wait_ge(SEM["gate_mm"], at("gate_mm", b))
                nc.vector.tensor_copy(logits[:, :, :], bank(BB)[:, 0:ST * E_N].rearrange("p (s e) -> p s e", e=E_N)
                                      ).then_inc(SEM["gate_read"], 1)
                alone(dve)
                dve.wait_ge(SEM["gate_read"], at("gate_read", b))
                for s in range(ST):
                    last = nc.vector.max(top8[:, s, :], logits[:, s, :])
                settled(last)
                nc.vector.tensor_tensor(gap[:, :], top8[:, :, 1], top8[:, :, 0], ALU.subtract
                                        ).then_inc(SEM["gap_ready"], 1)
                for s in range(ST):
                    last = nc.vector.max_index(top_i[:, s, :], top8[:, s, :], logits[:, s, :])
                settled(last)
                settled(nc.vector.tensor_copy(top_f[:, :, :], top_i[:, :, 0:2]))

            def combine(b, _):
                dve.wait_ge(SEM["e_gap_ready"], at("e_gap_ready", b))
                settled(nc.vector.tensor_scalar(gw[:, 0, :], e_gap[:, :], 1.0, None, ALU.add))
                settled(nc.vector.reciprocal(gw[:, 1, :], gw[:, 0, :]))
                nc.vector.tensor_tensor(gw[:, 2, :], e_gap[:, :], gw[:, 1, :], ALU.mult)
                for k in range(2):
                    last = nc.vector.tensor_tensor(pick[:, k, :, :],
                                                   cst("iota").unsqueeze(1).broadcast_to([P, ST, E_N]),
                                                   top_f[:, :, k].unsqueeze(2).broadcast_to([P, ST, E_N]),
                                                   ALU.is_equal)
                settled(last)
                for k in range(2):
                    last = nc.vector.tensor_tensor(pick[:, k, :, :], pick[:, k, :, :],
                                                   gw[:, k + 1, :].unsqueeze(2).broadcast_to([P, ST, E_N]),
                                                   ALU.mult)
                settled(last)
                settled(nc.vector.tensor_tensor(pick[:, 2, :, :], pick[:, 0, :, :], pick[:, 1, :, :], ALU.add))
                settled(nc.vector.tensor_scalar(wx[:, :, :], pick[:, 2, :, :], gates[:, 1:2], None, ALU.mult))

            def add_expert(b, e):
                dve.wait_ge(SEM["down_mm"], at("down_mm", b, e + 1))
                if e >= 1:
                    dve.wait_ge(SEM["added"], at("added", b, e))
                for s in range(ST):
                    last = nc.vector.scalar_tensor_tensor(
                        out=acc[:, e % 2, s, :], in0=bank(DOWNB[e % 2])[:, D * s:D * s + D], scalar=wx[:, s, e:e + 1],
                        in1=x1[:, s, :] if e == 0 else acc[:, (e + 1) % 2, s, :], op0=ALU.mult, op1=ALU.add)
                last.then_inc(SEM["added"], 1)

            def s1(b, h):
                dve.wait_ge(SEM["s1_mm"], at("s1_mm", b, h + 1))
                nc.vector.tensor_reduce(nmax1[:, tiles(h)[0]], half_bank(h)[:, :, 0:T], X, ALU.max, negate=True
                                        ).then_inc(SEM["nmax1_ready"], 1)

            def inverse_sums(b, h):
                t = tiles(h)[0]
                dve.wait_ge(SEM["p1_ready"], at("p1_ready", b, h + 1))
                settled(nc.vector.reciprocal(r1[:, t], sum1[:, t]))
                nc.vector.tensor_scalar(r1g[:, t], r1[:, t], gates[:, 2:3], None, ALU.mult
                                        ).then_inc(SEM["r1_ready"], 1)

            def o1(b, h):
                dve.wait_ge(SEM["r1_ready"], at("r1_ready", b, h + 1))
                dve.wait_ge(SEM["o1_mm"], at("o1_mm", b, h + 1))
                for s in range(ST // 2):
                    t = ST // 2 * h + s
                    last = nc.vector.scalar_tensor_tensor(
                        out=x3[:, t, :], in0=bank((BA, BB)[h])[:, D * s:D * s + D], scalar=r1g[:, t:t + 1],
                        in1=acc[:, 1, t, :], op0=ALU.mult, op1=ALU.add)
                last.then_inc(SEM["x3_ready"], 1)

            def quantize(b, h):
                t, c = tiles(h)[0], slice(SH * h, SH * h + SH)
                dve.wait_ge(SEM["xn3_ready"], at("xn3_ready", b, h + 1))
                settled(nc.vector.tensor_scalar(fv[:, c], xb[:, t, :].rearrange("p s d -> p (s d)"),
                                                s_inv[:, 0:1], None, ALU.mult))
                round_e4m3(settled, fv[:, c], c, xq[:, t, :].rearrange("p s d -> p (s d)")
                           ).then_inc(SEM["xq_ready"], 1)

            def y1(b, h):
                t = tiles(h)[0]
                dve.wait_ge(SEM["y1_ready"], at("y1_ready", b, h + 1))
                settled(nc.vector.tensor_tensor(y_sb[:, t, :], y_s[:, t, :],
                                                kbias_sb[:, :].unsqueeze(1).broadcast_to([P, ST // 2, D]),
                                                ALU.add))
                dve.wait_ge(stored, b * 16 + 1)
                nc.vector.scalar_tensor_tensor(out=x4[:, t, :], in0=y_sb[:, t, :], scalar=gates[:, 3:4],
                                               in1=x3[:, t, :], op0=ALU.mult, op1=ALU.add
                                               ).then_inc(SEM["x4_ready"], 1)

            steps = {
                "z": cosine_arguments, "v1": second_values, "w_gate": gate_weights,
                "w_fp8": fp8_weights, "ctx_rem": context_rest, "mask": mask_rows, "bias": mask_bias,
                "norm0_a": lambda b, _: norm_a(b, 0), "norm0_b": lambda b, _: norm_b(b, 0),
                "norm1_a": lambda b, _: norm_a(b, 1), "norm1_b": lambda b, _: norm_b(b, 1),
                "k_lo": k_low, "k_blocks": k_blocks, "v_blocks": v_blocks, "q_parts": query_parts,
                "row_scores": row_max, "max_rows": shift,
                "values_back": normalize, "project": project, "xn1_t": low_part, "top2": top2,
                "combine": combine, "down": add_expert, "s1": s1,
                "norm2_a": lambda b, half: norm_a(b, 2, half), "norm2_b": lambda b, half: norm_b(b, 2, half),
                "norm3_a": lambda b, half: norm_a(b, 3, half), "norm3_b": lambda b, half: norm_b(b, 3, half),
                "p1_t": inverse_sums, "o1": o1, "quantize": quantize, "y1": y1,
            }
            run(steps, FIRST, -2)
            dve.wait_ge(gates_set, 1)
            run(steps, START, -1)
            assert chain[1] == DVE_START, chain[1]
            with dve.Fori(0, B - 2) as i:
                chain[:] = [DVE_START + i * DVE_LOOP, 0]
                run(steps, LOOP, i)
            assert chain[1] == DVE_LOOP, chain[1]
            chain[:] = [DVE_START + (B - 2) * DVE_LOOP, 0]
            run(steps, LOOP, B - 2)
            run(steps, LOOP, B - 1)

        @block.tensor
        def _(pe):
            def transposes(dst, src, idn):
                for s in range(src.shape[1]):
                    last = nc.tensor.transpose(dst[:, P * s:P * s + P], src[:, s, :], idn)
                return last

            def context_features(*_):
                pe.wait_ge(late_in, 16)
                pe.wait_ge(ctx_all_in, 16)
                for h in range(2):
                    last = nc.tensor.matmul(ps[:, BA + h, 0:2 * T], w("wk1"),
                                            ctx_all[:, 2 * h:2 * h + 2, :].rearrange("p b t -> p (b t)"),
                                            start=True, stop=True)
                last.then_inc(kc_mm, 1)

            def context_projections(*_):
                pe.wait_ge(kc_ready, 1)
                for h in range(2):
                    last = nc.tensor.matmul(ps[:, BA + h, 0:2 * T], w("wr1"),
                                            kz[:, 2 * h:2 * h + 2, :].rearrange("p b t -> p (b t)"),
                                            start=True, stop=True)
                last.then_inc(z_mm, 1)

            def second_values(*_):
                pe.wait_ge(z_reduced, 1)
                for b in range(B):
                    for c in range(2):
                        o = ps[0:TH, BA + b // 2, D * (2 * (b % 2) + c):D * (2 * (b % 2) + c + 1)]
                        last = nc.tensor.matmul(o, ctx_all[:, b, TH * c:TH * c + TH], w("wv1"),
                                                start=True, stop=True)
                last.then_inc(v1_mm, 1)

            def context(b, _):
                pe.wait_ge(ctx_loaded, b * 16 + 16)
                nc.tensor.matmul(bank(ROWB[1])[:, 0:T], wk_s[:, :], ctx_sb[:, :], start=True, stop=True
                                 ).then_inc(SEM["k_mm"], 1)
                pe.wait_ge(SEM["ctx_rem_ready"], at("ctx_rem_ready", b))
                vb = bank(SCB[0])
                nc.tensor.matmul(vb[:, 0:P], ctx_sb[:, 0:T0], w("wv0"), start=True, stop=True)
                nc.tensor.matmul(vb[:, P:2 * P], ctx_rem[:, :, :].rearrange("p j r -> p (j r)"), w("wv0"),
                                 start=True, stop=True).then_inc(SEM["v_mm"], 1)

            def k_rows(b, _):
                pe.wait_ge(SEM["k_lo_ready"], at("k_lo_ready", b))
                for g in range(NG):
                    heads = slice(HG * g, HG * g + HG)
                    nc.tensor.matmul(k_ps[:, g, :], k_rep_hi[:, heads, :].rearrange("p h r -> p (h r)"),
                                     k_hi[:, :], start=True, stop=False)
                    last = nc.tensor.matmul(k_ps[:, g, :], k_rep_lo[:, heads, :].rearrange("p h r -> p (h r)"),
                                            k_lo[:, :], start=False, stop=True)
                last.then_inc(SEM["k_rep_mm"], 1)

            def turn_bias(b, _):
                pe.wait_ge(SEM["bias_ready"], at("bias_ready", b))
                t = bank16(TRB, BF16)
                transposes(t[:, 0:S], bias_st[:, :, 0:T0], identb[:, :])
                transposes(t[:, S:2 * S], bias_rem[:, :, :, :].rearrange("p s j r -> p s (j r)"), identb[:, :]
                           ).then_inc(SEM["bias_tr"], 1)

            def turn_xn0(b, _):
                pe.wait_ge(SEM["xn0_ready"], at("xn0_ready", b))
                if not (isinstance(b, int) and b == 0):
                    pe.wait_ge(SEM["probs_ready"], at("probs_ready", b - 1))
                transposes(bank(SCB[1]), xn0, ident).then_inc(SEM["xn0_tr"], 1)

            def query_parts(b, _):
                pe.wait_ge(SEM["xn0_t_ready"], at("xn0_t_ready", b))
                nc.tensor.matmul(bank(SCB[1]), wq_s[:, :], xn0_t[:, :], start=True, stop=True
                                 ).then_inc(SEM["q_mm"], 1)

            def queries(b, g):
                if g == 0:
                    pe.wait_ge(SEM["q_lo_ready"], at("q_lo_ready", b))
                    pe.wait_ge(SEM["v_ready"], at("v_ready", b))
                elif g >= 2:
                    pe.wait_ge(SEM["q_ready"], at("q_ready", b, g - 1))
                o, heads = bank(SCB[g % 2]), slice(HG * g, HG * g + HG)
                nc.tensor.matmul(o, q_rep_hi[:, heads, :].rearrange("p h r -> p (h r)"), q_hi[:, :],
                                 start=True, stop=False)
                nc.tensor.matmul(o, q_rep_lo[:, heads, :].rearrange("p h r -> p (h r)"), q_lo[:, :],
                                 start=False, stop=True).then_inc(SEM["q_rep_mm"], 1)

            def row_scores(b, n):
                g, s = divmod(n, ST)
                if s == 0:
                    pe.wait_ge(SEM["q_ready"], at("q_ready", b, g + 1))
                if n == 0:
                    pe.wait_ge(SEM["k_ready"], at("k_ready", b))
                for h in range(2):
                    if n >= 1:
                        pe.wait_ge(SEM["max_done"], at("max_done", b, 2 * n + h - 1))
                    o = bank(ROWB[h])[:, 0:2 * T]
                    nc.tensor.matmul(o, qst[:, g, P * s:P * s + P],
                                     kdiag[:, g, 2 * h:2 * h + 2, :].rearrange("p h t -> p (h t)"),
                                     start=True, stop=False)
                    nc.tensor.matmul(o.rearrange("p (h t) -> p h t", h=2), identb[:, :],
                                     bias_st[:, s, :].unsqueeze(1).broadcast_to([P, 2, T]),
                                     start=False, stop=True).then_inc(SEM["max_mm"], 1)

            def max_rows(b, g):
                pe.wait_ge(SEM["max_done"], at("max_done", b, 2 * ST * (g + 1)))
                if g == 0:
                    pe.wait_ge(SEM["bias_t_ready"], at("bias_t_ready", b))
                else:
                    pe.wait_ge(SEM["q_shifted"], at("q_shifted", b, g))
                transposes(bank16(TRB, F16)[:, 0:S], neg_max[:, g, :, :], ident16[:, :]
                           ).then_inc(SEM["max_tr"], 1)

            def scores(b, n):
                g, j = divmod(n, HG + 1)
                pe.wait_ge(SEM["q_shifted"], at("q_shifted", b, g + 1))
                if n == 0:
                    pe.wait_ge(SEM["q_ready"], at("q_ready", b))
                if n == 0 and not (isinstance(b, int) and b == 0):
                    pe.wait_ge(SEM["added"], at("added", b - 1))
                if n >= 2:
                    pe.wait_ge(SEM["probs_ready"], at("probs_ready", b, n - 1))
                keys = kdiag[:, g, j, 0:T0] if j < HG else krem[:, g, :, :].rearrange("p j r -> p (j r)")
                nc.tensor.matmul(bank(SCB[n % 2]), keys, qst[:, g, :], start=True, stop=False)
                nc.tensor.matmul(bank(SCB[n % 2]), identb[:, :], bias_t[:, j // HG, :],
                                 start=False, stop=True).then_inc(SEM["score_mm"], 1)

            def weighted_v(b, g):
                if g >= 1:
                    pe.wait_ge(SEM["av_ready"], at("av_ready", b, g))
                for j in range(HG):
                    pe.wait_ge(SEM["probs_ready"], at("probs_ready", b, (HG + 1) * g + j + 1))
                    nc.tensor.matmul(ps[ROWS * j:ROWS * j + ROWS, AVB, :], vaug[:, HG * g + j, :],
                                     probs_t[:, g % 2, j, :], start=True, stop=False, skip_group_check=True)
                pe.wait_ge(SEM["probs_ready"], at("probs_ready", b, (HG + 1) * (g + 1)))
                nc.tensor.matmul(bank(AVB), vrem[:, g, :, :].rearrange("p j r -> p (j r)"),
                                 probs_t[:, g % 2, HG, :], start=False, stop=True, skip_group_check=True
                                 ).then_inc(SEM["av_mm"], 1)

            def values_back(b, g):
                pe.wait_ge(SEM["av_ready"], at("av_ready", b, g + 1))
                if g == 0:
                    pe.wait_ge(SEM["q_shifted"], at("q_shifted", b))
                else:
                    pe.wait_ge(SEM["att_ready"], at("att_ready", b, g))
                transposes(bank(TRB), av_t[:, g % 2, :].rearrange("p (s q) -> p s q", q=P), ident
                           ).then_inc(SEM["av_tr"], 1)

            def project(b, _):
                pe.wait_ge(SEM["att_ready"], at("att_ready", b))
                transposes(bank(TRB), att, ident).then_inc(SEM["att_tr"], 1)
                pe.wait_ge(SEM["att_t_ready"], at("att_t_ready", b))
                for s in range(ST):
                    last = nc.tensor.matmul(bank(AVB)[:, D * s:D * s + D], att_t[:, P * s:P * s + P], w("wu0"),
                                            start=True, stop=True)
                last.then_inc(SEM["y0_mm"], 1)

            def turn_xn1(b, _):
                pe.wait_ge(SEM["xn1_ready"], at("xn1_ready", b))
                transposes(bank(BA), xn, ident).then_inc(SEM["xn1_tr"], 1)

            def gate_logits(b, _):
                pe.wait_ge(SEM["xlo_ready"], at("xlo_ready", b))
                for s in range(ST):
                    o = bank(BB)[:, E_N * s:E_N * s + E_N]
                    hi, lo = xn_hi[:, P * s:P * s + P], xn_lo[:, P * s:P * s + P]
                    nc.tensor.matmul(o, hi, wg_hi[:, :], start=True, stop=False)
                    nc.tensor.matmul(o, hi, wg_lo[:, :], start=False, stop=False)
                    last = nc.tensor.matmul(o, lo, wg_hi[:, :], start=False, stop=True)
                last.then_inc(SEM["gate_mm"], 1)

            def up(b, f):
                if f >= 2:
                    pe.wait_ge(SEM["h_ready"], at("h_ready", b, f - 1))
                o = bank(UPB[f % 2])
                nc.tensor.matmul(o, w1_hi[:, f, :], xn_hi[:, :], start=True, stop=False)
                nc.tensor.matmul(o, w1_hi[:, f, :], xn_lo[:, :], start=False, stop=False)
                nc.tensor.matmul(o, w1_lo[:, f, :], xn_hi[:, :], start=False, stop=True
                                 ).then_inc(SEM["up_mm"], 1)

            def down(b, e):
                pe.wait_ge(SEM["h_ready"], at("h_ready", b, 2 * e + 2))
                if e >= 2:
                    pe.wait_ge(SEM["added"], at("added", b, e - 1))
                for s in range(ST):
                    for f in (2 * e, 2 * e + 1):
                        last = nc.tensor.matmul(bank(DOWNB[e % 2])[:, D * s:D * s + D],
                                                h_sb[:, f % NH, P * s:P * s + P], w2_sb[:, f, :],
                                                start=(f % 2 == 0), stop=(f % 2 == 1))
                last.then_inc(SEM["down_mm"], 1)

            def turn_xn2(b, h):
                pe.wait_ge(SEM["xn2_ready"], at("xn2_ready", b, h + 1))
                transposes(bank((BA, BB)[h]), xn[:, tiles(h)[0], :], ident).then_inc(SEM["xn2_tr"], 1)

            def q1(b, h):
                pe.wait_ge(SEM["xn2_t_ready"], at("xn2_t_ready", b, h + 1))
                nc.tensor.matmul(bank((BA, BB)[h])[:, 0:SH], w("wq1"), xn_t[:, SH * h:SH * h + SH],
                                 start=True, stop=True).then_inc(SEM["q1_mm"], 1)

            def s1(b, h):
                pe.wait_ge(SEM["q1_ready"], at("q1_ready", b, h + 1))
                for s in range(ST // 2):
                    keys = khat[:, b, :] if isinstance(b, int) else khat[:, bass.ds(b, 1), :].rearrange(
                        "p b t -> p (b t)")
                    q = SH * h + P * s
                    last = nc.tensor.matmul(half_bank(h)[:, s, 0:T], q1_t[:, q:q + P], keys,
                                            start=True, stop=True)
                last.then_inc(SEM["s1_mm"], 1)

            def turn_p1(b, h):
                pe.wait_ge(SEM["p1_ready"], at("p1_ready", b, h + 1))
                for s in range(ST // 2):
                    for c in range(2):
                        q = P * (2 * s + c)
                        last = nc.tensor.transpose(ps[0:TH, (BA, BB)[h], q:q + P],
                                                   p1[:, ST // 2 * h + s, TH * c:TH * c + TH], ident)
                last.then_inc(SEM["p1_tr"], 1)

            def o1(b, h):
                pe.wait_ge(SEM["p1_t_ready"], at("p1_t_ready", b, h + 1))
                for s in range(ST // 2):
                    for c in range(2):
                        values = v1[0:TH, b, c, :] if isinstance(b, int) else v1[
                            0:TH, bass.ds(b, 1), c, :].rearrange("p b d -> p (b d)")
                        q = P * (2 * s + c)
                        last = nc.tensor.matmul(bank((BA, BB)[h])[:, D * s:D * s + D], p1_t[0:TH, h, q:q + P],
                                                values, start=(c == 0), stop=(c == 1))
                last.then_inc(SEM["o1_mm"], 1)

            def turn_xq(b, h):
                pe.wait_ge(SEM["xq_ready"], at("xq_ready", b, h + 1))
                transposes(bank16((BA, BB)[h], BF16), xq[:, tiles(h)[0], :], identb[:, :]
                           ).then_inc(SEM["xq_tr"], 1)

            def y1(b, h):
                pe.wait_ge(SEM["xq_t_ready"], at("xq_t_ready", b, h + 1))
                for s in range(ST // 2):
                    q = SH * h + P * s
                    last = nc.tensor.matmul(bank((BA, BB)[h])[:, D * s:D * s + D], xq_t[:, q:q + P], kern_q[:, :],
                                            start=True, stop=True)
                last.then_inc(SEM["y1_mm"], 1)

            def keep_warm(b, _):
                idle = BB if isinstance(b, int) and b < 0 else ROWB[1]
                for _ in range(4):
                    nc.tensor.matmul(bank(idle), ident16[:, :],
                                     ident16[:, :].unsqueeze(1).broadcast_to([P, 4, P]), start=True, stop=True)

            steps = {
                "warm": keep_warm, "warm_last": keep_warm, "kc": context_features, "z": context_projections,
                "v1": second_values, "k_rows": k_rows,
                "context": context, "bias_t": turn_bias, "xn0_t": turn_xn0,
                "q_parts": query_parts, "queries": queries,
                "row_scores": row_scores, "max_rows": max_rows, "scores": scores, "weighted_v": weighted_v,
                "values_back": values_back, "project": project, "xn1_t": turn_xn1, "gate": gate_logits,
                "up": up, "down": down,
                "xn2_t": turn_xn2, "q1": q1, "s1": s1, "p1_t": turn_p1, "o1": o1, "xq_t": turn_xq, "y1": y1,
            }
            pe.wait_ge(attn_w_set, 1)
            run(steps, FIRST, -2)
            run(steps, START, -1)
            pe.wait_ge(v1_ready, 1)
            pe.wait_ge(ffn_w_set, 1)
            pe.wait_ge(w2_in, 16)
            pe.wait_ge(khat_ready, 1)
            with pe.Fori(0, B - 2) as i:
                run(steps, LOOP, i)
            run(steps, LOOP, B - 2)
            run(steps, LOOP, B - 1)


def kernel(**inputs):
    import numpy as _np
    import concourse.bacc as _bacc
    from concourse import mybir as _mybir
    from concourse.bass_utils import run_bass_kernel_spmd as _run

    a = {n: _np.asarray(v) for n, v in inputs.items()}

    def rows(v):
        return _np.broadcast_to(v.reshape(1, -1), (P, v.size))

    def heads(v):
        return v.transpose(1, 0, 2).reshape(P, P)

    parts = {
        "wq0": heads(a["L0_xattn_Wq"]), "wk0": heads(a["L0_xattn_Wk"]), "wv0": heads(a["L0_xattn_Wv"]),
        "wu0": a["L0_xattn_Wu"], "bu0": rows(a["L0_xattn_bu"]),
        "g": rows(_np.stack([a["g_xattn"], a["g_ffn"]], 1)),
        "s": rows(_np.concatenate([a["L1_ffn_input_scale"], a["L1_ffn_kernel_scale"]])),
        "wg": a["L0_ffn_Wg"], "wq1": a["L1_xattn_Wq"], "wk1": a["L1_xattn_Wk"], "wv1": a["L1_xattn_Wv"],
        "wr1": a["L1_xattn_Wr"], "bq1": a["L1_xattn_bq"].reshape(P, 1), "bk1": a["L1_xattn_bk"].reshape(P, 1),
        "br1": a["L1_xattn_br"].reshape(P, 1), "bv1": rows(a["L1_xattn_bv"]),
    }
    wts = _np.concatenate([parts[n] for n in W_COLS], 1)
    row = _np.arange(P) % ROWS
    consts = _np.zeros((P, C_TOTAL), _np.float32)
    consts[:, 0:P] = _np.eye(P)
    consts[:, C_COLS["one"][0]] = row == MROW
    consts[:, slice(*C_COLS["iota"])] = _np.arange(E_N)
    arrays = {
        "x": a["x"],
        "ctx_t": a["ctx_1024"].transpose(0, 2, 1),
        "mask": a["mask_BxSxS2_ik1"],
        "wts": wts,
        "w1": a["L0_ffn_W1"].transpose(1, 0, 2).reshape(P, -1),
        "w2": a["L0_ffn_W2"].reshape(FC, P, P).transpose(1, 0, 2).reshape(P, -1),
        "kern": a["L1_ffn_kernel"],
        "kbias": rows(a["L1_ffn_bias"]),
        "consts": consts,
    }
    arrays = {n: _np.ascontiguousarray(v) for n, v in arrays.items()}
    nc = _bacc.Bacc("TRN2", target_bir_lowering=False, num_devices=1)
    args = [nc.dram_tensor(n, v.shape, _mybir.dt.from_np(v.dtype), kind="ExternalInput").ap()
            for n, v in arrays.items()]
    out = nc.dram_tensor("out", a["x"].shape, F32, kind="ExternalOutput").ap()
    flamingo_gated(nc, *args, out)
    return _run(nc, [arrays], core_ids=[0]).results[0]["out"]
```
